# Optimizing a Trainium2 kernel written in Bass

```python
import numpy as np
import jax
import jax.numpy as jnp

def _softmax(x, axis=-1):
    return jax.nn.softmax(x, axis=axis)

def _gelu(x):
    return jax.nn.gelu(x, approximate=True)

def _silu(x):
    return jax.nn.silu(x)

def _sigmoid(x):
    return jax.nn.sigmoid(x)

def _layernorm(x, axis=-1, eps=1e-05):
    m = jnp.mean(x, axis=axis, keepdims=True)
    v = jnp.var(x, axis=axis, keepdims=True)
    return (x - m) / jnp.sqrt(v + eps)

def _scatter_add(tgt, idx, src, axis=0):
    return tgt.at[idx].add(src)

def _segment_sum(src, seg, n):
    return jax.ops.segment_sum(src, seg, n)
kernel_name = 'mk_seq_preln_d2_jaxref_r4_5a1958'

def setup_inputs(seed: int=0):
    np.random.seed(seed)
    _w = jnp.asarray

    def _L0_attn_setup():
        import jax, jax.numpy as jnp
        import numpy as np
        from jax.lax import associative_scan
        B, S, D, F, G = (4, 1024, 256, 1024, 32)
        EPS = 1e-06

        def _gate_loop(k, v, q, a):
            kv = (k * v).astype(jnp.complex64)

            def op(e1, e2):
                a1, x1 = e1
                a2, x2 = e2
                return (a1 * a2, a2 * x1 + x2)
            _, h = associative_scan(op, (a, kv), axis=1)
            return q.astype(jnp.complex64) * h

        def _layernorm(x, scale, bias):
            mu = jnp.mean(x, axis=-1, keepdims=True)
            var = jnp.mean(jnp.square(x - mu), axis=-1, keepdims=True)
            return (x - mu) * jax.lax.rsqrt(var + EPS) * scale + bias

        def _groupnorm_complex(y, scale, bias):
            b, s, d = y.shape
            yr = y.reshape(b, s, G, d // G)
            mean = jnp.mean(yr, axis=(1, 3), keepdims=True)
            mean2 = jnp.mean(yr.real ** 2 + yr.imag ** 2, axis=(1, 3), keepdims=True)
            var = mean2 - (mean.real ** 2 + mean.imag ** 2)
            yn = (yr - mean) * jax.lax.rsqrt(var + EPS)
            return yn.reshape(b, s, d) * scale + bias
        key = jax.random.key(seed)
        ks = jax.random.split(key, 16)
        xn = lambda k, shp: jax.random.normal(k, shp, jnp.float32) / np.sqrt(shp[0])
        return {'x': jax.random.normal(ks[0], (B, S, D), jnp.float32), 'Wq': xn(ks[1], (D, D)), 'Wk': xn(ks[2], (D, D)), 'Wv': xn(ks[3], (D, D)), 'Wa': xn(ks[4], (D, 2 * D)), 'Wg': xn(ks[5], (D, D)), 'Wo': xn(ks[6], (D, D)), 'gn_scale': jnp.ones((D,), jnp.float32), 'gn_bias': jnp.zeros((D,), jnp.float32), 'ln1_scale': jnp.ones((D,), jnp.float32), 'ln1_bias': jnp.zeros((D,), jnp.float32), 'W1': xn(ks[7], (D, F)), 'b1': jax.random.normal(ks[8], (F,), jnp.float32) * 1e-06, 'W2': xn(ks[9], (F, D)), 'b2': jax.random.normal(ks[10], (D,), jnp.float32) * 1e-06, 'ln2_scale': jnp.ones((D,), jnp.float32), 'ln2_bias': jnp.zeros((D,), jnp.float32)}
    _L0_attn_in = _L0_attn_setup()

    def _L0_ffn_setup():
        import jax, jax.numpy as jnp
        import numpy as np
        NUM_EXPERTS = 64
        TOP_K = 2
        B, S, EMB, MLP = (4, 512, 256, 512)
        key = jax.random.key(seed)
        k1, k2, k3, k4, k5 = jax.random.split(key, 5)
        inputs = jax.random.normal(k1, (B, S, EMB), dtype=jnp.float32)
        gate_kernel = jax.random.normal(k2, (EMB, NUM_EXPERTS), dtype=jnp.float32) / np.sqrt(EMB)
        w0 = jax.random.normal(k3, (NUM_EXPERTS, EMB, MLP), dtype=jnp.float32) / np.sqrt(EMB)
        w1 = jax.random.normal(k4, (NUM_EXPERTS, EMB, MLP), dtype=jnp.float32) / np.sqrt(EMB)
        wo = jax.random.normal(k5, (NUM_EXPERTS, MLP, EMB), dtype=jnp.float32) / np.sqrt(MLP)
        return {'inputs': inputs, 'gate_kernel': gate_kernel, 'w0': w0, 'w1': w1, 'wo': wo}
    _L0_ffn_in = _L0_ffn_setup()

    def _L1_attn_setup():
        import jax, jax.numpy as jnp
        import numpy as np
        import math
        D_MODEL = 256
        D_STATE = 16
        D_CONV = 4
        EXPAND = 2
        D_INNER = EXPAND * D_MODEL
        DT_RANK = math.ceil(D_MODEL / 16)
        EPS = 1e-05

        def _rmsnorm(x, w):
            norm = jnp.linalg.norm(x, axis=-1, keepdims=True)
            rms = norm * (1.0 / math.sqrt(x.shape[-1]))
            return w * (x / (rms + EPS))

        def _mamba(h, in_proj_w, conv_w, conv_b, x_proj_w, dt_proj_w, dt_proj_b, A_log, D, out_proj_w):
            B, L, _ = h.shape
            xz = h @ in_proj_w.T
            x, z = jnp.split(xz, 2, axis=-1)
            xpad = jnp.pad(x, ((0, 0), (D_CONV - 1, 0), (0, 0)))
            xc = conv_b
            for k in range(D_CONV):
                xc = xc + xpad[:, k:k + L, :] * conv_w[:, k]
            xc = jax.nn.silu(xc)
            x_dbl = xc @ x_proj_w.T
            dt, Bm, Cm = jnp.split(x_dbl, [DT_RANK, DT_RANK + D_STATE], axis=-1)
            dt = jax.nn.softplus(dt @ dt_proj_w.T + dt_proj_b)
            A = -jnp.exp(A_log)
            deltaA = jnp.exp(dt[..., None] * A)
            deltaBu = (dt * xc)[..., None] * Bm[:, :, None, :]

            def step(hst, inp):
                dA, dBu, Ct = inp
                hst = dA * hst + dBu
                y = jnp.einsum('bdn,bn->bd', hst, Ct)
                return (hst, y)
            h0 = jnp.zeros((B, D_INNER, D_STATE), xc.dtype)
            _, ys = jax.lax.scan(step, h0, (deltaA.swapaxes(0, 1), deltaBu.swapaxes(0, 1), Cm.swapaxes(0, 1)))
            y = ys.swapaxes(0, 1)
            y = y + D * xc
            y = y * jax.nn.silu(z)
            return y @ out_proj_w.T

        def _reference_tuple_inner(hidden_states, norm_weight, in_proj_w, conv_w, conv_b, x_proj_w, dt_proj_w, dt_proj_b, A_log, D, out_proj_w):
            residual = hidden_states
            h = _rmsnorm(residual, norm_weight)
            out = _mamba(h, in_proj_w, conv_w, conv_b, x_proj_w, dt_proj_w, dt_proj_b, A_log, D, out_proj_w)
            return (out, residual)
        key = jax.random.key(seed)
        ks = jax.random.split(key, 8)
        B, L = (2, 256)
        s = 0.02
        return {'hidden_states': jax.random.normal(ks[0], (B, L, D_MODEL), jnp.float32), 'norm_weight': jnp.ones((D_MODEL,), jnp.float32), 'in_proj_w': jax.random.normal(ks[1], (2 * D_INNER, D_MODEL), jnp.float32) * s, 'conv_w': jax.random.normal(ks[2], (D_INNER, D_CONV), jnp.float32) * s, 'conv_b': jnp.zeros((D_INNER,), jnp.float32), 'x_proj_w': jax.random.normal(ks[3], (DT_RANK + 2 * D_STATE, D_INNER), jnp.float32) * s, 'dt_proj_w': jax.random.normal(ks[4], (D_INNER, DT_RANK), jnp.float32) * s, 'dt_proj_b': jax.random.uniform(ks[5], (D_INNER,), jnp.float32, -4.0, -2.0), 'A_log': jnp.log(jnp.broadcast_to(jnp.arange(1, D_STATE + 1, dtype=jnp.float32), (D_INNER, D_STATE))), 'D': jnp.ones((D_INNER,), jnp.float32), 'out_proj_w': jax.random.normal(ks[6], (D_MODEL, D_INNER), jnp.float32) * s}
    _L1_attn_in = _L1_attn_setup()

    def _L1_ffn_setup():
        import jax, jax.numpy as jnp
        import numpy as np
        E = 16
        H = 256
        F = 512
        TOP_K = 1
        B, S = (2, 256)
        key = jax.random.key(seed)
        ks = jax.random.split(key, 7)
        s = 0.02
        return {'hidden_states': jax.random.normal(ks[0], (B, S, H), jnp.float32), 'w_router': jax.random.normal(ks[1], (E, H), jnp.float32) * s, 'gate_up_proj': jax.random.normal(ks[2], (E, H, 2 * F), jnp.float32) * s, 'down_proj': jax.random.normal(ks[3], (E, F, H), jnp.float32) * s, 'w_gate': jax.random.normal(ks[4], (F, H), jnp.float32) * s, 'w_up': jax.random.normal(ks[5], (F, H), jnp.float32) * s, 'w_down': jax.random.normal(ks[6], (H, F), jnp.float32) * s}
    _L1_ffn_in = _L1_ffn_setup()
    _d = {'L0_attn_x': _L0_attn_in['x'], 'L0_attn_Wq': _L0_attn_in['Wq'], 'L0_attn_Wk': _L0_attn_in['Wk'], 'L0_attn_Wv': _L0_attn_in['Wv'], 'L0_attn_Wa': _L0_attn_in['Wa'], 'L0_attn_Wg': _L0_attn_in['Wg'], 'L0_attn_Wo': _L0_attn_in['Wo'], 'L0_attn_gn_scale': _L0_attn_in['gn_scale'], 'L0_attn_gn_bias': _L0_attn_in['gn_bias'], 'L0_attn_ln1_scale': _L0_attn_in['ln1_scale'], 'L0_attn_ln1_bias': _L0_attn_in['ln1_bias'], 'L0_attn_W1': _L0_attn_in['W1'], 'L0_attn_b1': _L0_attn_in['b1'], 'L0_attn_W2': _L0_attn_in['W2'], 'L0_attn_b2': _L0_attn_in['b2'], 'L0_attn_ln2_scale': _L0_attn_in['ln2_scale'], 'L0_attn_ln2_bias': _L0_attn_in['ln2_bias'], 'L0_ffn_gate_kernel': _L0_ffn_in['gate_kernel'], 'L0_ffn_w0': _L0_ffn_in['w0'], 'L0_ffn_w1': _L0_ffn_in['w1'], 'L0_ffn_wo': _L0_ffn_in['wo'], 'L1_attn_norm_weight': _L1_attn_in['norm_weight'], 'L1_attn_in_proj_w': _L1_attn_in['in_proj_w'], 'L1_attn_conv_w': _L1_attn_in['conv_w'], 'L1_attn_conv_b': _L1_attn_in['conv_b'], 'L1_attn_x_proj_w': _L1_attn_in['x_proj_w'], 'L1_attn_dt_proj_w': _L1_attn_in['dt_proj_w'], 'L1_attn_dt_proj_b': _L1_attn_in['dt_proj_b'], 'L1_attn_A_log': _L1_attn_in['A_log'], 'L1_attn_D': _L1_attn_in['D'], 'L1_attn_out_proj_w': _L1_attn_in['out_proj_w'], 'L1_ffn_w_router': _L1_ffn_in['w_router'], 'L1_ffn_gate_up_proj': _L1_ffn_in['gate_up_proj'], 'L1_ffn_down_proj': _L1_ffn_in['down_proj'], 'L1_ffn_w_gate': _L1_ffn_in['w_gate'], 'L1_ffn_w_up': _L1_ffn_in['w_up'], 'L1_ffn_w_down': _L1_ffn_in['w_down']}
    _x0 = _d['L0_attn_x']
    _d['L0_attn_x'] = jax.random.normal(jax.random.fold_in(jax.random.key(seed), 1), (2, 2048, 256), dtype=_x0.dtype)
    del _x0
    return _d

def reference(L0_attn_x, L0_attn_Wq, L0_attn_Wk, L0_attn_Wv, L0_attn_Wa, L0_attn_Wg, L0_attn_Wo, L0_attn_gn_scale, L0_attn_gn_bias, L0_attn_ln1_scale, L0_attn_ln1_bias, L0_attn_W1, L0_attn_b1, L0_attn_W2, L0_attn_b2, L0_attn_ln2_scale, L0_attn_ln2_bias, L0_ffn_gate_kernel, L0_ffn_w0, L0_ffn_w1, L0_ffn_wo, L1_attn_norm_weight, L1_attn_in_proj_w, L1_attn_conv_w, L1_attn_conv_b, L1_attn_x_proj_w, L1_attn_dt_proj_w, L1_attn_dt_proj_b, L1_attn_A_log, L1_attn_D, L1_attn_out_proj_w, L1_ffn_w_router, L1_ffn_gate_up_proj, L1_ffn_down_proj, L1_ffn_w_gate, L1_ffn_w_up, L1_ffn_w_down):

    def _L0_attn_ref(x, Wq, Wk, Wv, Wa, Wg, Wo, gn_scale, gn_bias, ln1_scale, ln1_bias, W1, b1, W2, b2, ln2_scale, ln2_bias):
        import jax, jax.numpy as jnp
        import numpy as np
        from jax.lax import associative_scan
        B, S, D, F, G = (4, 1024, 256, 1024, 32)
        EPS = 1e-06

        def _gate_loop(k, v, q, a):
            kv = (k * v).astype(jnp.complex64)

            def op(e1, e2):
                a1, x1 = e1
                a2, x2 = e2
                return (a1 * a2, a2 * x1 + x2)
            _, h = associative_scan(op, (a, kv), axis=1)
            return q.astype(jnp.complex64) * h

        def _layernorm(x, scale, bias):
            mu = jnp.mean(x, axis=-1, keepdims=True)
            var = jnp.mean(jnp.square(x - mu), axis=-1, keepdims=True)
            return (x - mu) * jax.lax.rsqrt(var + EPS) * scale + bias

        def _groupnorm_complex(y, scale, bias):
            b, s, d = y.shape
            yr = y.reshape(b, s, G, d // G)
            mean = jnp.mean(yr, axis=(1, 3), keepdims=True)
            mean2 = jnp.mean(yr.real ** 2 + yr.imag ** 2, axis=(1, 3), keepdims=True)
            var = mean2 - (mean.real ** 2 + mean.imag ** 2)
            yn = (yr - mean) * jax.lax.rsqrt(var + EPS)
            return yn.reshape(b, s, d) * scale + bias
        q = x @ Wq
        k = x @ Wk
        v = x @ Wv
        a = x @ Wa
        a_real, a_imag = jnp.split(a, 2, axis=-1)
        a_c = a_real + 1j * a_imag
        mag = jnp.abs(a_c)
        phase = jnp.angle(a_c)
        a_c = jax.nn.sigmoid(mag) * jnp.exp(1j * phase)
        g = (x @ Wg).astype(jnp.complex64)
        y = _gate_loop(k, v, q, a_c)
        y = _groupnorm_complex(y, gn_scale, gn_bias)
        silu_g = g / (1.0 + jnp.exp(-g))
        y = y * silu_g
        y = (y @ Wo.astype(jnp.complex64)).real
        x = _layernorm(x + y, ln1_scale, ln1_bias)
        h = jax.nn.gelu(x @ W1 + b1)
        out = x + (h @ W2 + b2)
        return _layernorm(out, ln2_scale, ln2_bias)

    def _L0_ffn_ref(inputs, gate_kernel, w0, w1, wo):
        import jax, jax.numpy as jnp
        import numpy as np
        NUM_EXPERTS = 64
        TOP_K = 2
        B, S, EMB, MLP = (4, 512, 256, 512)
        b, s, e = inputs.shape
        x = inputs.reshape(b * s, e)
        gate_logits = jnp.einsum('te,ex->tx', x, gate_kernel)
        weights, selected = jax.lax.top_k(gate_logits, TOP_K)
        weights = jax.nn.softmax(weights.astype(jnp.float32), axis=-1)
        flat_experts = selected.reshape(-1)
        sort_idx = jnp.argsort(flat_experts)
        token_idx = sort_idx // TOP_K
        sorted_x = jnp.take(x, token_idx, axis=0)
        group_sizes = jnp.bincount(flat_experts, length=NUM_EXPERTS).astype(jnp.int32)
        h0 = jax.lax.ragged_dot(sorted_x, w0, group_sizes)
        h1 = jax.lax.ragged_dot(sorted_x, w1, group_sizes)
        inter = jax.nn.silu(h0) * h1
        out_sorted = jax.lax.ragged_dot(inter, wo, group_sizes)
        unsorted = jnp.take(out_sorted, jnp.argsort(sort_idx), axis=0)
        per_tok = unsorted.reshape(b * s, TOP_K, e)
        out = jnp.einsum('BKE,BK->BE', per_tok.astype(jnp.float32), weights)
        return out.reshape(b, s, e)

    def _L1_attn_ref(hidden_states, norm_weight, in_proj_w, conv_w, conv_b, x_proj_w, dt_proj_w, dt_proj_b, A_log, D, out_proj_w):
        import jax, jax.numpy as jnp
        import numpy as np
        import math
        D_MODEL = 256
        D_STATE = 16
        D_CONV = 4
        EXPAND = 2
        D_INNER = EXPAND * D_MODEL
        DT_RANK = math.ceil(D_MODEL / 16)
        EPS = 1e-05

        def _rmsnorm(x, w):
            norm = jnp.linalg.norm(x, axis=-1, keepdims=True)
            rms = norm * (1.0 / math.sqrt(x.shape[-1]))
            return w * (x / (rms + EPS))

        def _mamba(h, in_proj_w, conv_w, conv_b, x_proj_w, dt_proj_w, dt_proj_b, A_log, D, out_proj_w):
            B, L, _ = h.shape
            xz = h @ in_proj_w.T
            x, z = jnp.split(xz, 2, axis=-1)
            xpad = jnp.pad(x, ((0, 0), (D_CONV - 1, 0), (0, 0)))
            xc = conv_b
            for k in range(D_CONV):
                xc = xc + xpad[:, k:k + L, :] * conv_w[:, k]
            xc = jax.nn.silu(xc)
            x_dbl = xc @ x_proj_w.T
            dt, Bm, Cm = jnp.split(x_dbl, [DT_RANK, DT_RANK + D_STATE], axis=-1)
            dt = jax.nn.softplus(dt @ dt_proj_w.T + dt_proj_b)
            A = -jnp.exp(A_log)
            deltaA = jnp.exp(dt[..., None] * A)
            deltaBu = (dt * xc)[..., None] * Bm[:, :, None, :]

            def step(hst, inp):
                dA, dBu, Ct = inp
                hst = dA * hst + dBu
                y = jnp.einsum('bdn,bn->bd', hst, Ct)
                return (hst, y)
            h0 = jnp.zeros((B, D_INNER, D_STATE), xc.dtype)
            _, ys = jax.lax.scan(step, h0, (deltaA.swapaxes(0, 1), deltaBu.swapaxes(0, 1), Cm.swapaxes(0, 1)))
            y = ys.swapaxes(0, 1)
            y = y + D * xc
            y = y * jax.nn.silu(z)
            return y @ out_proj_w.T

        def _reference_tuple_inner(hidden_states, norm_weight, in_proj_w, conv_w, conv_b, x_proj_w, dt_proj_w, dt_proj_b, A_log, D, out_proj_w):
            residual = hidden_states
            h = _rmsnorm(residual, norm_weight)
            out = _mamba(h, in_proj_w, conv_w, conv_b, x_proj_w, dt_proj_w, dt_proj_b, A_log, D, out_proj_w)
            return (out, residual)
        return _reference_tuple_inner(hidden_states, norm_weight, in_proj_w, conv_w, conv_b, x_proj_w, dt_proj_w, dt_proj_b, A_log, D, out_proj_w)[0]

    def _L1_ffn_ref(hidden_states, w_router, gate_up_proj, down_proj, w_gate, w_up, w_down):
        import jax, jax.numpy as jnp
        import numpy as np
        E = 16
        H = 256
        F = 512
        TOP_K = 1
        B, S = (2, 256)
        b, s, h = hidden_states.shape
        x = hidden_states.reshape(-1, h)
        logits = x @ w_router.T
        _, top_idx = jax.lax.top_k(logits, TOP_K)
        mask = jax.nn.one_hot(top_idx, E, dtype=logits.dtype).sum(axis=1)
        scores = jax.nn.sigmoid(logits) * mask
        masked_inputs = scores.T[:, :, None] * x[None, :, :]
        gate_up = jnp.einsum('eth,ehf->etf', masked_inputs, gate_up_proj)
        gate, up = jnp.split(gate_up, 2, axis=-1)
        expert_out = jnp.einsum('etf,efh->eth', up * jax.nn.silu(gate), down_proj)
        shared = jax.nn.silu(x @ w_gate.T) * (x @ w_up.T) @ w_down.T
        out = shared + expert_out.sum(axis=0)
        return out.reshape(b, s, h)
    x = L0_attn_x
    x = x + _L0_attn_ref(_layernorm(x, axis=-1), L0_attn_Wq, L0_attn_Wk, L0_attn_Wv, L0_attn_Wa, L0_attn_Wg, L0_attn_Wo, L0_attn_gn_scale, L0_attn_gn_bias, L0_attn_ln1_scale, L0_attn_ln1_bias, L0_attn_W1, L0_attn_b1, L0_attn_W2, L0_attn_b2, L0_attn_ln2_scale, L0_attn_ln2_bias)
    x = x + _L0_ffn_ref(_layernorm(x, axis=-1), L0_ffn_gate_kernel, L0_ffn_w0, L0_ffn_w1, L0_ffn_wo)
    x = x + _L1_attn_ref(_layernorm(x, axis=-1), L1_attn_norm_weight, L1_attn_in_proj_w, L1_attn_conv_w, L1_attn_conv_b, L1_attn_x_proj_w, L1_attn_dt_proj_w, L1_attn_dt_proj_b, L1_attn_A_log, L1_attn_D, L1_attn_out_proj_w)
    x = x + _L1_ffn_ref(_layernorm(x, axis=-1), L1_ffn_w_router, L1_ffn_gate_up_proj, L1_ffn_down_proj, L1_ffn_w_gate, L1_ffn_w_up, L1_ffn_w_down)
    return x

_drawn_inputs = setup_inputs


def setup_inputs(seed=0):
    import zlib

    import numpy as np

    out = dict(_drawn_inputs(seed))
    spreads = {'L0_attn_gn_scale': (1.0, 0.2),
     'L0_attn_gn_bias': (0.0, 0.1),
     'L0_attn_ln1_scale': (1.0, 0.2),
     'L0_attn_ln1_bias': (0.0, 0.1),
     'L0_attn_ln2_scale': (1.0, 0.2),
     'L0_attn_ln2_bias': (0.0, 0.1),
     'L1_attn_norm_weight': (1.0, 0.6),
     'L1_attn_conv_b': (0.0, 0.8),
     'L1_attn_D': (1.0, 0.6)}
    factors = {'L0_attn_b1': 8.0,
     'L0_attn_b2': 8.0,
     'L1_attn_in_proj_w': 8.0,
     'L1_attn_conv_w': 8.0,
     'L1_attn_x_proj_w': 8.0,
     'L1_attn_dt_proj_w': 8.0,
     'L1_attn_dt_proj_b': 8.0,
     'L1_attn_A_log': 8.0,
     'L1_attn_out_proj_w': 8.0,
     'L1_ffn_w_router': 8.0,
     'L1_ffn_gate_up_proj': 8.0,
     'L1_ffn_down_proj': 8.0,
     'L1_ffn_w_gate': 4.616,
     'L1_ffn_w_up': 4.533,
     'L1_ffn_w_down': 4.522}
    for name, (base, spread) in spreads.items():
        noise = np.random.default_rng([zlib.crc32(name.encode()), seed]).standard_normal(out[name].shape)
        drawn = base * np.exp(spread * noise) if base else spread * noise
        out[name] = jnp.asarray(drawn.astype(out[name].dtype))
    for name, factor in factors.items():
        out[name] = (out[name] * factor).astype(out[name].dtype)
    return out
```

```python
import math
from contextlib import ExitStack

import concourse.bass as bass
from concourse import mybir

F32 = mybir.dt.float32
BF16 = mybir.dt.bfloat16
I32 = mybir.dt.int32
U32 = mybir.dt.uint32
ALU = mybir.AluOpType
ACT = mybir.ActivationFunctionType
AX = mybir.AxisListType

P = 128
T = 4096
D = 256
KD = D // P
BATCH = 2
BT = 512
NB = T // BT
SB = NB // BATCH
TPB = BT // P
NT = T // P
ROUND = 12582912.0
RSQRT_SEED = float(0x5F3759DF)


class Chain:

    def __init__(self, engine, sem, base=0):
        self.engine, self.sem, self.base, self.n = engine, sem, base, 0

    def mark(self, ins):
        self.n += 1
        ins.then_inc(self.sem, 1)
        return self.n

    def wait(self, n):
        self.engine.wait_ge(self.sem, self.base + n)

    def link(self, ins):
        self.wait(self.mark(ins))


def rsqrt(nc, chain, out, v, tmp):
    V = nc.vector
    chain.link(V.tensor_scalar(tmp.bitcast(I32), v.bitcast(I32), 1, None, ALU.logical_shift_right))
    chain.link(V.tensor_scalar(out.bitcast(I32), tmp.bitcast(I32), -1.0, RSQRT_SEED, ALU.mult, ALU.add))
    for _ in range(3):
        chain.link(V.tensor_tensor(tmp, out, out, ALU.mult))
        chain.link(V.tensor_tensor(tmp, tmp, v, ALU.mult))
        chain.link(V.tensor_scalar(tmp, tmp, -0.5, 1.5, ALU.mult, ALU.add))
        chain.link(V.tensor_tensor(out, out, tmp, ALU.mult))


def norm_stats(nc, chain, src, stats, mv, rstd, tmp, eps, var=None):
    V = nc.vector
    n = stats.shape[1]
    for j in range(n):
        last = chain.mark(V.bn_stats(stats[:, j, :], src(j)))
    chain.wait(last)
    V.memset(tmp, 0.0)
    for j in range(n):
        last = chain.mark(V.bn_aggr(mv[:, j, :], stats[:, j, :]))
    chain.wait(last)
    if var is not None:
        chain.mark(V.tensor_copy(var, mv[:, :, 1]))
    chain.link(V.tensor_scalar(mv[:, :, 1], mv[:, :, 1], 1.0, eps, ALU.mult, ALU.add))
    rsqrt(nc, chain, rstd, mv[:, :, 1], tmp)


NORM_STEPS = 2 * TPB + 1 + 2 + 3 * 4


class Memory:

    def __init__(self, nc, stack, tag):
        self.nc, self.stack, self.tag, self.sems = nc, stack, tag, []

    def sb(self, name, shape, dt=F32):
        return self.stack.enter_context(self.nc.sbuf_tensor(f"{self.tag}_{name}", shape, dt))

    def ps(self, name, shape, dt=F32):
        return self.stack.enter_context(self.nc.psum_tensor(f"{self.tag}_{name}", shape, dt))

    def sem(self, name):
        self.sems.append(self.stack.enter_context(self.nc.semaphore(f"{self.tag}_{name}")))
        return self.sems[-1]

    def clear(self):
        with self.nc.Block() as block:

            @block.gpsimd
            def _(pool):
                for sem in self.sems:
                    pool.sem_clear(sem)


def gate_loop(nc, x_in, w_proj, XN, YS, SG, SUMS, ident):
    TURN = 2.0 * math.pi * (1.0 - 2.0 ** -23)
    AR, AI_, K_, V_, Q_, G_ = range(6)
    SEQ = [(AR, 0), (AI_, 0), (AR, 1), (AI_, 1), (K_, 0), (V_, 0), (K_, 1), (V_, 1), (Q_, 0), (G_, 0), (Q_, 1), (G_, 1)]
    RING = 6
    slot = {fc: n for n, fc in enumerate(SEQ)}
    with ExitStack() as stack:
        m_ = Memory(nc, stack, "gl")
        W = m_.sb("w", [P, KD, 6 * D])
        XB = m_.sb("xb", [P, TPB, D])
        XNB = m_.sb("xnb", [P, TPB, D])
        XT = m_.sb("xt", [P, KD, BT])
        stats, mv = m_.sb("stats", [P, TPB, 6]), m_.sb("mv", [P, TPB, 2])
        rstd, tmp = m_.sb("rstd", [P, TPB]), m_.sb("tmp", [P, TPB])
        SQR, SQI, AIM, ABR, KS, QS, KV, NEG, SGN, MAG, A, PHI, WR, SN, CS, UR, UI, T1, T2, T3, T4 = (
            m_.sb(n, [P, KD, BT]) for n in ("sqr", "sqi", "aim", "abr", "ks", "qs", "kv", "neg", "sgn", "mag",
                                            "a", "phi", "wr", "sn", "cs", "ur", "ui", "t1", "t2", "t3", "t4"))
        TAN, YI = SQI, MAG
        quarter = m_.sb("quarter", [P, 1])
        keep = m_.sb("keep", [P, NB + 1])
        c_phase, c_u = m_.sb("c_phase", [P, KD]), m_.sb("c_u", [P, KD, 2])
        pT = m_.ps("pT", [P, KD, BT])
        bank = [m_.ps(f"bank{i}", [P, BT]) for i in range(RING)]
        s = {n: m_.sem(n) for n in (
            "x_loaded", "w_loaded", "consts", "xn_done", "xt_raw", "xt_done", "sq_done", "m2_done", "mag_done",
            "t_done", "atan_done", "turn_done", "abs_done", "trig_done", "u_done", "hi_done", "pool_steps", "y_done", "steps")}
        bank_free = [m_.sem(f"bank_free{i}") for i in range(RING)]
        proj = [m_.sem(f"proj{i}") for i in range(6)]

        def freed(i, fc):
            return bank_free[slot[fc] % RING], i * 2 + (slot[fc] // RING + 2)

        with nc.Block() as block:

            @block.sync
            def _(sp):
                x_blocks = x_in.rearrange("(b t p) d -> b p t d", p=P, t=TPB)
                sp.dma_start(XB[:], x_blocks[0]).then_inc(s["x_loaded"], 16)
                sp.dma_start(W[:], w_proj.rearrange("(k p) n -> p k n", p=P)).then_inc(s["w_loaded"], 16)
                with sp.Fori(1, NB) as i:
                    sp.wait_ge(s["xn_done"], i * TPB)
                    sp.dma_start(XB[:], x_blocks[bass.ds(i, 1)].rearrange("b p t d -> (b p) t d"))\
                        .then_inc(s["x_loaded"], 16)

            @block.gpsimd
            def _(pool):
                pool.memset(ident[:], 0.0).then_inc(s["consts"], 1)
                pool.wait_ge(s["consts"], 1)
                pool.affine_select(out=ident[:], in_=ident[:], compare_op=ALU.not_equal, fill=1.0, base=0,
                                   pattern=[[-1, P]], channel_multiplier=1).then_inc(s["consts"], 1)
                pool.memset(quarter[:], math.pi / 2).then_inc(s["consts"], 1)
                with pool.Fori(0, NB) as i:
                    for c in range(KD):
                        n = i * KD + (c + 1)
                        pool.wait_ge(s["trig_done"], n)
                        pool.wait_ge(s["u_done"], n)
                        pool.tensor_tensor(T3[:, c], SN[:, c], UR[:, c], ALU.mult).then_inc(s["pool_steps"], 1)
                        pool.tensor_tensor(T4[:, c], CS[:, c], UI[:, c], ALU.mult).then_inc(s["pool_steps"], 1)
                        pool.wait_ge(s["pool_steps"], i * (2 * KD) + (2 * c + 2))
                        pool.tensor_tensor(T3[:, c], T3[:, c], T4[:, c], ALU.subtract).then_inc(s["hi_done"], 1)

            @block.tensor
            def _(pe):
                pe.wait_ge(s["consts"], 2)
                pe.wait_ge(s["w_loaded"], 16)
                for b in bank_free:
                    pe.sem_inc(b, 1)
                with pe.Fori(0, NB) as i:
                    pe.wait_ge(s["xn_done"], i * TPB + TPB)
                    for j in range(TPB):
                        for c in range(KD):
                            mm = pe.transpose(pT[:, c, j * P:(j + 1) * P], XNB[:, j, c * P:(c + 1) * P], ident[:])
                    mm.then_inc(s["xt_raw"], 1)
                    pe.wait_ge(s["xt_done"], i * KD + KD)
                    for n, (f, c) in enumerate(SEQ):
                        pe.wait_ge(bank_free[n % RING], i * 2 + (n // RING + 1))
                        for k in range(KD):
                            mm = pe.matmul(bank[n % RING][:], W[:, k, f * D + c * P:f * D + (c + 1) * P], XT[:, k],
                                           start=(k == 0), stop=(k == KD - 1))
                        mm.then_inc(proj[f], 1)

            @block.scalar
            def _(act):
                act.wait_ge(s["consts"], 3)
                A_ = nc.scalar.activation
                with act.Fori(0, NB) as i:
                    bank_of = lambda f, c: bank[slot[f, c] % RING][:]
                    free_of = lambda f, c: bank_free[slot[f, c] % RING]
                    act.wait_ge(s["xt_raw"], i + 1)
                    for c in range(KD):
                        A_(XT[:, c], pT[:, c], ACT.Copy).then_inc(s["xt_done"], 1)
                    A_(XN[:, bass.ds(i * TPB, TPB), :], XNB[:], ACT.Copy)
                    for c in range(KD):
                        act.wait_ge(proj[AR], i * KD + (c + 1))
                        A_(SQR[:, c], bank_of(AR, c), ACT.Square)
                        A_(ABR[:, c], bank_of(AR, c), ACT.Abs)
                        act.wait_ge(proj[AI_], i * KD + (c + 1))
                        A_(SQI[:, c], bank_of(AI_, c), ACT.Square).then_inc(s["sq_done"], 1)
                        A_(AIM[:, c], bank_of(AI_, c), ACT.Copy).then_inc(free_of(AI_, c), 1)
                    for c in range(KD):
                        act.wait_ge(proj[K_], i * KD + (c + 1))
                        A_(KS[:, c], bank_of(K_, c), ACT.Copy).then_inc(free_of(K_, c), 1)
                    for c in range(KD):
                        act.wait_ge(s["m2_done"], i * KD + (c + 1))
                        A_(MAG[:, c], SQR[:, c], ACT.Sqrt).then_inc(s["mag_done"], 1)
                    for c in range(KD):
                        act.wait_ge(s["mag_done"], i * KD + (c + 1))
                        A_(A[:, c], MAG[:, c], ACT.Sigmoid)
                    for c in range(KD):
                        act.wait_ge(s["t_done"], i * KD + (c + 1))
                        A_(PHI[:, c], TAN[:, c], ACT.Arctan).then_inc(s["atan_done"], 1)
                    for c in range(KD):
                        act.wait_ge(proj[Q_], i * KD + (c + 1))
                        A_(QS[:, c], bank_of(Q_, c), ACT.Copy).then_inc(free_of(Q_, c), 1)
                        act.wait_ge(proj[G_], i * KD + (c + 1))
                        A_(SG[:, c, bass.ds(i * BT, BT)], bank_of(G_, c), ACT.Silu).then_inc(free_of(G_, c), 1)
                    for c in range(KD):
                        act.wait_ge(s["turn_done"], i * KD + (c + 1))
                        A_(ABR[:, c], WR[:, c], ACT.Abs).then_inc(s["abs_done"], 1)
                        A_(SN[:, c], WR[:, c], ACT.Sin, scale=TURN)
                        act.wait_ge(s["abs_done"], i * KD + (c + 1))
                        A_(CS[:, c], ABR[:, c], ACT.Sin, scale=-TURN, bias=quarter[:]).then_inc(s["trig_done"], 1)

            @block.vector
            def _(dve):
                V = nc.vector
                pre = Chain(dve, s["steps"])
                pre.mark(V.memset(c_phase[:], 0.0))
                pre.mark(V.memset(c_u[:], 0.0))
                pre.link(V.memset(keep[:], 1.0))
                pre.link(V.memset(keep[:, SB:SB + 1], 0.0))
                dve.wait_ge(s["consts"], 3)
                PER = NORM_STEPS + 19 * KD
                with dve.Fori(0, NB) as i:
                    ch = Chain(dve, s["steps"], i * PER + pre.n)
                    def after(name, c):
                        dve.wait_ge(s[name], i * KD + (c + 1))
                    dve.wait_ge(s["x_loaded"], i * 16 + 16)
                    norm_stats(nc, ch, lambda j: XB[:, j], stats, mv, rstd[:], tmp[:], 1e-5)
                    for j in range(TPB):
                        V.tensor_scalar(XNB[:, j], XB[:, j],
                                        mv[:, j, 0:1], rstd[:, j:j + 1], ALU.subtract, ALU.mult).then_inc(s["xn_done"], 1)
                    for c in range(KD):
                        after("sq_done", c)
                        V.tensor_tensor(SQR[:, c], SQR[:, c], SQI[:, c], ALU.add).then_inc(s["m2_done"], 1)
                        V.tensor_scalar(NEG[:, c], bank[slot[AR, c] % RING][:], 0.0, 0.5, ALU.is_lt, ALU.mult)\
                            .then_inc(bank_free[slot[AR, c] % RING], 1)
                    for c in range(KD):
                        dve.wait_ge(*freed(i, (AR, c)))
                        ch.mark(V.tensor_scalar(SGN[:, c], NEG[:, c], -4.0 / math.pi, 1.0 / math.pi, ALU.mult, ALU.add))
                        dve.wait_ge(proj[V_], i * KD + (c + 1))
                        dve.wait_ge(*freed(i, (K_, c)))
                        V.tensor_tensor(KV[:, c], KS[:, c], bank[slot[V_, c] % RING][:], ALU.mult)\
                            .then_inc(bank_free[slot[V_, c] % RING], 1)
                    for c in range(KD):
                        after("mag_done", c)
                        ch.link(V.scalar_tensor_tensor(T1[:, c], ABR[:, c], 1e-30, MAG[:, c], ALU.add, ALU.add))
                        ch.link(V.reciprocal(T2[:, c], T1[:, c]))
                        V.tensor_tensor(TAN[:, c], AIM[:, c], T2[:, c], ALU.mult).then_inc(s["t_done"], 1)
                    for c in range(KD):
                        after("atan_done", c)
                        ch.link(V.tensor_tensor(T1[:, c], PHI[:, c], SGN[:, c], ALU.mult))
                        ch.link(V.tensor_tensor_scan(PHI[:, c], T1[:, c], NEG[:, c], c_phase[:, c:c + 1], ALU.add, ALU.add))
                        ch.link(V.tensor_scalar(T2[:, c], PHI[:, c], ROUND, ROUND, ALU.add, ALU.subtract))
                        V.tensor_tensor(WR[:, c], PHI[:, c], T2[:, c], ALU.subtract).then_inc(s["turn_done"], 1)
                        after("turn_done", c)
                        ch.mark(V.tensor_copy(c_phase[:, c:c + 1], WR[:, c, BT - 1:BT]))
                    for c in range(KD):
                        after("trig_done", c)
                        ch.mark(V.tensor_tensor(T1[:, c], KV[:, c], CS[:, c], ALU.mult))
                        ch.link(V.tensor_tensor(T2[:, c], KV[:, c], SN[:, c], ALU.mult))
                        ch.link(V.tensor_tensor_scan(UR[:, c], A[:, c], T1[:, c], c_u[:, c, 0:1], ALU.mult, ALU.add))
                        V.tensor_tensor_scan(UI[:, c], A[:, c], T2[:, c], c_u[:, c, 1:2], ALU.mult, ALU.add)\
                            .then_inc(s["u_done"], 1)
                        after("u_done", c)
                        ch.mark(V.tensor_scalar(c_u[:, c, 0:1], UR[:, c, BT - 1:BT], keep[:, bass.ds(i + 1, 1)], None, ALU.mult))
                        ch.mark(V.tensor_scalar(c_u[:, c, 1:2], UI[:, c, BT - 1:BT], keep[:, bass.ds(i + 1, 1)], None, ALU.mult))
                        ch.mark(V.tensor_tensor(T1[:, c], CS[:, c], UR[:, c], ALU.mult))
                        ch.link(V.tensor_tensor(T2[:, c], SN[:, c], UI[:, c], ALU.mult))
                        ch.link(V.tensor_tensor(T1[:, c], T1[:, c], T2[:, c], ALU.add))
                    for c in range(KD):
                        ys = YS[:, c, bass.ds(i * BT, BT)]
                        at = lambda n: SUMS[:, bass.ds((i * KD + c) * 4 + n, 1)]
                        ch.link(V.scalar_tensor_tensor(ys, T1[:, c], 1.0, QS[:, c], ALU.mult, ALU.mult, accum_out=at(0)))
                        ch.mark(V.scalar_tensor_tensor(T2[:, c], ys, 1.0, ys, ALU.mult, ALU.mult, accum_out=at(2)))
                        after("hi_done", c)
                        ch.link(V.scalar_tensor_tensor(YI[:, c], T3[:, c], 1.0, QS[:, c], ALU.mult, ALU.mult, accum_out=at(1)))
                        ch.link(V.scalar_tensor_tensor(T2[:, c], YI[:, c], 1.0, YI[:, c], ALU.mult, ALU.mult, accum_out=at(3)))
                assert ch.n == PER, ch.n
        m_.clear()


def gate_ffn(nc, g, X, YS, SG, SUMS, ident):
    F = 4 * D
    FC = F // P
    with ExitStack() as stack:
        m_ = Memory(nc, stack, "gf")
        WO, W1, W2 = m_.sb("wo", [P, KD, D]), m_.sb("w1", [P, KD, F]), m_.sb("w2", [P, FC, D])
        gns, gnb, b1 = m_.sb("gns", [P, KD]), m_.sb("gnb", [P, KD]), m_.sb("b1", [P, FC])
        rows = {n: m_.sb(n, [P, D]) for n in ("ln1s", "ln1b", "b2", "ln2s", "ln2b")}
        group = m_.sb("group", [P, P])
        ST, MEAN = m_.sb("st", [P, BATCH, KD, 4]), m_.sb("mean", [P, BATCH, KD, 4])
        VAR, SQ, RS, TMP = (m_.sb(n, [P, BATCH, KD]) for n in ("var", "sq", "rs", "tmp"))
        AB = m_.sb("ab", [P, NB, KD, 2])
        Z = m_.sb("z", [P, KD, BT])
        XB = m_.sb("xb", [P, TPB, D])
        R, R2, X1N, X1, O2N = (m_.sb(n, [P, TPB, D]) for n in ("r", "r2", "x1n", "x1", "o2n"))
        XT, H = m_.sb("xt", [P, KD, BT]), m_.sb("h", [P, FC, BT])
        stats, mv = m_.sb("stats", [P, TPB, 6]), m_.sb("mv", [P, TPB, 2])
        rstd, tmp = m_.sb("rstd", [P, TPB]), m_.sb("tmp2", [P, TPB])
        pO, pW, pT = (m_.ps(n, [P, TPB, D]) for n in ("pO", "pW", "pT"))
        pH = [m_.ps(f"pH{n}", [P, BT]) for n in range(2)]
        pTf = pT[:].rearrange("p (c a) d -> p c (a d)", c=KD)
        s = {n: m_.sem(n) for n in ("loaded", "group_done", "st_done", "mean_done", "steps", "z_steps", "z_done", "wo_done",
                                    "residual_done", "x_loaded", "x1n_done", "x1_done", "xt_raw", "xt_done", "h_ready", "h_free", "w2_done",
                                    "r2_done", "o2n_done", "out_done", "pool_steps", "act_steps")}
        row = lambda n: rows[n][:].unsqueeze(1).to_broadcast([P, TPB, D])
        blk = lambda buf, i: buf[:, bass.ds(i * TPB, TPB), :]

        with nc.Block() as block:

            @block.sync
            def _(sp):
                sp.dma_start(W1[:], g["W1"].rearrange("(k p) n -> p k n", p=P)).then_inc(s["loaded"], 16)
                sp.dma_start(W2[:], g["W2"].rearrange("(k p) n -> p k n", p=P)).then_inc(s["loaded"], 16)
                sp.dma_start(WO[:], g["Wo"].rearrange("(k p) n -> p k n", p=P)).then_inc(s["loaded"], 16)
                for dst, name in ((gns, "gn_scale"), (gnb, "gn_bias"), (b1, "b1")):
                    sp.dma_start(dst[:], g[name].rearrange("(k p) -> p k", p=P), allow_slow_non_contiguous=True)\
                        .then_inc(s["loaded"], 16)
                for name in rows:
                    sp.dma_start(rows[name][:], g[name].partition_broadcast(P)).then_inc(s["loaded"], 16)
                x_blocks = g["x"].rearrange("(b t p) d -> b p t d", p=P, t=TPB)
                sp.dma_start(XB[:], x_blocks[0]).then_inc(s["x_loaded"], 16)
                with sp.Fori(1, NB) as i:
                    sp.wait_ge(s["out_done"], i + 1)
                    sp.dma_start(XB[:], x_blocks[bass.ds(i, 1)].rearrange("b p t d -> (b p) t d"))\
                        .then_inc(s["x_loaded"], 16)
            LOADED = 16 * 11

            @block.gpsimd
            def _(pool):
                gm = group[:].rearrange("p (a b) -> p a b", b=8)
                pool.memset(group[:], 1.0 / (8 * (T // BATCH))).then_inc(s["pool_steps"], 1)
                pool.wait_ge(s["pool_steps"], 1)
                pool.affine_select(out=gm, in_=gm, compare_op=ALU.is_ge, fill=0.0, base=0,
                                   pattern=[[-8, P // 8], [0, 8]], channel_multiplier=1).then_inc(s["pool_steps"], 1)
                pool.wait_ge(s["pool_steps"], 2)
                pool.affine_select(out=gm, in_=gm, compare_op=ALU.is_ge, fill=0.0, base=7,
                                   pattern=[[8, P // 8], [0, 8]], channel_multiplier=-1).then_inc(s["group_done"], 1)
                pool.wait_ge(s["loaded"], LOADED)
                pool.sem_inc(s["out_done"], 1)

                def x1(i, base, first=False):
                    if not first:
                        pool.wait_ge(s["xt_raw"], i)
                    pool.wait_ge(s["x1n_done"], i * TPB + TPB)
                    ch = Chain(pool, s["pool_steps"], base)
                    ch.link(pool.tensor_tensor(X1[:], X1N[:], row("ln1s"), ALU.mult))
                    pool.tensor_tensor(X1[:], X1[:], row("ln1b"), ALU.add).then_inc(s["x1_done"], 1)
                    pool.wait_ge(s["x1_done"], i + 1)
                    pool.tensor_tensor(blk(X, i), X1[:], row("b2"), ALU.add).then_inc(s["residual_done"], 1)
                    pool.wait_ge(s["residual_done"], i + 1)

                def out(i, base):
                    pool.wait_ge(s["o2n_done"], i * TPB + 2 * TPB)
                    ch = Chain(pool, s["pool_steps"], base)
                    ch.link(pool.tensor_tensor(O2N[:], O2N[:], row("ln2s"), ALU.mult))
                    ch.link(pool.tensor_tensor(O2N[:], O2N[:], row("ln2b"), ALU.add))
                    pool.wait_ge(s["x_loaded"], i * 16 + 16)
                    pool.tensor_tensor(blk(X, i), XB[:], O2N[:], ALU.add).then_inc(s["out_done"], 1)

                x1(0, 2, first=True)
                with pool.Fori(1, NB) as i:
                    x1(i, i * 3)
                    out(i - 1, i * 3 + 1)
                out(NB - 1, NB * 3)

            @block.tensor
            def _(pe):
                pe.wait_ge(s["loaded"], LOADED)
                pe.wait_ge(s["group_done"], 1)
                pe.wait_ge(s["st_done"], BATCH)
                pe.matmul(pO[:].rearrange("p t d -> p (t d)")[:, 0:16], group[:], ST[:].rearrange("p b c f -> p (b c f)"),
                          start=True, stop=True).then_inc(s["mean_done"], 1)
                pe.sem_inc(s["h_free"], 2)
                pe.sem_inc(s["o2n_done"], TPB)

                def wo(i):
                    pe.wait_ge(s["z_done"], i * KD + KD)
                    for j in range(TPB):
                        for k in range(KD):
                            mm = pe.matmul(pO[:, j], Z[:, k, j * P:(j + 1) * P], WO[:, k], start=(k == 0), stop=(k == KD - 1))
                        mm.then_inc(s["wo_done"], 1)

                def turn(i):
                    pe.wait_ge(s["x1_done"], i + 1)
                    for c in range(KD):
                        for j in range(TPB):
                            mm = pe.transpose(pTf[:, c, j * P:(j + 1) * P], X1[:, j, c * P:(c + 1) * P], ident[:])
                    mm.then_inc(s["xt_raw"], 1)

                def ffn(i):
                    pe.wait_ge(s["xt_done"], i * KD + KD)
                    for f in range(FC):
                        pe.wait_ge(s["h_free"], i * FC + (f + 1))
                        for k in range(KD):
                            mm = pe.matmul(pH[f % 2][:], W1[:, k, f * P:(f + 1) * P], XT[:, k], start=(k == 0), stop=(k == KD - 1))
                        mm.then_inc(s["h_ready"], 1)
                    pe.wait_ge(s["h_free"], i * FC + (FC + 2))
                    pe.wait_ge(s["o2n_done"], i * TPB + TPB)
                    for j in range(TPB):
                        for f in range(FC):
                            mm = pe.matmul(pW[:, j], H[:, f, j * P:(j + 1) * P], W2[:, f], start=(f == 0), stop=(f == FC - 1))
                        mm.then_inc(s["w2_done"], 1)

                wo(0)
                turn(0)
                with pe.Fori(1, NB) as i:
                    wo(i)
                    ffn(i - 1)
                    turn(i)
                ffn(NB - 1)

            @block.scalar
            def _(act):
                act.wait_ge(s["loaded"], LOADED)

                def copy_xt(i):
                    act.wait_ge(s["xt_raw"], i + 1)
                    for c in range(KD):
                        nc.scalar.activation(XT[:, c], pTf[:, c], ACT.Copy).then_inc(s["xt_done"], 1)

                def gelu(i):
                    for f in range(FC):
                        act.wait_ge(s["h_ready"], i * FC + (f + 1))
                        nc.scalar.activation(H[:, f], pH[f % 2][:], ACT.Gelu_apprx_tanh, bias=b1[:, f:f + 1])\
                            .then_inc(s["h_free"], 1)

                copy_xt(0)
                with act.Fori(1, NB) as i:
                    gelu(i - 1)
                    copy_xt(i)
                gelu(NB - 1)

            @block.vector
            def _(dve):
                V = nc.vector
                pre = Chain(dve, s["steps"])
                for b in range(BATCH):
                    V.tensor_reduce(ST[:, b], SUMS[:].rearrange("p (b s c f) -> p b c f s", b=BATCH, s=SB, c=KD)[:, b], AX.X, ALU.add)\
                        .then_inc(s["st_done"], 1)
                dve.wait_ge(s["loaded"], LOADED)
                dve.wait_ge(s["mean_done"], 1)
                pre.link(V.tensor_copy(MEAN[:].rearrange("p b c f -> p (b c f)"), pO[:].rearrange("p t d -> p (t d)")[:, 0:16]))
                f_ = lambda n: MEAN[:, :, :, n]
                pre.link(V.tensor_tensor(VAR[:], f_(2), f_(3), ALU.add))
                pre.link(V.tensor_tensor(SQ[:], f_(0), f_(0), ALU.mult))
                pre.link(V.tensor_tensor(VAR[:], VAR[:], SQ[:], ALU.subtract))
                pre.link(V.tensor_tensor(SQ[:], f_(1), f_(1), ALU.mult))
                pre.link(V.tensor_tensor(VAR[:], VAR[:], SQ[:], ALU.subtract))
                pre.link(V.tensor_scalar(VAR[:], VAR[:], 1.0, 1e-6, ALU.mult, ALU.add))
                rsqrt(nc, pre, RS[:], VAR[:], TMP[:])
                gs = gns[:].unsqueeze(1).to_broadcast([P, BATCH, KD])
                gb = gnb[:].unsqueeze(1).to_broadcast([P, BATCH, KD])
                pre.link(V.tensor_tensor(RS[:], RS[:], gs, ALU.mult))
                pre.link(V.tensor_tensor(SQ[:], f_(0), RS[:], ALU.mult))
                pre.link(V.tensor_tensor(SQ[:], gb, SQ[:], ALU.subtract))
                for n, src in ((0, RS), (1, SQ)):
                    pre.link(V.tensor_copy(AB[:, :, :, n].rearrange("p (b s) c -> p b s c", b=BATCH),
                                           src[:].unsqueeze(2).to_broadcast([P, BATCH, SB, KD])))

                def z(i):
                    scale = lambda c, n: AB[:, bass.ds(i, 1), c, n] if not isinstance(i, int) else AB[:, i:i + 1, c, n]
                    for c in range(KD):
                        pre_z = V.tensor_scalar(Z[:, c], YS[:, c, bass.ds(i * BT, BT)], scale(c, 0), scale(c, 1), ALU.mult, ALU.add)
                        pre_z.then_inc(s["z_steps"], 1)
                        dve.wait_ge(s["z_steps"], i * KD + (c + 1))
                        V.tensor_tensor(Z[:, c], Z[:, c], SG[:, c, bass.ds(i * BT, BT)], ALU.mult).then_inc(s["z_done"], 1)

                def norm(i, base, psum, psum_done, residual, buf, out, out_done):
                    ch = Chain(dve, s["steps"], base)
                    for j in range(TPB):
                        if j % 2 == 0:
                            dve.wait_ge(s[psum_done], i * TPB + (j + 2))
                        last = ch.mark(V.tensor_tensor(buf[:, j], psum[:, j], residual(j), ALU.add))
                    ch.wait(last)
                    norm_stats(nc, ch, lambda j: buf[:, j], stats, mv, rstd[:], tmp[:], 1e-6)
                    for j in range(TPB):
                        V.tensor_scalar(out[:, j], buf[:, j], mv[:, j, 0:1], rstd[:, j:j + 1], ALU.subtract, ALU.mult)\
                            .then_inc(s[out_done], 1)

                PER = TPB + NORM_STEPS
                tile = lambda i: (lambda j: X[:, bass.ds(i * TPB + j, 1), :].rearrange("p o d -> p (o d)"))

                def first(i, base):
                    norm(i, base, pO, "wo_done", tile(i), R, X1N, "x1n_done")

                def second(i, base):
                    dve.wait_ge(s["out_done"], i + 1)
                    dve.wait_ge(s["residual_done"], i + 1)
                    norm(i, base, pW, "w2_done", tile(i), R2, O2N, "o2n_done")

                n0 = pre.n
                z(0)
                first(0, n0)
                z(1)
                with dve.Fori(1, NB - 1) as i:
                    dve.wait_ge(s["x1_done"], i)
                    first(i, (i * 2 - 1) * PER + n0)
                    z(i + 1)
                    second(i - 1, (i * 2) * PER + n0)
                dve.wait_ge(s["x1_done"], NB - 1)
                first(NB - 1, (2 * NB - 3) * PER + n0)
                second(NB - 2, (2 * NB - 2) * PER + n0)
                second(NB - 1, (2 * NB - 1) * PER + n0)
        m_.clear()


class Routing:

    def __init__(self, nc, stack, tag, experts, k):
        m_ = Memory(nc, stack, tag)
        self.E, self.K = experts, k
        self.tiles = (T * k + experts * (P - 1)) // P
        self.tiles += -self.tiles % 4
        self.slot = m_.sb("slot", [P, NT, k], I32)
        self.weight = m_.sb("weight", [P, NT, k])
        self.expert = m_.sb("expert", [1, P], I32)
        self.xs = nc.dram_tensor(f"{tag}_xs", (self.tiles * P, D), F32).ap()
        self.ys = nc.dram_tensor(f"{tag}_ys", (self.tiles * P, D), F32).ap()


def fill_zeros(nc, tag, routings):
    ZT = 4
    with ExitStack() as stack:
        m_ = Memory(nc, stack, tag)
        zeros = m_.sb("zeros", [P, ZT * D])
        made, filled = m_.sem("made"), m_.sem("filled")
        with nc.Block() as block:

            @block.gpsimd
            def _(pool):
                pool.memset(zeros[:], 0.0).then_inc(made, 1)

            @block.sync
            def _(sp):
                sp.wait_ge(made, 1)
                for r in routings:
                    xs = r.xs.rearrange("(q p t) d -> q p (t d)", p=P, t=ZT)
                    with sp.Fori(0, r.tiles // ZT) as q:
                        sp.dma_start(xs[bass.ds(q, 1)].rearrange("q p d -> (q p) d"), zeros[:]).then_inc(filled, 16)
                sp.wait_ge(filled, 16 * sum(r.tiles // ZT for r in routings))
        m_.clear()


def route(nc, tag, X, gate, r, ident, shared=None):
    E, K = r.E, r.K
    FS = 512 // P
    with ExitStack() as stack:
        m_ = Memory(nc, stack, tag)
        G = m_.sb("gate", [P, KD, E])
        iota_i, iota = m_.sb("iota_i", [P, E], I32), m_.sb("iota", [P, E])
        part_i, part = m_.sb("part_i", [P, 1], I32), m_.sb("part", [P, 1])
        tri, ones = m_.sb("tri", [P, P], BF16), m_.sb("ones", [P, P], BF16)
        onef = m_.sb("onef", [P, E])
        stats, mv = m_.sb("stats", [P, TPB, 6]), m_.sb("mv", [P, TPB, 2])
        rstd, tmp = m_.sb("rstd", [P, TPB]), m_.sb("tmp", [P, TPB])
        XN = m_.sb("xn", [P, TPB, D])
        XA, IDXA, RKA = m_.sb("xa", [P, NT, D]), m_.sb("idxa", [P, NT, K]), m_.sb("rka", [P, NT, K])
        XS = [m_.sb(f"xs{h}", [P, TPB, D]) for h in range(2)]
        SL = [m_.sb(f"sl{h}", [P, TPB, K], I32) for h in range(2)]
        BASE, pause = m_.sb("base", [P, TPB, K]), m_.sb("pause", [P, 1])
        XT = m_.sb("xt", [P, KD, BT])
        V8, I8 = m_.sb("v8", [P, TPB, 8]), m_.sb("i8", [P, TPB, 8], U32)
        IDX, RK = m_.sb("idx", [P, TPB, K]), m_.sb("rk", [P, TPB, K])
        DIF, EX, DEN, W0 = (m_.sb(n, [P, TPB]) for n in ("dif", "ex", "den", "w0"))
        OH0, OH, JUNK = m_.sb("oh0", [P, TPB, E], BF16), m_.sb("oh", [P, TPB, E], BF16), m_.sb("junk", [P, TPB * K, E])
        JUNKS = [JUNK[:, n] for n in range(TPB * K)]
        COUNT = m_.sb("count", [P, E])
        NTILE, END = m_.sb("ntile", [P, E]), m_.sb("end", [P, E])
        START, OWNER = m_.sb("start", [P, E]), m_.sb("owner", [P, 1])
        pT = m_.ps("pT", [P, KD, BT])
        pL, pR = m_.ps("pL", [P, BT]), m_.ps("pR", [P, BT])
        pLt = pL[:, 0:TPB * E].rearrange("p (t e) -> p t e", e=E)
        pRt = pR[:, 0:(TPB + 1) * E].rearrange("p (t e) -> p t e", e=E)
        names = ["loaded", "consts", "steps", "pool_steps", "xn_done", "xt_raw", "xt_done", "logits_done", "max_done",
                 "index_done", "dif_done", "exp_done", "onehot_done", "rank_done", "rows_ready", "passed",
                 "owner_done", "owner_turned", "expert_ready"]
        if shared:
            SW = [m_.sb(f"sw{n}", [P, KD, 512]) for n in range(2)]
            SD = m_.sb("sd", [P, FS, D])
            SIL, IN = m_.sb("sil", [P, BT]), m_.sb("in", [P, FS, BT])
            pG, pU, pS = m_.ps("pG", [P, BT]), m_.ps("pU", [P, BT]), m_.ps("pS", [P, TPB, D])
            names += ["gate_up", "silu_done", "inner_done", "shared_done", "shared_added"]
        s = {n: m_.sem(n) for n in names}
        sent = [m_.sem(f"sent{h}") for h in range(2)]
        SENT = 16 * TPB * K
        LOADED = 16 * (4 if shared else 1)

        with nc.Block() as block:

            @block.sync
            def _(sp):
                sp.dma_start(G[:], gate.rearrange("(k p) e -> p k e", p=P)).then_inc(s["loaded"], 16)
                if shared:
                    for dst, src in zip(SW, shared):
                        sp.dma_start(dst[:], src.rearrange("(k p) n -> p k n", p=P)).then_inc(s["loaded"], 16)
                    sp.dma_start(SD[:], shared[2].rearrange("(k p) n -> p k n", p=P)).then_inc(s["loaded"], 16)

            @block.gpsimd
            def _(pool):
                pool.memset(onef[:], 1.0)
                pool.memset(pause[:], 0.0)
                pool.memset(ones[:], 1.0)
                pool.memset(tri[:], 1.0).then_inc(s["pool_steps"], 1)
                pool.iota(iota_i[:], [[1, E]], base=0, channel_multiplier=0)
                pool.iota(part_i[:], [[0, 1]], base=0, channel_multiplier=1).then_inc(s["pool_steps"], 1)
                pool.wait_ge(s["pool_steps"], 2)
                pool.affine_select(out=tri[:], in_=tri[:], compare_op=ALU.is_gt, fill=0.0, base=0,
                                   pattern=[[1, P]], channel_multiplier=-1)
                pool.tensor_copy(iota[:], iota_i[:])
                pool.tensor_copy(part[:], part_i[:]).then_inc(s["consts"], 1)
                with pool.Fori(0, NB // 2) as i:
                    for h in range(2):
                        pool.wait_ge(s["rows_ready"], i * 2 + (h + 1))
                        pool.tensor_tensor(pause[:], onef[:, 0:1], onef[:, 0:1], ALU.add).then_inc(s["passed"], 1)
                        pool.wait_ge(s["passed"], 1)
                        pool.sem_clear(s["passed"])
                        for j in range(TPB):
                            for k in range(K):
                                pool.indirect_dma_start(r.xs, bass.IndirectOffsetOnAxis(ap=SL[h][:, j, k:k + 1], axis=0),
                                                        XS[h][:, j], None).then_inc(sent[h], 16)
                for h in range(2):
                    pool.wait_ge(sent[h], SENT * (NB // 2))

            @block.tensor
            def _(pe):
                pe.wait_ge(s["consts"], 1)
                pe.wait_ge(s["loaded"], LOADED)
                with pe.Fori(0, NB) as i:
                    n = lambda c: i * c
                    pe.wait_ge(s["xn_done"], n(TPB) + TPB)
                    for c in range(KD):
                        for j in range(TPB):
                            mm = pe.transpose(pT[:, c, j * P:(j + 1) * P], XN[:, j, c * P:(c + 1) * P], ident[:])
                    mm.then_inc(s["xt_raw"], 1)
                    pe.wait_ge(s["xt_done"], n(KD) + KD)
                    for j in range(TPB):
                        for k in range(KD):
                            mm = pe.matmul(pLt[:, j], XT[:, k, j * P:(j + 1) * P], G[:, k], start=(k == 0), stop=(k == KD - 1))
                    mm.then_inc(s["logits_done"], 1)
                    if shared:
                        for f in range(FS):
                            if f > 0:
                                pe.wait_ge(s["inner_done"], n(FS) + f)
                            for w, out in zip(SW, (pG, pU)):
                                for k in range(KD):
                                    mm = pe.matmul(out[:], w[:, k, f * P:(f + 1) * P], XT[:, k], start=(k == 0), stop=(k == KD - 1))
                            mm.then_inc(s["gate_up"], 1)
                    pe.wait_ge(s["onehot_done"], n(TPB) + TPB)
                    for j in range(TPB + 1):
                        pe.matmul(pRt[:, j], ident[:], COUNT[:], start=True, stop=False)
                        for q in range(j):
                            mm = pe.matmul(pRt[:, j], ones[:], OH[:, q], start=False, stop=(j == TPB and q == TPB - 1))
                        if j < TPB:
                            mm = pe.matmul(pRt[:, j], tri[:], OH[:, j], start=False, stop=True)
                    mm.then_inc(s["rank_done"], 1)
                    if shared:
                        pe.wait_ge(s["inner_done"], n(FS) + FS)
                        for j in range(TPB):
                            for f in range(FS):
                                mm = pe.matmul(pS[:, j], IN[:, f, j * P:(j + 1) * P], SD[:, f], start=(f == 0), stop=(f == FS - 1))
                        mm.then_inc(s["shared_done"], 1)
                pe.wait_ge(s["owner_done"], 1)
                pe.matmul(pL[0:1, 0:P], OWNER[:], ident[:], start=True, stop=True).then_inc(s["owner_turned"], 1)

            @block.scalar
            def _(act):
                with act.Fori(0, NB) as i:
                    n = lambda c: i * c
                    act.wait_ge(s["xt_raw"], n(1) + 1)
                    for c in range(KD):
                        nc.scalar.activation(XT[:, c], pT[:, c], ACT.Copy).then_inc(s["xt_done"], 1)
                    if K == 2:
                        nc.scalar.activation(XA[:, bass.ds(i * TPB, TPB), :], XN[:], ACT.Copy)
                    act.wait_ge(s["dif_done"], n(1) + 1)
                    nc.scalar.activation(EX[:], DIF[:], ACT.Exp).then_inc(s["exp_done"], 1)
                    if shared:
                        for f in range(FS):
                            act.wait_ge(s["gate_up"], n(FS) + (f + 1))
                            nc.scalar.activation(SIL[:], pG[:], ACT.Silu).then_inc(s["silu_done"], 1)

            @block.vector
            def _(dve):
                V = nc.vector
                pre = Chain(dve, s["steps"])
                dve.wait_ge(s["consts"], 1)
                pre.link(V.memset(COUNT[:], 0.0))
                n0 = pre.n
                PER = NORM_STEPS + 3 + 3 + (1 if K == 2 else TPB) + TPB * (K - 1) + TPB * K + 1
                with dve.Fori(0, NB) as i:
                    n = lambda c: i * c
                    ch = Chain(dve, s["steps"], n(PER) + n0)
                    tile = lambda j: X[:, bass.ds(i * TPB + j, 1), :].rearrange("p o d -> p (o d)")
                    norm_stats(nc, ch, tile, stats, mv, rstd[:], tmp[:], 1e-5)
                    for j in range(TPB):
                        V.tensor_scalar(XN[:, j], tile(j), mv[:, j, 0:1], rstd[:, j:j + 1], ALU.subtract, ALU.mult)\
                            .then_inc(s["xn_done"], 1)
                    dve.wait_ge(s["logits_done"], n(1) + 1)
                    V.memset(tmp[:], 0.0)
                    for j in range(TPB):
                        mx = V.max(V8[:, j], pLt[:, j])
                    mx.then_inc(s["max_done"], 1)
                    dve.wait_ge(s["max_done"], 1)
                    dve.sem_clear(s["max_done"])
                    for j in range(TPB):
                        mx = V.max_index(I8[:, j], V8[:, j], pLt[:, j])
                    mx.then_inc(s["index_done"], 1)
                    if K == 2:
                        V.tensor_tensor(DIF[:], V8[:, :, 1], V8[:, :, 0], ALU.subtract).then_inc(s["dif_done"], 1)
                    else:
                        V.tensor_scalar(DIF[:], V8[:, :, 0], -1.0, None, ALU.mult).then_inc(s["dif_done"], 1)
                    dve.wait_ge(s["index_done"], n(1) + 1)
                    ch.link(V.tensor_copy(IDX[:], I8[:, :, 0:K]))
                    for j in range(TPB):
                        out = OH[:, j] if K == 1 else OH0[:, j]
                        ins = V.tensor_scalar(out, iota[:], IDX[:, j, 0:1], None, ALU.is_equal)
                        if K == 1:
                            ins.then_inc(s["onehot_done"], 1)
                        else:
                            last = ch.mark(ins)
                    if K == 2:
                        ch.wait(last)
                        for j in range(TPB):
                            V.scalar_tensor_tensor(OH[:, j], iota[:], IDX[:, j, 1:2], OH0[:, j], ALU.is_equal, ALU.add)\
                                .then_inc(s["onehot_done"], 1)
                    dve.wait_ge(s["exp_done"], n(1) + 1)
                    ch.link(V.tensor_scalar(DEN[:], EX[:], 1.0, None, ALU.add))
                    ch.link(V.reciprocal(W0[:], DEN[:]))
                    ch.mark(V.tensor_scalar(r.weight[:, bass.ds(i * TPB, TPB), 0], W0[:], 1.0, None, ALU.mult))
                    if K == 2:
                        ch.mark(V.tensor_tensor(r.weight[:, bass.ds(i * TPB, TPB), 1], W0[:], EX[:], ALU.mult))
                    if K == 1:
                        for j in range(TPB):
                            ch.mark(V.tensor_scalar(XA[:, bass.ds(i * TPB + j, 1), :].rearrange("p o d -> p (o d)"),
                                                    XN[:, j], W0[:, j:j + 1], None, ALU.mult))
                    if shared:
                        for f in range(FS):
                            dve.wait_ge(s["silu_done"], n(FS) + (f + 1))
                            V.tensor_tensor(IN[:, f], SIL[:], pU[:], ALU.mult).then_inc(s["inner_done"], 1)
                    dve.wait_ge(s["rank_done"], n(1) + 1)
                    for j in range(TPB):
                        for k in range(K):
                            last = ch.mark(V.scalar_tensor_tensor(JUNKS[j * K + k], iota[:], IDX[:, j, k:k + 1], pRt[:, j],
                                                                  ALU.is_equal, ALU.mult, accum_out=RK[:, j, k:k + 1]))
                    ch.mark(V.tensor_copy(IDXA[:, bass.ds(i * TPB, TPB), :], IDX[:]))
                    last = ch.mark(V.tensor_copy(COUNT[:], pRt[:, TPB]))
                    ch.wait(last)
                    ch.mark(V.tensor_copy(RKA[:, bass.ds(i * TPB, TPB), :], RK[:]))
                    if shared:
                        dve.wait_ge(s["shared_done"], n(1) + 1)
                        xb = X[:, bass.ds(i * TPB, TPB), :]
                        V.tensor_tensor(xb, xb, pS[:], ALU.add).then_inc(s["shared_added"], 1)
                    assert ch.n == PER, (ch.n, PER)
                ch = Chain(dve, s["steps"], NB * PER + n0)
                ch.link(V.tensor_scalar(NTILE[:], COUNT[:], 1.0 / P, 0.5 - 0.5 / P, ALU.mult, ALU.add))
                ch.link(V.tensor_scalar(NTILE[:], NTILE[:], ROUND, ROUND, ALU.add, ALU.subtract))
                ch.link(V.tensor_tensor_scan(END[:], NTILE[:], NTILE[:], 0.0, ALU.add, ALU.bypass))
                ch.link(V.tensor_tensor(START[:], END[:], NTILE[:], ALU.subtract))
                ch.mark(V.tensor_scalar(START[:], START[:], float(P), None, ALU.mult))
                ch.link(V.scalar_tensor_tensor(JUNKS[0], END[:], part[:], onef[:], ALU.is_le, ALU.mult, accum_out=OWNER[:]))
                V.tensor_scalar(OWNER[:], OWNER[:], float(E - 1), None, ALU.min).then_inc(s["owner_done"], 1)
                n1 = ch.base + ch.n
                PER2 = TPB * K + 2
                def send(i, again):
                    for h in range(2):
                        ch = Chain(dve, s["steps"], (i * 2 + h) * PER2 + n1)
                        at = lambda buf: buf[:, bass.ds((i * 2 + h) * TPB, TPB), :]
                        if again:
                            dve.wait_ge(sent[h], i * SENT)
                        ch.mark(V.tensor_scalar(XS[h][:], at(XA), 1.0, None, ALU.mult))
                        for j in range(TPB):
                            for k in range(K):
                                expert = IDXA[:, bass.ds((i * 2 + h) * TPB + j, 1), k]
                                last = ch.mark(V.scalar_tensor_tensor(JUNKS[j * K + k], iota[:], expert, START[:],
                                                                      ALU.is_equal, ALU.mult, accum_out=BASE[:, j, k:k + 1]))
                        ch.wait(last)
                        ch.link(V.tensor_tensor(at(r.slot), BASE[:], at(RKA), ALU.add))
                        V.tensor_tensor(SL[h][:], BASE[:], at(RKA), ALU.add).then_inc(s["rows_ready"], 1)
                        dve.wait_ge(s["rows_ready"], i * 2 + (h + 1))

                send(0, False)
                with dve.Fori(1, NB // 2) as i:
                    send(i, True)
                dve.wait_ge(s["owner_turned"], 1)
                V.tensor_copy(r.expert[:], pL[0:1, 0:P]).then_inc(s["expert_ready"], 1)
        m_.clear()


def expert_tiles(nc, tag, r, w_gate, w_up, w_down, ident):
    BUF = 4
    FS = 512 // P
    N = r.tiles
    xs, ys = (a.rearrange("(t p) d -> t p d", p=P) for a in (r.xs, r.ys))
    assert N % BUF == 0
    with ExitStack() as stack:
        m_ = Memory(nc, stack, tag)
        ring = lambda name, shape, n=BUF: [m_.sb(f"{name}{b}", shape) for b in range(n)]
        WG, WU, WD = ring("wg", [P, KD, 512]), ring("wu", [P, KD, 512]), ring("wd", [P, FS, D])
        XR, Y = ring("xr", [P, D]), ring("y", [P, D])
        XT, SIL, IN = ring("xt", [P, KD, P], 2), ring("sil", [P, FS, P], 2), ring("in", [P, FS, P], 2)
        pT, pG, pU, pY = ([m_.ps(f"{n}{b}", [P, 512]) for b in range(2)] for n in ("pT", "pG", "pU", "pY"))
        s = {n: m_.sem(n) for n in ("xt_raw", "xt_done", "gate_done", "up_done", "silu_done", "inner_done", "down_done", "y_done")}
        x_loaded, w_loaded, stored = ([m_.sem(f"{n}{b}") for b in range(BUF)] for n in ("x_loaded", "w_loaded", "stored"))

        class Tile:

            def __init__(self, q, b):
                self.q, self.b, self.two = q, b, b % 2
                self.t = q * BUF + b

            def __add__(self, d):
                return Tile(self.q + (self.b + d) // BUF, (self.b + d) % BUF)

            def at_least(self, n):
                return not isinstance(self.q, int) or self.t >= n

        def steps(engine, body):
            for b in range(BUF):
                body(Tile(0, b), b == 0, False)
            with engine.Fori(1, N // BUF - 1) as q:
                for b in range(BUF):
                    body(Tile(q, b), False, False)
            for b in range(BUF):
                body(Tile(N // BUF - 1, b), False, b == BUF - 1)

        with nc.Block() as block:

            @block.sync
            def _(sp):
                def load(t, first, last):
                    if t.at_least(BUF):
                        sp.wait_ge(s["down_done"], t.t - (BUF - 1))
                    sp.dma_start(XR[t.b][:], xs[bass.ds(t.t, 1)].rearrange("t p d -> (t p) d")).then_inc(x_loaded[t.b], 16)
                    e = sp.value_load(r.expert[0:1, bass.ds(t.t, 1)], min_val=0, max_val=r.E - 1)
                    for dst, src in ((WG, w_gate), (WU, w_up), (WD, w_down)):
                        sp.dma_start(dst[t.b][:], src[bass.ds(e, 1)].rearrange("e (k p) n -> p (e k) n", p=P))\
                            .then_inc(w_loaded[t.b], 16)
                steps(sp, load)

            @block.tensor
            def _(pe):
                def turn(t):
                    pe.wait_ge(x_loaded[t.b], t.q * 16 + 16)
                    for k in range(KD):
                        mm = pe.transpose(pT[t.two][:, k * P:(k + 1) * P], XR[t.b][:, k * P:(k + 1) * P], ident[:])
                    mm.then_inc(s["xt_raw"], 1)

                def up(t):
                    pe.wait_ge(s["xt_done"], t.t + 1)
                    pe.wait_ge(w_loaded[t.b], t.q * 48 + 48)
                    for w, out, done in ((WG, pG, "gate_done"), (WU, pU, "up_done")):
                        for f in range(FS):
                            for k in range(KD):
                                mm = pe.matmul(out[t.two][:, f * P:(f + 1) * P], w[t.b][:, k, f * P:(f + 1) * P],
                                               XT[t.two][:, k], start=(k == 0), stop=(k == KD - 1))
                        mm.then_inc(s[done], 1)

                def down(t):
                    pe.wait_ge(s["inner_done"], t.t + 1)
                    if t.at_least(2):
                        pe.wait_ge(s["y_done"], t.t - 1)
                    for f in range(FS):
                        mm = pe.matmul(pY[t.two][:, 0:D], IN[t.two][:, f], WD[t.b][:, f], start=(f == 0), stop=(f == FS - 1))
                    mm.then_inc(s["down_done"], 1)

                def step(t, first, last):
                    if not last:
                        turn(t + 1)
                    up(t)
                    if not first:
                        down(t + -1)
                turn(Tile(0, 0))
                steps(pe, step)
                down(Tile(N // BUF - 1, BUF - 1))

            @block.scalar
            def _(act):
                def copy_xt(t):
                    act.wait_ge(s["xt_raw"], t.t + 1)
                    nc.scalar.activation(XT[t.two][:].rearrange("p k t -> p (k t)"), pT[t.two][:, 0:D], ACT.Copy)\
                        .then_inc(s["xt_done"], 1)

                def store(t):
                    act.wait_ge(s["y_done"], t.t + 1)
                    act.dma_start(ys[bass.ds(t.t, 1)].rearrange("t p d -> (t p) d"), Y[t.b][:]).then_inc(stored[t.b], 16)

                def step(t, first, last):
                    if not last:
                        copy_xt(t + 1)
                    act.wait_ge(s["gate_done"], t.t + 1)
                    if t.at_least(2):
                        act.wait_ge(s["inner_done"], t.t - 1)
                    nc.scalar.activation(SIL[t.two][:].rearrange("p f t -> p (f t)"), pG[t.two][:], ACT.Silu)\
                        .then_inc(s["silu_done"], 1)
                    if t.at_least(2):
                        store(t + -2)
                copy_xt(Tile(0, 0))
                steps(act, step)
                store(Tile(N // BUF - 1, BUF - 2))
                store(Tile(N // BUF - 1, BUF - 1))
                for b in range(BUF):
                    act.wait_ge(stored[b], 16 * (N // BUF))

            @block.vector
            def _(dve):
                def copy_y(t):
                    dve.wait_ge(s["down_done"], t.t + 1)
                    if t.at_least(BUF):
                        dve.wait_ge(stored[t.b], t.q * 16)
                    nc.vector.tensor_scalar(Y[t.b][:], pY[t.two][:, 0:D], 1.0, None, ALU.mult).then_inc(s["y_done"], 1)

                def step(t, first, last):
                    dve.wait_ge(s["silu_done"], t.t + 1)
                    dve.wait_ge(s["up_done"], t.t + 1)
                    if t.at_least(2):
                        dve.wait_ge(s["down_done"], t.t - 1)
                    nc.vector.tensor_tensor(IN[t.two][:].rearrange("p f t -> p (f t)"), SIL[t.two][:], pU[t.two][:], ALU.mult)\
                        .then_inc(s["inner_done"], 1)
                    if not first:
                        copy_y(t + -1)
                steps(dve, step)
                copy_y(Tile(N // BUF - 1, BUF - 1))
        m_.clear()


def combine(nc, tag, X, r, out=None):
    with ExitStack() as stack:
        m_ = Memory(nc, stack, tag)
        Y = [[m_.sb(f"y{h}{k}", [P, TPB, D]) for k in range(r.K)] for h in range(2)]
        SL = [m_.sb(f"sl{h}", [P, TPB * r.K], I32) for h in range(2)]
        copied = m_.sem("copied")
        fetched, added = ([m_.sem(f"{n}{h}") for h in range(2)] for n in ("fetched", "added"))
        stored = m_.sem("stored")
        ONE = 16 * TPB * r.K
        with nc.Block() as block:

            @block.gpsimd
            def _(pool):
                for h in range(2):
                    pool.sem_inc(added[h], TPB)
                with pool.Fori(0, NB // 2) as i:
                    for h in range(2):
                        pool.wait_ge(added[h], i * TPB + TPB)
                        pool.tensor_copy(SL[h][:], r.slot[:, bass.ds((i * 2 + h) * TPB, TPB), :].rearrange("p t k -> p (t k)"))\
                            .then_inc(copied, 1)
                        pool.wait_ge(copied, 1)
                        pool.sem_clear(copied)
                        for j in range(TPB):
                            for k in range(r.K):
                                n = j * r.K + k
                                pool.indirect_dma_start(Y[h][k][:, j], None, r.ys,
                                                        bass.IndirectOffsetOnAxis(ap=SL[h][:, n:n + 1], axis=0)).then_inc(fetched[h], 16)

            @block.vector
            def _(dve):
                V = nc.vector
                steps = m_.sem("steps")
                with dve.Fori(0, NB // 2) as i:
                    for h in range(2):
                        dve.wait_ge(fetched[h], i * ONE + ONE)
                        for j in range(TPB):
                            t = (i * 2 + h) * TPB + j
                            x = X[:, bass.ds(t, 1), :].rearrange("p o d -> p (o d)")
                            if r.K == 1:
                                V.tensor_tensor(x, x, Y[h][0][:, j], ALU.add).then_inc(added[h], 1)
                            else:
                                V.scalar_tensor_tensor(x, Y[h][0][:, j], r.weight[:, bass.ds(t, 1), 0], x, ALU.mult, ALU.add)\
                                    .then_inc(steps, 1)
                                dve.wait_ge(steps, i * (2 * TPB) + (h * TPB + j + 1))
                                V.scalar_tensor_tensor(x, Y[h][1][:, j], r.weight[:, bass.ds(t, 1), 1], x, ALU.mult, ALU.add)\
                                    .then_inc(added[h], 1)

            if out is not None:

                @block.sync
                def _(sp):
                    o = out.rearrange("(b t p) d -> b p t d", p=P, t=TPB)
                    with sp.Fori(0, NB // 2) as i:
                        for h in range(2):
                            sp.wait_ge(added[h], i * TPB + 2 * TPB)
                            sp.dma_start(o[bass.ds(i * 2 + h, 1)].rearrange("b p t d -> (b p) t d"),
                                         X[:, bass.ds((i * 2 + h) * TPB, TPB), :]).then_inc(stored, 16)
                    sp.wait_ge(stored, 16 * NB)
        m_.clear()


def state_space(nc, g, X, ident):
    DI = 2 * D
    CI = DI // P
    N = 16
    TAPS = 4
    with ExitStack() as stack:
        m_ = Memory(nc, stack, "ss")
        WI, WO = m_.sb("wi", [P, KD, 2 * DI]), m_.sb("wo", [P, CI, D])
        WX, WT = m_.sb("wx", [P, CI, P]), m_.sb("wt", [N, DI])
        norm_w = m_.sb("norm_w", [P, KD])
        conv_w, conv_b, dt_b, skip = m_.sb("conv_w", [P, CI, TAPS]), m_.sb("conv_b", [P, CI]), m_.sb("dt_b", [P, CI]), m_.sb("skip", [P, CI])
        DECAY = m_.sb("decay", [P, CI, N])
        SEL = m_.sb("sel", [P, 2 * N, P], BF16)
        keep = m_.sb("keep", [P, NB + 1])
        stats, mv = m_.sb("stats", [P, TPB, 6]), m_.sb("mv", [P, TPB, 2])
        rstd, tmp, var, rms = (m_.sb(n, [P, TPB]) for n in ("rstd", "tmp", "var", "rms"))
        HN, HT = m_.sb("hn", [P, TPB, D]), m_.sb("ht", [P, KD, BT])
        XR = m_.sb("xr", [P, CI, TAPS - 1 + BT])
        XC, ZS, DT, DTX, DBU, YZ = (m_.sb(n, [P, CI, BT]) for n in ("xc", "zs", "dt", "dtx", "dbu", "yz"))
        DA, H, PR = ([m_.sb(f"{n}{b}", [P, CI, BT]) for b in range(2)] for n in ("da", "h", "pr"))
        CS = [m_.sb(f"cs{b}", [P, BT]) for b in range(2)]
        CV, EX, SUM1, LN1, U = DBU, DA[0], DA[1], PR[0], PR[1]
        DR, R1 = m_.sb("dr", [N, BT]), m_.sb("r1", [P, BT])
        BC, BC2 = m_.sb("bc", [P, BT], BF16), m_.sb("bc2", [P, BT], BF16)
        c_h = m_.sb("c_h", [P, N, CI])
        y = m_.ps("y", [P, CI, BT])
        bB, bC = m_.ps("bB", [P, 2, BT]), m_.ps("bC", [P, 2, BT])
        x_bank = [y[:, 2], y[:, 3], bB[:, 0], bB[:, 1]]
        z_bank = [bC[:, 0], bC[:, 1], y[:, 0], y[:, 1]]
        xp_bank = y[:, 2]
        dt_bank = [y[:, 3], bB[:, 0], bB[:, 1], bC[:, 0]]
        po = bB[:].rearrange("p b (t d) -> p (b t) d", d=D)
        s = {n: m_.sem(n) for n in (
            "loaded", "sel_steps", "decay_done", "steps", "h_done", "ht_raw", "ht_done", "x_raw", "x_done", "z_raw", "z_done",
            "conv_done", "xc_done", "xp_raw", "bc1_done", "bc_done", "dt_raw", "abs_done", "u_done", "exp_done", "sum1_done", "ln_done",
            "dt_done", "spread", "c_copied", "da_done", "dbu_done", "h_scanned", "pr_done", "summed", "skip_done", "yz_done", "out_raw", "out_done")}

        with nc.Block() as block:

            @block.sync
            def _(sp):
                for dst, src in ((WI, g["in_w"]), (WO, g["out_w"]), (WX, g["xp_w"])):
                    sp.dma_start(dst[:], src.rearrange("(k p) n -> p k n", p=P)).then_inc(s["loaded"], 16)
                sp.dma_start(WT[:], g["dt_w"]).then_inc(s["loaded"], 16)
                for dst, name in ((DECAY, "A_log"), (conv_w, "conv_w")):
                    sp.dma_start(dst[:], g[name].rearrange("(c p) n -> p c n", p=P)).then_inc(s["loaded"], 16)
                for dst, name in ((norm_w, "norm_weight"), (conv_b, "conv_b"), (dt_b, "dt_b"), (skip, "skip")):
                    sp.dma_start(dst[:], g[name].rearrange("(c p) -> p c", p=P), allow_slow_non_contiguous=True)\
                        .then_inc(s["loaded"], 16)
            LOADED = 16 * 10

            @block.gpsimd
            def _(pool):
                pool.memset(SEL[:], 0.0).then_inc(s["sel_steps"], 1)
                for part in range(1, 4):
                    pool.wait_ge(s["sel_steps"], part)
                    pool.affine_select(out=SEL[:], in_=SEL[:], compare_op=ALU.not_equal, fill=1.0, base=-32 * part,
                                       pattern=[[-1, 2 * N], [0, P]], channel_multiplier=1).then_inc(s["sel_steps"], 1)
                pool.sem_inc(s["out_done"], 1)
                pool.sem_inc(s["yz_done"], CI)
                with pool.Fori(0, NB) as i:
                    for n in range(N):
                        pool.wait_ge(s["h_scanned"], i * N + (n + 1))
                        pool.wait_ge(s["c_copied"], i * N + (n + 1))
                        pool.wait_ge(s["summed"], i * N + (n + 1))
                        pool.tensor_tensor(PR[n % 2][:], H[n % 2][:], CS[n % 2][:].unsqueeze(1).to_broadcast([P, CI, BT]), ALU.mult)\
                            .then_inc(s["pr_done"], 1)
                    for c in range(CI):
                        pool.wait_ge(s["skip_done"], i * CI + (c + 1))
                        pool.tensor_tensor(YZ[:, c], YZ[:, c], ZS[:, c], ALU.mult).then_inc(s["yz_done"], 1)

            @block.tensor
            def _(pe):
                pe.wait_ge(s["loaded"], LOADED)
                pe.wait_ge(s["sel_steps"], 4)
                pe.sem_inc(s["summed"], 2)

                def project(out, w, col, rhs, chunks):
                    for k in range(chunks):
                        mm = pe.matmul(out, w[:, k, col:col + P], rhs[:, k], start=(k == 0), stop=(k == chunks - 1))
                    return mm

                with pe.Fori(0, NB) as i:
                    pe.wait_ge(s["h_done"], i * TPB + TPB)
                    pe.wait_ge(s["out_done"], i + 1)
                    for c in range(KD):
                        for j in range(TPB):
                            mm = pe.transpose(y[:, c, j * P:(j + 1) * P], HN[:, j, c * P:(c + 1) * P], ident[:])
                    mm.then_inc(s["ht_raw"], 1)
                    pe.wait_ge(s["ht_done"], i * KD + KD)
                    for c in range(CI):
                        project(x_bank[c], WI, c * P, HT, KD).then_inc(s["x_raw"], 1)
                    for c in range(CI):
                        project(z_bank[c], WI, DI + c * P, HT, KD).then_inc(s["z_raw"], 1)
                    pe.wait_ge(s["xc_done"], i * CI + CI)
                    project(xp_bank, WX, 0, XC, CI).then_inc(s["xp_raw"], 1)
                    pe.wait_ge(s["z_done"], i * CI + CI)
                    pe.wait_ge(s["bc1_done"], i + 1)
                    for c in range(CI):
                        pe.matmul(dt_bank[c], WT[:, c * P:(c + 1) * P], DR[:], start=True, stop=True).then_inc(s["dt_raw"], 1)
                    pe.wait_ge(s["bc_done"], i + 1)
                    pe.wait_ge(s["abs_done"], i * CI + CI)
                    pe.wait_ge(s["u_done"], i * CI + CI)

                    def spread(n):
                        if n >= 2:
                            pe.wait_ge(s["dbu_done"], i * N + (n - 1))
                            pe.wait_ge(s["c_copied"], i * N + (n - 1))
                        pe.matmul(bB[:, n % 2], SEL[:, n], BC[:], start=True, stop=True)
                        pe.matmul(bC[:, n % 2], SEL[:, N + n], BC[:], start=True, stop=True).then_inc(s["spread"], 1)
                    spread(0)
                    for n in range(N):
                        if n + 1 < N:
                            spread(n + 1)
                        pe.wait_ge(s["pr_done"], i * N + (n + 1))
                        for c in range(CI):
                            mm = pe.matmul(y[:, c], ident[:], PR[n % 2][:, c], start=(n == 0), stop=(n == N - 1))
                        mm.then_inc(s["summed"], 1)
                    pe.wait_ge(s["yz_done"], i * CI + 2 * CI)
                    for j in range(TPB):
                        for c in range(CI):
                            mm = pe.matmul(po[:, j], YZ[:, c, j * P:(j + 1) * P], WO[:, c], start=(c == 0), stop=(c == CI - 1))
                    mm.then_inc(s["out_raw"], 1)

            @block.scalar
            def _(act):
                A_ = nc.scalar.activation
                act.wait_ge(s["loaded"], LOADED)
                A_(DECAY[:], DECAY[:], ACT.Exp).then_inc(s["decay_done"], 1)
                act.wait_ge(s["decay_done"], 2)
                with act.Fori(0, NB) as i:
                    act.wait_ge(s["ht_raw"], i + 1)
                    for c in range(KD):
                        A_(HT[:, c], y[:, c], ACT.Copy, scale=norm_w[:, c:c + 1]).then_inc(s["ht_done"], 1)
                    act.wait_ge(s["conv_done"], i * CI + 1)
                    for c in range(CI):
                        act.wait_ge(s["x_raw"], i * CI + (c + 1))
                        A_(XR[:, c, TAPS - 1:], x_bank[c], ACT.Copy).then_inc(s["x_done"], 1)
                    act.wait_ge(s["yz_done"], i * CI + CI)
                    for c in range(CI):
                        act.wait_ge(s["z_raw"], i * CI + (c + 1))
                        A_(ZS[:, c], z_bank[c], ACT.Silu).then_inc(s["z_done"], 1)
                    for c in range(CI):
                        act.wait_ge(s["conv_done"], i * CI + (c + 2))
                        A_(XC[:, c], CV[:, c], ACT.Silu).then_inc(s["xc_done"], 1)
                    act.wait_ge(s["xp_raw"], i + 1)
                    A_(BC[:], xp_bank, ACT.Copy)
                    A_(DR[:], xp_bank[0:N], ACT.Copy).then_inc(s["bc1_done"], 1)
                    for c in range(CI):
                        act.wait_ge(s["dt_raw"], i * CI + (c + 1))
                        A_(EX[:, c], dt_bank[c], ACT.Abs, bias=dt_b[:, c:c + 1]).then_inc(s["abs_done"], 1)
                        A_(U[:, c], dt_bank[c], ACT.Identity, bias=dt_b[:, c:c + 1]).then_inc(s["u_done"], 1)
                    act.wait_ge(s["abs_done"], i * CI + CI)
                    A_(EX[:], EX[:], ACT.Exp, scale=-1.0).then_inc(s["exp_done"], 1)
                    act.wait_ge(s["sum1_done"], i + 1)
                    A_(LN1[:], SUM1[:], ACT.Ln).then_inc(s["ln_done"], 1)
                    act.wait_ge(s["dt_done"], i + 1)
                    for n in range(N):
                        if n >= 2:
                            act.wait_ge(s["h_scanned"], i * N + (n - 1))
                        for c in range(CI):
                            ins = A_(DA[n % 2][:, c], DT[:, c], ACT.Exp, scale=DECAY[:, c, n:n + 1])
                        ins.then_inc(s["da_done"], 1)
                        act.wait_ge(s["spread"], i * N + (n + 1))
                        if n >= 2:
                            act.wait_ge(s["pr_done"], i * N + (n - 1))
                        A_(CS[n % 2][:], bC[:, n % 2], ACT.Copy).then_inc(s["c_copied"], 1)

            @block.vector
            def _(dve):
                V = nc.vector
                pre = Chain(dve, s["steps"])
                pre.link(V.memset(keep[:], 1.0))
                pre.link(V.memset(keep[:, SB:SB + 1], 0.0))
                pre.mark(V.memset(c_h[:], 0.0))
                pre.link(V.memset(XR[:], 0.0))
                dve.sem_inc(s["conv_done"], 1)
                dve.wait_ge(s["decay_done"], 1)
                V.tensor_scalar(DECAY[:], DECAY[:], -1.0, None, ALU.mult).then_inc(s["decay_done"], 1)
                n0 = pre.n
                PER = NORM_STEPS + 1 + 20 + CI * (TAPS - 1) + 1 + 3 + 3 + N
                with dve.Fori(0, NB) as i:
                    ch = Chain(dve, s["steps"], i * PER + n0)
                    tile = lambda j: X[:, bass.ds(i * TPB + j, 1), :].rearrange("p o d -> p (o d)")
                    norm_stats(nc, ch, tile, stats, mv, rstd[:], tmp[:], 1e-5, var=var[:])
                    ch.link(V.tensor_tensor(var[:], var[:], rstd[:], ALU.mult))
                    ch.link(V.tensor_tensor(var[:], var[:], rstd[:], ALU.mult))
                    rsqrt(nc, ch, rms[:], var[:], tmp[:])
                    ch.link(V.tensor_tensor(rms[:], rms[:], var[:], ALU.mult))
                    ch.link(V.tensor_scalar(rms[:], rms[:], 1e-5, None, ALU.add))
                    ch.link(V.reciprocal(tmp[:], rms[:]))
                    ch.link(V.tensor_tensor(rstd[:], rstd[:], tmp[:], ALU.mult))
                    for j in range(TPB):
                        V.tensor_scalar(HN[:, j], tile(j), mv[:, j, 0:1], rstd[:, j:j + 1], ALU.subtract, ALU.mult)\
                            .then_inc(s["h_done"], 1)
                    for c in range(CI):
                        dve.wait_ge(s["x_done"], i * CI + (c + 1))
                        ch.link(V.tensor_scalar(CV[:, c], XR[:, c, 0:BT], conv_w[:, c, 0:1], conv_b[:, c:c + 1], ALU.mult, ALU.add))
                        for t in range(1, TAPS):
                            ins = V.scalar_tensor_tensor(CV[:, c], XR[:, c, t:t + BT], conv_w[:, c, t:t + 1], CV[:, c], ALU.mult, ALU.add)
                            if t < TAPS - 1:
                                ch.link(ins)
                        if c < CI - 1:
                            ins.then_inc(s["conv_done"], 1)
                    ch.link(ins)
                    V.tensor_scalar(XR[:, :, 0:TAPS - 1], XR[:, :, BT:], keep[:, bass.ds(i + 1, 1)], None, ALU.mult)\
                        .then_inc(s["conv_done"], 1)
                    dve.wait_ge(s["bc1_done"], i + 1)
                    ch.link(V.tensor_tensor(R1[:], xp_bank, BC[:], ALU.subtract))
                    ch.link(V.tensor_scalar(BC2[:], R1[:], 1.0, None, ALU.mult))
                    ch.mark(V.tensor_scalar(BC[2 * 32:3 * 32], BC2[2 * 32:3 * 32], 1.0, None, ALU.mult))
                    V.tensor_tensor(BC[3 * 32:], R1[3 * 32:], BC2[3 * 32:], ALU.subtract).then_inc(s["bc_done"], 1)
                    dve.wait_ge(s["exp_done"], i + 1)
                    V.tensor_scalar(SUM1[:], EX[:], 1.0, None, ALU.add).then_inc(s["sum1_done"], 1)
                    dve.wait_ge(s["sum1_done"], i + 1)
                    ch.link(V.scalar_tensor_tensor(DT[:], SUM1[:], 1.0, EX[:], ALU.subtract, ALU.subtract))
                    ch.link(V.scalar_tensor_tensor(DT[:], U[:], 0.0, DT[:], ALU.max, ALU.subtract))
                    dve.wait_ge(s["ln_done"], i + 1)
                    V.tensor_tensor(DT[:], DT[:], LN1[:], ALU.add).then_inc(s["dt_done"], 1)
                    dve.wait_ge(s["dt_done"], i + 1)
                    ch.link(V.tensor_tensor(DTX[:], DT[:], XC[:], ALU.mult))
                    for n in range(N):
                        dve.wait_ge(s["spread"], i * N + (n + 1))
                        V.tensor_tensor(DBU[:], DTX[:], bB[:, n % 2].unsqueeze(1).to_broadcast([P, CI, BT]), ALU.mult)\
                            .then_inc(s["dbu_done"], 1)
                        dve.wait_ge(s["dbu_done"], i * N + (n + 1))
                        dve.wait_ge(s["da_done"], i * N + (n + 1))
                        if n >= 2:
                            dve.wait_ge(s["pr_done"], i * N + (n - 1))
                        for c in range(CI):
                            ins = V.tensor_tensor_scan(H[n % 2][:, c], DA[n % 2][:, c], DBU[:, c], c_h[:, n, c:c + 1], ALU.mult, ALU.add)
                        ins.then_inc(s["h_scanned"], 1)
                        dve.wait_ge(s["h_scanned"], i * N + (n + 1))
                        ch.mark(V.tensor_scalar(c_h[:, n, :], H[n % 2][:, :, BT - 1], keep[:, bass.ds(i + 1, 1)], None, ALU.mult))
                    dve.wait_ge(s["summed"], i * N + (N + 2))
                    dve.wait_ge(s["out_done"], i + 1)
                    for c in range(CI):
                        V.scalar_tensor_tensor(YZ[:, c], XC[:, c], skip[:, c:c + 1], y[:, c], ALU.mult, ALU.add).then_inc(s["skip_done"], 1)
                    dve.wait_ge(s["out_raw"], i + 1)
                    x = X[:, bass.ds(i * TPB, TPB), :]
                    V.tensor_tensor(x, x, po, ALU.add).then_inc(s["out_done"], 1)
                    assert ch.n == PER, ch.n
        m_.clear()



def build(nc, g, out):
    with ExitStack() as stack:
        m_ = Memory(nc, stack, "all")
        ident = m_.sb("ident", [P, P])
        X = m_.sb("x", [P, NT, D])
        r0, r1 = Routing(nc, stack, "moe0", 64, 2), Routing(nc, stack, "moe1", 16, 1)
        fill_zeros(nc, "fill", [r0, r1])
        with ExitStack() as inner:
            m_ = Memory(nc, inner, "attn")
            YS, SG = m_.sb("ys", [P, KD, T]), m_.sb("sg", [P, KD, T])
            SUMS = m_.sb("sums", [P, NB * KD * 4])
            gate_loop(nc, g["x"], g["w_proj"], X, YS, SG, SUMS, ident)
            gate_ffn(nc, g, X, YS, SG, SUMS, ident)
        route(nc, "route0", X, g["router0"], r0, ident)
        expert_tiles(nc, "experts0", r0, g["w0"], g["w1"], g["wo"], ident)
        combine(nc, "combine0", X, r0)
        state_space(nc, g, X, ident)
        route(nc, "route1", X, g["router1"], r1, ident, shared=(g["sh_gate"], g["sh_up"], g["sh_down"]))
        half = g["gate_up"].shape[2] // 2
        expert_tiles(nc, "experts1", r1, g["gate_up"][:, :, 0:half], g["gate_up"][:, :, half:], g["down"], ident)
        combine(nc, "combine1", X, r1, out=out)


def mamba_layout(inputs):
    import numpy as np
    L = lambda n: np.asarray(inputs["L1_attn_" + n])
    w = L("x_proj_w")
    return {"in_w": L("in_proj_w").T, "out_w": L("out_proj_w").T, "dt_w": L("dt_proj_w").T,
            "xp_w": np.concatenate([w[:16], w[:16], w[16:], w[16:], w[16:]]).T,
            "A_log": L("A_log"), "conv_w": L("conv_w"), "norm_weight": L("norm_weight"), "conv_b": L("conv_b"),
            "dt_b": L("dt_proj_b"), "skip": L("D")}


def layout(inputs):
    import numpy as np
    g = mamba_layout(inputs)
    A = lambda n: np.asarray(inputs["L0_attn_" + n])
    F = lambda n: np.asarray(inputs["L1_ffn_" + n])
    g["x"] = A("x").reshape(T, D)
    g["w_proj"] = np.concatenate([A("Wa"), A("Wk"), A("Wv"), A("Wq"), A("Wg")], axis=1)
    for ours, theirs in (("Wo", "Wo"), ("gn_scale", "gn_scale"), ("gn_bias", "gn_bias"), ("W1", "W1"), ("W2", "W2"),
                         ("b1", "b1"), ("b2", "b2"), ("ln1s", "ln1_scale"), ("ln1b", "ln1_bias"),
                         ("ln2s", "ln2_scale"), ("ln2b", "ln2_bias")):
        g[ours] = A(theirs)
    g["router0"] = inputs["L0_ffn_gate_kernel"]
    for n in ("w0", "w1", "wo"):
        g[n] = inputs["L0_ffn_" + n]
    g["router1"], g["gate_up"], g["down"] = F("w_router").T, F("gate_up_proj"), F("down_proj")
    g["sh_gate"], g["sh_up"], g["sh_down"] = F("w_gate").T, F("w_up").T, F("w_down").T
    return g


_OUTS = [((BATCH, T // BATCH, D), "float32")]


def kernel(**inputs):
    import numpy as _np
    import concourse.bacc as _bacc
    from concourse.bass_utils import run_bass_kernel_spmd as _run

    given = layout(inputs)
    nc = _bacc.Bacc("TRN2", target_bir_lowering=False, num_devices=1)
    arrays, args = {}, {}
    for name, a in given.items():
        a = _np.ascontiguousarray(a)
        arrays[f"in_{name}"] = a
        args[name] = nc.dram_tensor(f"in_{name}", a.shape, mybir.dt.from_np(a.dtype), kind="ExternalInput").ap()
    outs = [nc.dram_tensor(f"out_{i}", shape, F32, kind="ExternalOutput").ap() for i, (shape, _) in enumerate(_OUTS)]
    build(nc, args, outs[0].rearrange("b s d -> (b s) d"))
    r = _run(nc, [arrays], core_ids=[0])
    return r.results[0]["out_0"]
```

```python
import math
from contextlib import ExitStack

import concourse.bass as bass
from concourse import mybir

F32 = mybir.dt.float32
BF16 = mybir.dt.bfloat16
I32 = mybir.dt.int32
U32 = mybir.dt.uint32
ALU = mybir.AluOpType
ACT = mybir.ActivationFunctionType
AX = mybir.AxisListType

P = 128
T = 4096
D = 256
KD = D // P
BATCH = 2
BT = 512
NB = T // BT
SB = NB // BATCH
TPB = BT // P
NT = T // P
ROUND = 12582912.0
RSQRT_SEED = float(0x5F3759DF)


class Chain:

    def __init__(self, engine, sem, base=0):
        self.engine, self.sem, self.base, self.n = engine, sem, base, 0

    def mark(self, ins):
        self.n += 1
        ins.then_inc(self.sem, 1)
        return self.n

    def wait(self, n):
        self.engine.wait_ge(self.sem, self.base + n)

    def link(self, ins):
        self.wait(self.mark(ins))


def rsqrt(nc, chain, out, v, tmp):
    V = nc.vector
    chain.link(V.tensor_scalar(tmp.bitcast(I32), v.bitcast(I32), 1, None, ALU.logical_shift_right))
    chain.link(V.tensor_scalar(out.bitcast(I32), tmp.bitcast(I32), -1.0, RSQRT_SEED, ALU.mult, ALU.add))
    for _ in range(3):
        chain.link(V.tensor_tensor(tmp, out, out, ALU.mult))
        chain.link(V.tensor_tensor(tmp, tmp, v, ALU.mult))
        chain.link(V.tensor_scalar(tmp, tmp, -0.5, 1.5, ALU.mult, ALU.add))
        chain.link(V.tensor_tensor(out, out, tmp, ALU.mult))


def norm_stats(nc, chain, src, stats, mv, rstd, tmp, eps, var=None):
    V = nc.vector
    n = stats.shape[1]
    for j in range(n):
        last = chain.mark(V.bn_stats(stats[:, j, :], src(j)))
    chain.wait(last)
    V.memset(tmp, 0.0)
    for j in range(n):
        last = chain.mark(V.bn_aggr(mv[:, j, :], stats[:, j, :]))
    chain.wait(last)
    if var is not None:
        chain.mark(V.tensor_copy(var, mv[:, :, 1]))
    chain.link(V.tensor_scalar(mv[:, :, 1], mv[:, :, 1], 1.0, eps, ALU.mult, ALU.add))
    rsqrt(nc, chain, rstd, mv[:, :, 1], tmp)


NORM_STEPS = 2 * TPB + 1 + 2 + 3 * 4


class Memory:

    def __init__(self, nc, stack, tag):
        self.nc, self.stack, self.tag, self.sems = nc, stack, tag, []

    def sb(self, name, shape, dt=F32):
        return self.stack.enter_context(self.nc.sbuf_tensor(f"{self.tag}_{name}", shape, dt))

    def ps(self, name, shape, dt=F32):
        return self.stack.enter_context(self.nc.psum_tensor(f"{self.tag}_{name}", shape, dt))

    def sem(self, name):
        self.sems.append(self.stack.enter_context(self.nc.semaphore(f"{self.tag}_{name}")))
        return self.sems[-1]

    def clear(self):
        with self.nc.Block() as block:

            @block.gpsimd
            def _(pool):
                for sem in self.sems:
                    pool.sem_clear(sem)


def gate_loop(nc, x_in, w_proj, XN, YS, SG, SUMS, ident, to_zero):
    TURN = 2.0 * math.pi * (1.0 - 2.0 ** -23)
    AR, AI_, K_, V_, Q_, G_ = range(6)
    SEQ = [(AR, 0), (AI_, 0), (AR, 1), (AI_, 1), (K_, 0), (V_, 0), (K_, 1), (V_, 1), (Q_, 0), (G_, 0), (Q_, 1), (G_, 1)]
    RING = 6
    slot = {fc: n for n, fc in enumerate(SEQ)}
    with ExitStack() as stack:
        m_ = Memory(nc, stack, "gl")
        W = m_.sb("w", [P, KD, 6 * D])
        XB = m_.sb("xb", [P, TPB, D])
        XNB = m_.sb("xnb", [P, TPB, D])
        XT = m_.sb("xt", [P, KD, BT])
        stats, mv = m_.sb("stats", [P, TPB, 6]), m_.sb("mv", [P, TPB, 2])
        rstd, tmp = m_.sb("rstd", [P, TPB]), m_.sb("tmp", [P, TPB])
        SQR, SQI, AIM, ABR, KS, QS, KV, NEG, SGN, MAG, A, PHI, WR, SN, CS, UR, UI, T1, T2, T3, T4 = (
            m_.sb(n, [P, KD, BT]) for n in ("sqr", "sqi", "aim", "abr", "ks", "qs", "kv", "neg", "sgn", "mag",
                                            "a", "phi", "wr", "sn", "cs", "ur", "ui", "t1", "t2", "t3", "t4"))
        TAN, YI = SQI, MAG
        zeros = m_.sb("zeros", [P, D])
        quarter = m_.sb("quarter", [P, 1])
        keep = m_.sb("keep", [P, NB + 1])
        c_phase, c_u = m_.sb("c_phase", [P, KD]), m_.sb("c_u", [P, KD, 2])
        pT = m_.ps("pT", [P, KD, BT])
        bank = [m_.ps(f"bank{i}", [P, BT]) for i in range(RING)]
        s = {n: m_.sem(n) for n in (
            "x_loaded", "w_loaded", "consts", "zeroed", "xn_done", "xt_raw", "xt_done", "sq_done", "m2_done", "mag_done",
            "t_done", "atan_done", "turn_done", "abs_done", "trig_done", "u_done", "hi_done", "pool_steps", "y_done", "steps")}
        bank_free = [m_.sem(f"bank_free{i}") for i in range(RING)]
        proj = [m_.sem(f"proj{i}") for i in range(6)]

        def freed(i, fc):
            return bank_free[slot[fc] % RING], i * 2 + (slot[fc] // RING + 2)

        with nc.Block() as block:

            @block.sync
            def _(sp):
                x_blocks = x_in.rearrange("(b t p) d -> b p t d", p=P, t=TPB)
                sp.dma_start(XB[:], x_blocks[0]).then_inc(s["x_loaded"], 16)
                sp.dma_start(W[:], w_proj.rearrange("(k p) n -> p k n", p=P)).then_inc(s["w_loaded"], 16)

                def fill(i):
                    for array in to_zero:
                        part = array.rearrange("(b t p) d -> b p t d", b=NB, p=P)
                        n = part.shape[2]
                        part = part[i] if isinstance(i, int) else part[bass.ds(i, 1)].rearrange("b p t d -> (b p) t d")
                        sp.dma_start(part, zeros[:].unsqueeze(1).to_broadcast([P, n, D])).then_inc(s["zeroed"], 16)
                sp.wait_ge(s["consts"], 3)
                fill(0)
                with sp.Fori(1, NB) as i:
                    sp.wait_ge(s["xn_done"], i * TPB)
                    sp.dma_start(XB[:], x_blocks[bass.ds(i, 1)].rearrange("b p t d -> (b p) t d"))\
                        .then_inc(s["x_loaded"], 16)
                    fill(i)
                sp.wait_ge(s["zeroed"], 16 * NB * len(to_zero))

            @block.gpsimd
            def _(pool):
                pool.memset(ident[:], 0.0).then_inc(s["consts"], 1)
                pool.wait_ge(s["consts"], 1)
                pool.affine_select(out=ident[:], in_=ident[:], compare_op=ALU.not_equal, fill=1.0, base=0,
                                   pattern=[[-1, P]], channel_multiplier=1).then_inc(s["consts"], 1)
                pool.memset(zeros[:], 0.0)
                pool.memset(quarter[:], math.pi / 2).then_inc(s["consts"], 1)
                with pool.Fori(0, NB) as i:
                    for c in range(KD):
                        n = i * KD + (c + 1)
                        pool.wait_ge(s["trig_done"], n)
                        pool.wait_ge(s["u_done"], n)
                        pool.tensor_tensor(T3[:, c], SN[:, c], UR[:, c], ALU.mult).then_inc(s["pool_steps"], 1)
                        pool.tensor_tensor(T4[:, c], CS[:, c], UI[:, c], ALU.mult).then_inc(s["pool_steps"], 1)
                        pool.wait_ge(s["pool_steps"], i * (2 * KD) + (2 * c + 2))
                        pool.tensor_tensor(T3[:, c], T3[:, c], T4[:, c], ALU.subtract).then_inc(s["hi_done"], 1)

            @block.tensor
            def _(pe):
                pe.wait_ge(s["consts"], 2)
                pe.wait_ge(s["w_loaded"], 16)
                for b in bank_free:
                    pe.sem_inc(b, 1)
                with pe.Fori(0, NB) as i:
                    pe.wait_ge(s["xn_done"], i * TPB + TPB)
                    for j in range(TPB):
                        for c in range(KD):
                            mm = pe.transpose(pT[:, c, j * P:(j + 1) * P], XNB[:, j, c * P:(c + 1) * P], ident[:])
                    mm.then_inc(s["xt_raw"], 1)
                    pe.wait_ge(s["xt_done"], i * KD + KD)
                    for n, (f, c) in enumerate(SEQ):
                        pe.wait_ge(bank_free[n % RING], i * 2 + (n // RING + 1))
                        for k in range(KD):
                            mm = pe.matmul(bank[n % RING][:], W[:, k, f * D + c * P:f * D + (c + 1) * P], XT[:, k],
                                           start=(k == 0), stop=(k == KD - 1))
                        mm.then_inc(proj[f], 1)

            @block.scalar
            def _(act):
                act.wait_ge(s["consts"], 3)
                A_ = nc.scalar.activation
                with act.Fori(0, NB) as i:
                    bank_of = lambda f, c: bank[slot[f, c] % RING][:]
                    free_of = lambda f, c: bank_free[slot[f, c] % RING]
                    act.wait_ge(s["xt_raw"], i + 1)
                    for c in range(KD):
                        A_(XT[:, c], pT[:, c], ACT.Copy).then_inc(s["xt_done"], 1)
                    A_(XN[:, bass.ds(i * TPB, TPB), :], XNB[:], ACT.Copy)
                    for c in range(KD):
                        act.wait_ge(proj[AR], i * KD + (c + 1))
                        A_(SQR[:, c], bank_of(AR, c), ACT.Square)
                        A_(ABR[:, c], bank_of(AR, c), ACT.Abs)
                        act.wait_ge(proj[AI_], i * KD + (c + 1))
                        A_(SQI[:, c], bank_of(AI_, c), ACT.Square).then_inc(s["sq_done"], 1)
                        A_(AIM[:, c], bank_of(AI_, c), ACT.Copy).then_inc(free_of(AI_, c), 1)
                    for c in range(KD):
                        act.wait_ge(proj[K_], i * KD + (c + 1))
                        A_(KS[:, c], bank_of(K_, c), ACT.Copy).then_inc(free_of(K_, c), 1)
                    for c in range(KD):
                        act.wait_ge(s["m2_done"], i * KD + (c + 1))
                        A_(MAG[:, c], SQR[:, c], ACT.Sqrt).then_inc(s["mag_done"], 1)
                    for c in range(KD):
                        act.wait_ge(s["mag_done"], i * KD + (c + 1))
                        A_(A[:, c], MAG[:, c], ACT.Sigmoid)
                    for c in range(KD):
                        act.wait_ge(s["t_done"], i * KD + (c + 1))
                        A_(PHI[:, c], TAN[:, c], ACT.Arctan).then_inc(s["atan_done"], 1)
                    for c in range(KD):
                        act.wait_ge(proj[Q_], i * KD + (c + 1))
                        A_(QS[:, c], bank_of(Q_, c), ACT.Copy).then_inc(free_of(Q_, c), 1)
                        act.wait_ge(proj[G_], i * KD + (c + 1))
                        A_(SG[:, c, bass.ds(i * BT, BT)], bank_of(G_, c), ACT.Silu).then_inc(free_of(G_, c), 1)
                    for c in range(KD):
                        act.wait_ge(s["turn_done"], i * KD + (c + 1))
                        A_(ABR[:, c], WR[:, c], ACT.Abs).then_inc(s["abs_done"], 1)
                        A_(SN[:, c], WR[:, c], ACT.Sin, scale=TURN)
                        act.wait_ge(s["abs_done"], i * KD + (c + 1))
                        A_(CS[:, c], ABR[:, c], ACT.Sin, scale=-TURN, bias=quarter[:]).then_inc(s["trig_done"], 1)

            @block.vector
            def _(dve):
                V = nc.vector
                pre = Chain(dve, s["steps"])
                pre.mark(V.memset(c_phase[:], 0.0))
                pre.mark(V.memset(c_u[:], 0.0))
                pre.link(V.memset(keep[:], 1.0))
                pre.link(V.memset(keep[:, SB:SB + 1], 0.0))
                dve.wait_ge(s["consts"], 3)
                PER = NORM_STEPS + 19 * KD
                with dve.Fori(0, NB) as i:
                    ch = Chain(dve, s["steps"], i * PER + pre.n)
                    def after(name, c):
                        dve.wait_ge(s[name], i * KD + (c + 1))
                    dve.wait_ge(s["x_loaded"], i * 16 + 16)
                    norm_stats(nc, ch, lambda j: XB[:, j], stats, mv, rstd[:], tmp[:], 1e-5)
                    for j in range(TPB):
                        V.tensor_scalar(XNB[:, j], XB[:, j],
                                        mv[:, j, 0:1], rstd[:, j:j + 1], ALU.subtract, ALU.mult).then_inc(s["xn_done"], 1)
                    for c in range(KD):
                        after("sq_done", c)
                        V.tensor_tensor(SQR[:, c], SQR[:, c], SQI[:, c], ALU.add).then_inc(s["m2_done"], 1)
                        V.tensor_scalar(NEG[:, c], bank[slot[AR, c] % RING][:], 0.0, 0.5, ALU.is_lt, ALU.mult)\
                            .then_inc(bank_free[slot[AR, c] % RING], 1)
                    for c in range(KD):
                        dve.wait_ge(*freed(i, (AR, c)))
                        ch.mark(V.tensor_scalar(SGN[:, c], NEG[:, c], -4.0 / math.pi, 1.0 / math.pi, ALU.mult, ALU.add))
                        dve.wait_ge(proj[V_], i * KD + (c + 1))
                        dve.wait_ge(*freed(i, (K_, c)))
                        V.tensor_tensor(KV[:, c], KS[:, c], bank[slot[V_, c] % RING][:], ALU.mult)\
                            .then_inc(bank_free[slot[V_, c] % RING], 1)
                    for c in range(KD):
                        after("mag_done", c)
                        ch.link(V.scalar_tensor_tensor(T1[:, c], ABR[:, c], 1e-30, MAG[:, c], ALU.add, ALU.add))
                        ch.link(V.reciprocal(T2[:, c], T1[:, c]))
                        V.tensor_tensor(TAN[:, c], AIM[:, c], T2[:, c], ALU.mult).then_inc(s["t_done"], 1)
                    for c in range(KD):
                        after("atan_done", c)
                        ch.link(V.tensor_tensor(T1[:, c], PHI[:, c], SGN[:, c], ALU.mult))
                        ch.link(V.tensor_tensor_scan(PHI[:, c], T1[:, c], NEG[:, c], c_phase[:, c:c + 1], ALU.add, ALU.add))
                        ch.link(V.tensor_scalar(T2[:, c], PHI[:, c], ROUND, ROUND, ALU.add, ALU.subtract))
                        V.tensor_tensor(WR[:, c], PHI[:, c], T2[:, c], ALU.subtract).then_inc(s["turn_done"], 1)
                        after("turn_done", c)
                        ch.mark(V.tensor_copy(c_phase[:, c:c + 1], WR[:, c, BT - 1:BT]))
                    for c in range(KD):
                        after("trig_done", c)
                        ch.mark(V.tensor_tensor(T1[:, c], KV[:, c], CS[:, c], ALU.mult))
                        ch.link(V.tensor_tensor(T2[:, c], KV[:, c], SN[:, c], ALU.mult))
                        ch.link(V.tensor_tensor_scan(UR[:, c], A[:, c], T1[:, c], c_u[:, c, 0:1], ALU.mult, ALU.add))
                        V.tensor_tensor_scan(UI[:, c], A[:, c], T2[:, c], c_u[:, c, 1:2], ALU.mult, ALU.add)\
                            .then_inc(s["u_done"], 1)
                        after("u_done", c)
                        ch.mark(V.tensor_scalar(c_u[:, c, 0:1], UR[:, c, BT - 1:BT], keep[:, bass.ds(i + 1, 1)], None, ALU.mult))
                        ch.mark(V.tensor_scalar(c_u[:, c, 1:2], UI[:, c, BT - 1:BT], keep[:, bass.ds(i + 1, 1)], None, ALU.mult))
                        ch.mark(V.tensor_tensor(T1[:, c], CS[:, c], UR[:, c], ALU.mult))
                        ch.link(V.tensor_tensor(T2[:, c], SN[:, c], UI[:, c], ALU.mult))
                        ch.link(V.tensor_tensor(T1[:, c], T1[:, c], T2[:, c], ALU.add))
                    for c in range(KD):
                        ys = YS[:, c, bass.ds(i * BT, BT)]
                        at = lambda n: SUMS[:, bass.ds((i * KD + c) * 4 + n, 1)]
                        ch.link(V.scalar_tensor_tensor(ys, T1[:, c], 1.0, QS[:, c], ALU.mult, ALU.mult, accum_out=at(0)))
                        ch.mark(V.scalar_tensor_tensor(T2[:, c], ys, 1.0, ys, ALU.mult, ALU.mult, accum_out=at(2)))
                        after("hi_done", c)
                        ch.link(V.scalar_tensor_tensor(YI[:, c], T3[:, c], 1.0, QS[:, c], ALU.mult, ALU.mult, accum_out=at(1)))
                        ch.link(V.scalar_tensor_tensor(T2[:, c], YI[:, c], 1.0, YI[:, c], ALU.mult, ALU.mult, accum_out=at(3)))
                assert ch.n == PER, ch.n
        m_.clear()


def gate_ffn(nc, g, X, YS, SG, SUMS, ident):
    F = 4 * D
    FC = F // P
    with ExitStack() as stack:
        m_ = Memory(nc, stack, "gf")
        WO, W1, W2 = m_.sb("wo", [P, KD, D]), m_.sb("w1", [P, KD, F]), m_.sb("w2", [P, FC, D])
        gns, gnb, b1 = m_.sb("gns", [P, KD]), m_.sb("gnb", [P, KD]), m_.sb("b1", [P, FC])
        rows = {n: m_.sb(n, [P, D]) for n in ("ln1s", "ln1b", "b2", "ln2s", "ln2b")}
        group = m_.sb("group", [P, P])
        ST, MEAN = m_.sb("st", [P, BATCH, KD, 4]), m_.sb("mean", [P, BATCH, KD, 4])
        VAR, SQ, RS, TMP = (m_.sb(n, [P, BATCH, KD]) for n in ("var", "sq", "rs", "tmp"))
        AB = m_.sb("ab", [P, NB, KD, 2])
        Z = m_.sb("z", [P, KD, BT])
        XB = m_.sb("xb", [P, TPB, D])
        R, R2, X1N, X1, O2N = (m_.sb(n, [P, TPB, D]) for n in ("r", "r2", "x1n", "x1", "o2n"))
        XT, H = m_.sb("xt", [P, KD, BT]), m_.sb("h", [P, FC, BT])
        stats, mv = m_.sb("stats", [P, TPB, 6]), m_.sb("mv", [P, TPB, 2])
        rstd, tmp = m_.sb("rstd", [P, TPB]), m_.sb("tmp2", [P, TPB])
        pO, pW, pT = (m_.ps(n, [P, TPB, D]) for n in ("pO", "pW", "pT"))
        pH = [m_.ps(f"pH{n}", [P, BT]) for n in range(2)]
        pTf = pT[:].rearrange("p (c a) d -> p c (a d)", c=KD)
        s = {n: m_.sem(n) for n in ("loaded", "group_done", "st_done", "mean_done", "steps", "z_steps", "z_done", "wo_done",
                                    "residual_done", "x_loaded", "x1n_done", "x1_done", "xt_raw", "xt_done", "h_ready", "h_free", "w2_done",
                                    "r2_done", "o2n_done", "out_done", "pool_steps", "act_steps")}
        row = lambda n: rows[n][:].unsqueeze(1).to_broadcast([P, TPB, D])
        blk = lambda buf, i: buf[:, bass.ds(i * TPB, TPB), :]

        with nc.Block() as block:

            @block.sync
            def _(sp):
                sp.dma_start(W1[:], g["W1"].rearrange("(k p) n -> p k n", p=P)).then_inc(s["loaded"], 16)
                sp.dma_start(W2[:], g["W2"].rearrange("(k p) n -> p k n", p=P)).then_inc(s["loaded"], 16)
                sp.dma_start(WO[:], g["Wo"].rearrange("(k p) n -> p k n", p=P)).then_inc(s["loaded"], 16)
                for dst, name in ((gns, "gn_scale"), (gnb, "gn_bias"), (b1, "b1")):
                    sp.dma_start(dst[:], g[name].rearrange("(k p) -> p k", p=P), allow_slow_non_contiguous=True)\
                        .then_inc(s["loaded"], 16)
                for name in rows:
                    sp.dma_start(rows[name][:], g[name].partition_broadcast(P)).then_inc(s["loaded"], 16)
                x_blocks = g["x"].rearrange("(b t p) d -> b p t d", p=P, t=TPB)
                sp.dma_start(XB[:], x_blocks[0]).then_inc(s["x_loaded"], 16)
                with sp.Fori(1, NB) as i:
                    sp.wait_ge(s["out_done"], i + 1)
                    sp.dma_start(XB[:], x_blocks[bass.ds(i, 1)].rearrange("b p t d -> (b p) t d"))\
                        .then_inc(s["x_loaded"], 16)
            LOADED = 16 * 11

            @block.gpsimd
            def _(pool):
                gm = group[:].rearrange("p (a b) -> p a b", b=8)
                pool.memset(group[:], 1.0 / (8 * (T // BATCH))).then_inc(s["pool_steps"], 1)
                pool.wait_ge(s["pool_steps"], 1)
                pool.affine_select(out=gm, in_=gm, compare_op=ALU.is_ge, fill=0.0, base=0,
                                   pattern=[[-8, P // 8], [0, 8]], channel_multiplier=1).then_inc(s["pool_steps"], 1)
                pool.wait_ge(s["pool_steps"], 2)
                pool.affine_select(out=gm, in_=gm, compare_op=ALU.is_ge, fill=0.0, base=7,
                                   pattern=[[8, P // 8], [0, 8]], channel_multiplier=-1).then_inc(s["group_done"], 1)
                pool.wait_ge(s["loaded"], LOADED)
                pool.sem_inc(s["out_done"], 1)

                def x1(i, base, first=False):
                    if not first:
                        pool.wait_ge(s["xt_raw"], i)
                    pool.wait_ge(s["x1n_done"], i * TPB + TPB)
                    ch = Chain(pool, s["pool_steps"], base)
                    ch.link(pool.tensor_tensor(X1[:], X1N[:], row("ln1s"), ALU.mult))
                    pool.tensor_tensor(X1[:], X1[:], row("ln1b"), ALU.add).then_inc(s["x1_done"], 1)
                    pool.wait_ge(s["x1_done"], i + 1)
                    pool.tensor_tensor(blk(X, i), X1[:], row("b2"), ALU.add).then_inc(s["residual_done"], 1)
                    pool.wait_ge(s["residual_done"], i + 1)

                def out(i, base):
                    pool.wait_ge(s["o2n_done"], i * TPB + 2 * TPB)
                    ch = Chain(pool, s["pool_steps"], base)
                    ch.link(pool.tensor_tensor(O2N[:], O2N[:], row("ln2s"), ALU.mult))
                    ch.link(pool.tensor_tensor(O2N[:], O2N[:], row("ln2b"), ALU.add))
                    pool.wait_ge(s["x_loaded"], i * 16 + 16)
                    pool.tensor_tensor(blk(X, i), XB[:], O2N[:], ALU.add).then_inc(s["out_done"], 1)

                x1(0, 2, first=True)
                with pool.Fori(1, NB) as i:
                    x1(i, i * 3)
                    out(i - 1, i * 3 + 1)
                out(NB - 1, NB * 3)

            @block.tensor
            def _(pe):
                pe.wait_ge(s["loaded"], LOADED)
                pe.wait_ge(s["group_done"], 1)
                pe.wait_ge(s["st_done"], BATCH)
                pe.matmul(pO[:].rearrange("p t d -> p (t d)")[:, 0:16], group[:], ST[:].rearrange("p b c f -> p (b c f)"),
                          start=True, stop=True).then_inc(s["mean_done"], 1)
                pe.sem_inc(s["h_free"], 2)
                pe.sem_inc(s["o2n_done"], TPB)

                def wo(i):
                    pe.wait_ge(s["z_done"], i * KD + KD)
                    for j in range(TPB):
                        for k in range(KD):
                            mm = pe.matmul(pO[:, j], Z[:, k, j * P:(j + 1) * P], WO[:, k], start=(k == 0), stop=(k == KD - 1))
                        mm.then_inc(s["wo_done"], 1)

                def turn(i):
                    pe.wait_ge(s["x1_done"], i + 1)
                    for c in range(KD):
                        for j in range(TPB):
                            mm = pe.transpose(pTf[:, c, j * P:(j + 1) * P], X1[:, j, c * P:(c + 1) * P], ident[:])
                    mm.then_inc(s["xt_raw"], 1)

                def ffn(i):
                    pe.wait_ge(s["xt_done"], i * KD + KD)
                    for f in range(FC):
                        pe.wait_ge(s["h_free"], i * FC + (f + 1))
                        for k in range(KD):
                            mm = pe.matmul(pH[f % 2][:], W1[:, k, f * P:(f + 1) * P], XT[:, k], start=(k == 0), stop=(k == KD - 1))
                        mm.then_inc(s["h_ready"], 1)
                    pe.wait_ge(s["h_free"], i * FC + (FC + 2))
                    pe.wait_ge(s["o2n_done"], i * TPB + TPB)
                    for j in range(TPB):
                        for f in range(FC):
                            mm = pe.matmul(pW[:, j], H[:, f, j * P:(j + 1) * P], W2[:, f], start=(f == 0), stop=(f == FC - 1))
                        mm.then_inc(s["w2_done"], 1)

                wo(0)
                turn(0)
                with pe.Fori(1, NB) as i:
                    wo(i)
                    ffn(i - 1)
                    turn(i)
                ffn(NB - 1)

            @block.scalar
            def _(act):
                act.wait_ge(s["loaded"], LOADED)

                def copy_xt(i):
                    act.wait_ge(s["xt_raw"], i + 1)
                    for c in range(KD):
                        nc.scalar.activation(XT[:, c], pTf[:, c], ACT.Copy).then_inc(s["xt_done"], 1)

                def gelu(i):
                    for f in range(FC):
                        act.wait_ge(s["h_ready"], i * FC + (f + 1))
                        nc.scalar.activation(H[:, f], pH[f % 2][:], ACT.Gelu_apprx_tanh, bias=b1[:, f:f + 1])\
                            .then_inc(s["h_free"], 1)

                copy_xt(0)
                with act.Fori(1, NB) as i:
                    gelu(i - 1)
                    copy_xt(i)
                gelu(NB - 1)

            @block.vector
            def _(dve):
                V = nc.vector
                pre = Chain(dve, s["steps"])
                for b in range(BATCH):
                    V.tensor_reduce(ST[:, b], SUMS[:].rearrange("p (b s c f) -> p b c f s", b=BATCH, s=SB, c=KD)[:, b], AX.X, ALU.add)\
                        .then_inc(s["st_done"], 1)
                dve.wait_ge(s["loaded"], LOADED)
                dve.wait_ge(s["mean_done"], 1)
                pre.link(V.tensor_copy(MEAN[:].rearrange("p b c f -> p (b c f)"), pO[:].rearrange("p t d -> p (t d)")[:, 0:16]))
                f_ = lambda n: MEAN[:, :, :, n]
                pre.link(V.tensor_tensor(VAR[:], f_(2), f_(3), ALU.add))
                pre.link(V.tensor_tensor(SQ[:], f_(0), f_(0), ALU.mult))
                pre.link(V.tensor_tensor(VAR[:], VAR[:], SQ[:], ALU.subtract))
                pre.link(V.tensor_tensor(SQ[:], f_(1), f_(1), ALU.mult))
                pre.link(V.tensor_tensor(VAR[:], VAR[:], SQ[:], ALU.subtract))
                pre.link(V.tensor_scalar(VAR[:], VAR[:], 1.0, 1e-6, ALU.mult, ALU.add))
                rsqrt(nc, pre, RS[:], VAR[:], TMP[:])
                gs = gns[:].unsqueeze(1).to_broadcast([P, BATCH, KD])
                gb = gnb[:].unsqueeze(1).to_broadcast([P, BATCH, KD])
                pre.link(V.tensor_tensor(RS[:], RS[:], gs, ALU.mult))
                pre.link(V.tensor_tensor(SQ[:], f_(0), RS[:], ALU.mult))
                pre.link(V.tensor_tensor(SQ[:], gb, SQ[:], ALU.subtract))
                for n, src in ((0, RS), (1, SQ)):
                    pre.link(V.tensor_copy(AB[:, :, :, n].rearrange("p (b s) c -> p b s c", b=BATCH),
                                           src[:].unsqueeze(2).to_broadcast([P, BATCH, SB, KD])))

                def z(i):
                    scale = lambda c, n: AB[:, bass.ds(i, 1), c, n] if not isinstance(i, int) else AB[:, i:i + 1, c, n]
                    for c in range(KD):
                        pre_z = V.tensor_scalar(Z[:, c], YS[:, c, bass.ds(i * BT, BT)], scale(c, 0), scale(c, 1), ALU.mult, ALU.add)
                        pre_z.then_inc(s["z_steps"], 1)
                        dve.wait_ge(s["z_steps"], i * KD + (c + 1))
                        V.tensor_tensor(Z[:, c], Z[:, c], SG[:, c, bass.ds(i * BT, BT)], ALU.mult).then_inc(s["z_done"], 1)

                def norm(i, base, psum, psum_done, residual, buf, out, out_done):
                    ch = Chain(dve, s["steps"], base)
                    for j in range(TPB):
                        if j % 2 == 0:
                            dve.wait_ge(s[psum_done], i * TPB + (j + 2))
                        last = ch.mark(V.tensor_tensor(buf[:, j], psum[:, j], residual(j), ALU.add))
                    ch.wait(last)
                    norm_stats(nc, ch, lambda j: buf[:, j], stats, mv, rstd[:], tmp[:], 1e-6)
                    for j in range(TPB):
                        V.tensor_scalar(out[:, j], buf[:, j], mv[:, j, 0:1], rstd[:, j:j + 1], ALU.subtract, ALU.mult)\
                            .then_inc(s[out_done], 1)

                PER = TPB + NORM_STEPS
                tile = lambda i: (lambda j: X[:, bass.ds(i * TPB + j, 1), :].rearrange("p o d -> p (o d)"))

                def first(i, base):
                    norm(i, base, pO, "wo_done", tile(i), R, X1N, "x1n_done")

                def second(i, base):
                    dve.wait_ge(s["out_done"], i + 1)
                    dve.wait_ge(s["residual_done"], i + 1)
                    norm(i, base, pW, "w2_done", tile(i), R2, O2N, "o2n_done")

                n0 = pre.n
                z(0)
                first(0, n0)
                z(1)
                with dve.Fori(1, NB - 1) as i:
                    dve.wait_ge(s["x1_done"], i)
                    first(i, (i * 2 - 1) * PER + n0)
                    z(i + 1)
                    second(i - 1, (i * 2) * PER + n0)
                dve.wait_ge(s["x1_done"], NB - 1)
                first(NB - 1, (2 * NB - 3) * PER + n0)
                second(NB - 2, (2 * NB - 2) * PER + n0)
                second(NB - 1, (2 * NB - 1) * PER + n0)
        m_.clear()


class Routing:

    def __init__(self, nc, stack, tag, experts, k):
        m_ = Memory(nc, stack, tag)
        self.E, self.K = experts, k
        self.tiles = (T * k + experts * (P - 1)) // P
        self.tiles += -self.tiles % 4
        self.slot = m_.sb("slot", [P, NT, k], I32)
        self.weight = m_.sb("weight", [P, NT, k])
        self.expert = m_.sb("expert", [1, P], I32)
        self.xs = nc.dram_tensor(f"{tag}_xs", (self.tiles * P, D), F32).ap()
        self.ys = nc.dram_tensor(f"{tag}_ys", (self.tiles * P, D), F32).ap()


def route(nc, tag, X, gate, r, ident, shared=None):
    E, K = r.E, r.K
    FS = 512 // P
    with ExitStack() as stack:
        m_ = Memory(nc, stack, tag)
        G = m_.sb("gate", [P, KD, E])
        iota_i, iota = m_.sb("iota_i", [P, E], I32), m_.sb("iota", [P, E])
        part_i, part = m_.sb("part_i", [P, 1], I32), m_.sb("part", [P, 1])
        tri, ones = m_.sb("tri", [P, P], BF16), m_.sb("ones", [P, P], BF16)
        onef = m_.sb("onef", [P, E])
        stats, mv = m_.sb("stats", [P, TPB, 6]), m_.sb("mv", [P, TPB, 2])
        rstd, tmp = m_.sb("rstd", [P, TPB]), m_.sb("tmp", [P, TPB])
        XN = m_.sb("xn", [P, TPB, D])
        XA, IDXA, RKA = m_.sb("xa", [P, NT, D]), m_.sb("idxa", [P, NT, K]), m_.sb("rka", [P, NT, K])
        XS = [m_.sb(f"xs{h}", [P, TPB, D]) for h in range(2)]
        SL = [m_.sb(f"sl{h}", [P, TPB, K], I32) for h in range(2)]
        BASE, pause = m_.sb("base", [P, TPB, K]), m_.sb("pause", [P, 1])
        XT = m_.sb("xt", [P, KD, BT])
        V8, I8 = m_.sb("v8", [P, TPB, 8]), m_.sb("i8", [P, TPB, 8], U32)
        IDX, RK = m_.sb("idx", [P, TPB, K]), m_.sb("rk", [P, TPB, K])
        DIF, EX, DEN, W0 = (m_.sb(n, [P, TPB]) for n in ("dif", "ex", "den", "w0"))
        OH0, OH, JUNK = m_.sb("oh0", [P, TPB, E], BF16), m_.sb("oh", [P, TPB, E], BF16), m_.sb("junk", [P, TPB * K, E])
        JUNKS = [JUNK[:, n] for n in range(TPB * K)]
        COUNT = m_.sb("count", [P, E])
        NTILE, END = m_.sb("ntile", [P, E]), m_.sb("end", [P, E])
        START, OWNER = m_.sb("start", [P, E]), m_.sb("owner", [P, 1])
        pT = m_.ps("pT", [P, KD, BT])
        pL, pR = m_.ps("pL", [P, BT]), m_.ps("pR", [P, BT])
        pLt = pL[:, 0:TPB * E].rearrange("p (t e) -> p t e", e=E)
        pRt = pR[:, 0:(TPB + 1) * E].rearrange("p (t e) -> p t e", e=E)
        names = ["loaded", "consts", "steps", "pool_steps", "xn_done", "xt_raw", "xt_done", "logits_done", "max_done",
                 "index_done", "dif_done", "exp_done", "onehot_done", "rank_done", "rows_ready", "passed",
                 "owner_done", "owner_turned", "expert_ready"]
        if shared:
            SW = [m_.sb(f"sw{n}", [P, KD, 512]) for n in range(2)]
            SD = m_.sb("sd", [P, FS, D])
            SIL, IN = m_.sb("sil", [P, BT]), m_.sb("in", [P, FS, BT])
            pG, pU, pS = m_.ps("pG", [P, BT]), m_.ps("pU", [P, BT]), m_.ps("pS", [P, TPB, D])
            names += ["gate_up", "silu_done", "inner_done", "shared_done", "shared_added"]
        s = {n: m_.sem(n) for n in names}
        sent = [m_.sem(f"sent{h}") for h in range(2)]
        SENT = 16 * TPB * K
        LOADED = 16 * (4 if shared else 1)

        with nc.Block() as block:

            @block.sync
            def _(sp):
                sp.dma_start(G[:], gate.rearrange("(k p) e -> p k e", p=P)).then_inc(s["loaded"], 16)
                if shared:
                    for dst, src in zip(SW, shared):
                        sp.dma_start(dst[:], src.rearrange("(k p) n -> p k n", p=P)).then_inc(s["loaded"], 16)
                    sp.dma_start(SD[:], shared[2].rearrange("(k p) n -> p k n", p=P)).then_inc(s["loaded"], 16)

            @block.gpsimd
            def _(pool):
                pool.memset(onef[:], 1.0)
                pool.memset(pause[:], 0.0)
                pool.memset(ones[:], 1.0)
                pool.memset(tri[:], 1.0).then_inc(s["pool_steps"], 1)
                pool.iota(iota_i[:], [[1, E]], base=0, channel_multiplier=0)
                pool.iota(part_i[:], [[0, 1]], base=0, channel_multiplier=1).then_inc(s["pool_steps"], 1)
                pool.wait_ge(s["pool_steps"], 2)
                pool.affine_select(out=tri[:], in_=tri[:], compare_op=ALU.is_gt, fill=0.0, base=0,
                                   pattern=[[1, P]], channel_multiplier=-1)
                pool.tensor_copy(iota[:], iota_i[:])
                pool.tensor_copy(part[:], part_i[:]).then_inc(s["consts"], 1)
                with pool.Fori(0, NB // 2) as i:
                    for h in range(2):
                        pool.wait_ge(s["rows_ready"], i * 2 + (h + 1))
                        pool.tensor_tensor(pause[:], onef[:, 0:1], onef[:, 0:1], ALU.add).then_inc(s["passed"], 1)
                        pool.wait_ge(s["passed"], 1)
                        pool.sem_clear(s["passed"])
                        for j in range(TPB):
                            for k in range(K):
                                pool.indirect_dma_start(r.xs, bass.IndirectOffsetOnAxis(ap=SL[h][:, j, k:k + 1], axis=0),
                                                        XS[h][:, j], None).then_inc(sent[h], 16)
                for h in range(2):
                    pool.wait_ge(sent[h], SENT * (NB // 2))

            @block.tensor
            def _(pe):
                pe.wait_ge(s["consts"], 1)
                pe.wait_ge(s["loaded"], LOADED)
                with pe.Fori(0, NB) as i:
                    n = lambda c: i * c
                    pe.wait_ge(s["xn_done"], n(TPB) + TPB)
                    for c in range(KD):
                        for j in range(TPB):
                            mm = pe.transpose(pT[:, c, j * P:(j + 1) * P], XN[:, j, c * P:(c + 1) * P], ident[:])
                    mm.then_inc(s["xt_raw"], 1)
                    pe.wait_ge(s["xt_done"], n(KD) + KD)
                    for j in range(TPB):
                        for k in range(KD):
                            mm = pe.matmul(pLt[:, j], XT[:, k, j * P:(j + 1) * P], G[:, k], start=(k == 0), stop=(k == KD - 1))
                    mm.then_inc(s["logits_done"], 1)
                    if shared:
                        for f in range(FS):
                            if f > 0:
                                pe.wait_ge(s["inner_done"], n(FS) + f)
                            for w, out in zip(SW, (pG, pU)):
                                for k in range(KD):
                                    mm = pe.matmul(out[:], w[:, k, f * P:(f + 1) * P], XT[:, k], start=(k == 0), stop=(k == KD - 1))
                            mm.then_inc(s["gate_up"], 1)
                    pe.wait_ge(s["onehot_done"], n(TPB) + TPB)
                    for j in range(TPB + 1):
                        pe.matmul(pRt[:, j], ident[:], COUNT[:], start=True, stop=False)
                        for q in range(j):
                            mm = pe.matmul(pRt[:, j], ones[:], OH[:, q], start=False, stop=(j == TPB and q == TPB - 1))
                        if j < TPB:
                            mm = pe.matmul(pRt[:, j], tri[:], OH[:, j], start=False, stop=True)
                    mm.then_inc(s["rank_done"], 1)
                    if shared:
                        pe.wait_ge(s["inner_done"], n(FS) + FS)
                        for j in range(TPB):
                            for f in range(FS):
                                mm = pe.matmul(pS[:, j], IN[:, f, j * P:(j + 1) * P], SD[:, f], start=(f == 0), stop=(f == FS - 1))
                        mm.then_inc(s["shared_done"], 1)
                pe.wait_ge(s["owner_done"], 1)
                pe.matmul(pL[0:1, 0:P], OWNER[:], ident[:], start=True, stop=True).then_inc(s["owner_turned"], 1)

            @block.scalar
            def _(act):
                with act.Fori(0, NB) as i:
                    n = lambda c: i * c
                    act.wait_ge(s["xt_raw"], n(1) + 1)
                    for c in range(KD):
                        nc.scalar.activation(XT[:, c], pT[:, c], ACT.Copy).then_inc(s["xt_done"], 1)
                    if K == 2:
                        nc.scalar.activation(XA[:, bass.ds(i * TPB, TPB), :], XN[:], ACT.Copy)
                    act.wait_ge(s["dif_done"], n(1) + 1)
                    nc.scalar.activation(EX[:], DIF[:], ACT.Exp).then_inc(s["exp_done"], 1)
                    if shared:
                        for f in range(FS):
                            act.wait_ge(s["gate_up"], n(FS) + (f + 1))
                            nc.scalar.activation(SIL[:], pG[:], ACT.Silu).then_inc(s["silu_done"], 1)

            @block.vector
            def _(dve):
                V = nc.vector
                pre = Chain(dve, s["steps"])
                dve.wait_ge(s["consts"], 1)
                pre.link(V.memset(COUNT[:], 0.0))
                n0 = pre.n
                PER = NORM_STEPS + 3 + 3 + (1 if K == 2 else TPB) + TPB * (K - 1) + TPB * K + 1
                with dve.Fori(0, NB) as i:
                    n = lambda c: i * c
                    ch = Chain(dve, s["steps"], n(PER) + n0)
                    tile = lambda j: X[:, bass.ds(i * TPB + j, 1), :].rearrange("p o d -> p (o d)")
                    norm_stats(nc, ch, tile, stats, mv, rstd[:], tmp[:], 1e-5)
                    for j in range(TPB):
                        V.tensor_scalar(XN[:, j], tile(j), mv[:, j, 0:1], rstd[:, j:j + 1], ALU.subtract, ALU.mult)\
                            .then_inc(s["xn_done"], 1)
                    dve.wait_ge(s["logits_done"], n(1) + 1)
                    V.memset(tmp[:], 0.0)
                    for j in range(TPB):
                        mx = V.max(V8[:, j], pLt[:, j])
                    mx.then_inc(s["max_done"], 1)
                    dve.wait_ge(s["max_done"], 1)
                    dve.sem_clear(s["max_done"])
                    for j in range(TPB):
                        mx = V.max_index(I8[:, j], V8[:, j], pLt[:, j])
                    mx.then_inc(s["index_done"], 1)
                    if K == 2:
                        V.tensor_tensor(DIF[:], V8[:, :, 1], V8[:, :, 0], ALU.subtract).then_inc(s["dif_done"], 1)
                    else:
                        V.tensor_scalar(DIF[:], V8[:, :, 0], -1.0, None, ALU.mult).then_inc(s["dif_done"], 1)
                    dve.wait_ge(s["index_done"], n(1) + 1)
                    ch.link(V.tensor_copy(IDX[:], I8[:, :, 0:K]))
                    for j in range(TPB):
                        out = OH[:, j] if K == 1 else OH0[:, j]
                        ins = V.tensor_scalar(out, iota[:], IDX[:, j, 0:1], None, ALU.is_equal)
                        if K == 1:
                            ins.then_inc(s["onehot_done"], 1)
                        else:
                            last = ch.mark(ins)
                    if K == 2:
                        ch.wait(last)
                        for j in range(TPB):
                            V.scalar_tensor_tensor(OH[:, j], iota[:], IDX[:, j, 1:2], OH0[:, j], ALU.is_equal, ALU.add)\
                                .then_inc(s["onehot_done"], 1)
                    dve.wait_ge(s["exp_done"], n(1) + 1)
                    ch.link(V.tensor_scalar(DEN[:], EX[:], 1.0, None, ALU.add))
                    ch.link(V.reciprocal(W0[:], DEN[:]))
                    ch.mark(V.tensor_scalar(r.weight[:, bass.ds(i * TPB, TPB), 0], W0[:], 1.0, None, ALU.mult))
                    if K == 2:
                        ch.mark(V.tensor_tensor(r.weight[:, bass.ds(i * TPB, TPB), 1], W0[:], EX[:], ALU.mult))
                    if K == 1:
                        for j in range(TPB):
                            ch.mark(V.tensor_scalar(XA[:, bass.ds(i * TPB + j, 1), :].rearrange("p o d -> p (o d)"),
                                                    XN[:, j], W0[:, j:j + 1], None, ALU.mult))
                    if shared:
                        for f in range(FS):
                            dve.wait_ge(s["silu_done"], n(FS) + (f + 1))
                            V.tensor_tensor(IN[:, f], SIL[:], pU[:], ALU.mult).then_inc(s["inner_done"], 1)
                    dve.wait_ge(s["rank_done"], n(1) + 1)
                    for j in range(TPB):
                        for k in range(K):
                            last = ch.mark(V.scalar_tensor_tensor(JUNKS[j * K + k], iota[:], IDX[:, j, k:k + 1], pRt[:, j],
                                                                  ALU.is_equal, ALU.mult, accum_out=RK[:, j, k:k + 1]))
                    ch.mark(V.tensor_copy(IDXA[:, bass.ds(i * TPB, TPB), :], IDX[:]))
                    last = ch.mark(V.tensor_copy(COUNT[:], pRt[:, TPB]))
                    ch.wait(last)
                    ch.mark(V.tensor_copy(RKA[:, bass.ds(i * TPB, TPB), :], RK[:]))
                    if shared:
                        dve.wait_ge(s["shared_done"], n(1) + 1)
                        xb = X[:, bass.ds(i * TPB, TPB), :]
                        V.tensor_tensor(xb, xb, pS[:], ALU.add).then_inc(s["shared_added"], 1)
                    assert ch.n == PER, (ch.n, PER)
                ch = Chain(dve, s["steps"], NB * PER + n0)
                ch.link(V.tensor_scalar(NTILE[:], COUNT[:], 1.0 / P, 0.5 - 0.5 / P, ALU.mult, ALU.add))
                ch.link(V.tensor_scalar(NTILE[:], NTILE[:], ROUND, ROUND, ALU.add, ALU.subtract))
                ch.link(V.tensor_tensor_scan(END[:], NTILE[:], NTILE[:], 0.0, ALU.add, ALU.bypass))
                ch.link(V.tensor_tensor(START[:], END[:], NTILE[:], ALU.subtract))
                ch.mark(V.tensor_scalar(START[:], START[:], float(P), None, ALU.mult))
                ch.link(V.scalar_tensor_tensor(JUNKS[0], END[:], part[:], onef[:], ALU.is_le, ALU.mult, accum_out=OWNER[:]))
                V.tensor_scalar(OWNER[:], OWNER[:], float(E - 1), None, ALU.min).then_inc(s["owner_done"], 1)
                n1 = ch.base + ch.n
                PER2 = TPB * K + 2
                def send(i, again):
                    for h in range(2):
                        ch = Chain(dve, s["steps"], (i * 2 + h) * PER2 + n1)
                        at = lambda buf: buf[:, bass.ds((i * 2 + h) * TPB, TPB), :]
                        if again:
                            dve.wait_ge(sent[h], i * SENT)
                        ch.mark(V.tensor_scalar(XS[h][:], at(XA), 1.0, None, ALU.mult))
                        for j in range(TPB):
                            for k in range(K):
                                expert = IDXA[:, bass.ds((i * 2 + h) * TPB + j, 1), k]
                                last = ch.mark(V.scalar_tensor_tensor(JUNKS[j * K + k], iota[:], expert, START[:],
                                                                      ALU.is_equal, ALU.mult, accum_out=BASE[:, j, k:k + 1]))
                        ch.wait(last)
                        ch.link(V.tensor_tensor(at(r.slot), BASE[:], at(RKA), ALU.add))
                        V.tensor_tensor(SL[h][:], BASE[:], at(RKA), ALU.add).then_inc(s["rows_ready"], 1)
                        dve.wait_ge(s["rows_ready"], i * 2 + (h + 1))

                send(0, False)
                with dve.Fori(1, NB // 2) as i:
                    send(i, True)
                dve.wait_ge(s["owner_turned"], 1)
                V.tensor_copy(r.expert[:], pL[0:1, 0:P]).then_inc(s["expert_ready"], 1)
        m_.clear()


def expert_tiles(nc, tag, r, w_gate, w_up, w_down, ident):
    BUF = 4
    FS = 512 // P
    N = r.tiles
    xs, ys = (a.rearrange("(t p) d -> t p d", p=P) for a in (r.xs, r.ys))
    assert N % BUF == 0
    with ExitStack() as stack:
        m_ = Memory(nc, stack, tag)
        ring = lambda name, shape, n=BUF: [m_.sb(f"{name}{b}", shape) for b in range(n)]
        WG, WU, WD = ring("wg", [P, KD, 512]), ring("wu", [P, KD, 512]), ring("wd", [P, FS, D])
        XR, Y = ring("xr", [P, D]), ring("y", [P, D])
        XT, SIL, IN = ring("xt", [P, KD, P], 2), ring("sil", [P, FS, P], 2), ring("in", [P, FS, P], 2)
        pT, pG, pU, pY = ([m_.ps(f"{n}{b}", [P, 512]) for b in range(2)] for n in ("pT", "pG", "pU", "pY"))
        s = {n: m_.sem(n) for n in ("xt_raw", "xt_done", "gate_done", "up_done", "silu_done", "inner_done", "down_done", "y_done")}
        x_loaded, w_loaded, stored = ([m_.sem(f"{n}{b}") for b in range(BUF)] for n in ("x_loaded", "w_loaded", "stored"))

        class Tile:

            def __init__(self, q, b):
                self.q, self.b, self.two = q, b, b % 2
                self.t = q * BUF + b

            def __add__(self, d):
                return Tile(self.q + (self.b + d) // BUF, (self.b + d) % BUF)

            def at_least(self, n):
                return not isinstance(self.q, int) or self.t >= n

        def steps(engine, body):
            for b in range(BUF):
                body(Tile(0, b), b == 0, False)
            with engine.Fori(1, N // BUF - 1) as q:
                for b in range(BUF):
                    body(Tile(q, b), False, False)
            for b in range(BUF):
                body(Tile(N // BUF - 1, b), False, b == BUF - 1)

        with nc.Block() as block:

            @block.sync
            def _(sp):
                def load(t, first, last):
                    if t.at_least(BUF):
                        sp.wait_ge(s["down_done"], t.t - (BUF - 1))
                    sp.dma_start(XR[t.b][:], xs[bass.ds(t.t, 1)].rearrange("t p d -> (t p) d")).then_inc(x_loaded[t.b], 16)
                    e = sp.value_load(r.expert[0:1, bass.ds(t.t, 1)], min_val=0, max_val=r.E - 1)
                    for dst, src in ((WG, w_gate), (WU, w_up), (WD, w_down)):
                        sp.dma_start(dst[t.b][:], src[bass.ds(e, 1)].rearrange("e (k p) n -> p (e k) n", p=P))\
                            .then_inc(w_loaded[t.b], 16)
                steps(sp, load)

            @block.tensor
            def _(pe):
                def turn(t):
                    pe.wait_ge(x_loaded[t.b], t.q * 16 + 16)
                    for k in range(KD):
                        mm = pe.transpose(pT[t.two][:, k * P:(k + 1) * P], XR[t.b][:, k * P:(k + 1) * P], ident[:])
                    mm.then_inc(s["xt_raw"], 1)

                def up(t):
                    pe.wait_ge(s["xt_done"], t.t + 1)
                    pe.wait_ge(w_loaded[t.b], t.q * 48 + 48)
                    for w, out, done in ((WG, pG, "gate_done"), (WU, pU, "up_done")):
                        for f in range(FS):
                            for k in range(KD):
                                mm = pe.matmul(out[t.two][:, f * P:(f + 1) * P], w[t.b][:, k, f * P:(f + 1) * P],
                                               XT[t.two][:, k], start=(k == 0), stop=(k == KD - 1))
                        mm.then_inc(s[done], 1)

                def down(t):
                    pe.wait_ge(s["inner_done"], t.t + 1)
                    if t.at_least(2):
                        pe.wait_ge(s["y_done"], t.t - 1)
                    for f in range(FS):
                        mm = pe.matmul(pY[t.two][:, 0:D], IN[t.two][:, f], WD[t.b][:, f], start=(f == 0), stop=(f == FS - 1))
                    mm.then_inc(s["down_done"], 1)

                def step(t, first, last):
                    if not last:
                        turn(t + 1)
                    up(t)
                    if not first:
                        down(t + -1)
                turn(Tile(0, 0))
                steps(pe, step)
                down(Tile(N // BUF - 1, BUF - 1))

            @block.scalar
            def _(act):
                def copy_xt(t):
                    act.wait_ge(s["xt_raw"], t.t + 1)
                    nc.scalar.activation(XT[t.two][:].rearrange("p k t -> p (k t)"), pT[t.two][:, 0:D], ACT.Copy)\
                        .then_inc(s["xt_done"], 1)

                def store(t):
                    act.wait_ge(s["y_done"], t.t + 1)
                    act.dma_start(ys[bass.ds(t.t, 1)].rearrange("t p d -> (t p) d"), Y[t.b][:]).then_inc(stored[t.b], 16)

                def step(t, first, last):
                    if not last:
                        copy_xt(t + 1)
                    act.wait_ge(s["gate_done"], t.t + 1)
                    if t.at_least(2):
                        act.wait_ge(s["inner_done"], t.t - 1)
                    nc.scalar.activation(SIL[t.two][:].rearrange("p f t -> p (f t)"), pG[t.two][:], ACT.Silu)\
                        .then_inc(s["silu_done"], 1)
                    if t.at_least(2):
                        store(t + -2)
                copy_xt(Tile(0, 0))
                steps(act, step)
                store(Tile(N // BUF - 1, BUF - 2))
                store(Tile(N // BUF - 1, BUF - 1))
                for b in range(BUF):
                    act.wait_ge(stored[b], 16 * (N // BUF))

            @block.vector
            def _(dve):
                def copy_y(t):
                    dve.wait_ge(s["down_done"], t.t + 1)
                    if t.at_least(BUF):
                        dve.wait_ge(stored[t.b], t.q * 16)
                    nc.vector.tensor_scalar(Y[t.b][:], pY[t.two][:, 0:D], 1.0, None, ALU.mult).then_inc(s["y_done"], 1)

                def step(t, first, last):
                    dve.wait_ge(s["silu_done"], t.t + 1)
                    dve.wait_ge(s["up_done"], t.t + 1)
                    if t.at_least(2):
                        dve.wait_ge(s["down_done"], t.t - 1)
                    nc.vector.tensor_tensor(IN[t.two][:].rearrange("p f t -> p (f t)"), SIL[t.two][:], pU[t.two][:], ALU.mult)\
                        .then_inc(s["inner_done"], 1)
                    if not first:
                        copy_y(t + -1)
                steps(dve, step)
                copy_y(Tile(N // BUF - 1, BUF - 1))
        m_.clear()


def combine(nc, tag, X, r, out=None):
    with ExitStack() as stack:
        m_ = Memory(nc, stack, tag)
        Y = [[m_.sb(f"y{h}{k}", [P, TPB, D]) for k in range(r.K)] for h in range(2)]
        SL = [m_.sb(f"sl{h}", [P, TPB * r.K], I32) for h in range(2)]
        copied = m_.sem("copied")
        fetched, added = ([m_.sem(f"{n}{h}") for h in range(2)] for n in ("fetched", "added"))
        stored = m_.sem("stored")
        ONE = 16 * TPB * r.K
        with nc.Block() as block:

            @block.gpsimd
            def _(pool):
                for h in range(2):
                    pool.sem_inc(added[h], TPB)
                with pool.Fori(0, NB // 2) as i:
                    for h in range(2):
                        pool.wait_ge(added[h], i * TPB + TPB)
                        pool.tensor_copy(SL[h][:], r.slot[:, bass.ds((i * 2 + h) * TPB, TPB), :].rearrange("p t k -> p (t k)"))\
                            .then_inc(copied, 1)
                        pool.wait_ge(copied, 1)
                        pool.sem_clear(copied)
                        for j in range(TPB):
                            for k in range(r.K):
                                n = j * r.K + k
                                pool.indirect_dma_start(Y[h][k][:, j], None, r.ys,
                                                        bass.IndirectOffsetOnAxis(ap=SL[h][:, n:n + 1], axis=0)).then_inc(fetched[h], 16)

            @block.vector
            def _(dve):
                V = nc.vector
                steps = m_.sem("steps")
                with dve.Fori(0, NB // 2) as i:
                    for h in range(2):
                        dve.wait_ge(fetched[h], i * ONE + ONE)
                        for j in range(TPB):
                            t = (i * 2 + h) * TPB + j
                            x = X[:, bass.ds(t, 1), :].rearrange("p o d -> p (o d)")
                            if r.K == 1:
                                V.tensor_tensor(x, x, Y[h][0][:, j], ALU.add).then_inc(added[h], 1)
                            else:
                                V.scalar_tensor_tensor(x, Y[h][0][:, j], r.weight[:, bass.ds(t, 1), 0], x, ALU.mult, ALU.add)\
                                    .then_inc(steps, 1)
                                dve.wait_ge(steps, i * (2 * TPB) + (h * TPB + j + 1))
                                V.scalar_tensor_tensor(x, Y[h][1][:, j], r.weight[:, bass.ds(t, 1), 1], x, ALU.mult, ALU.add)\
                                    .then_inc(added[h], 1)

            if out is not None:

                @block.sync
                def _(sp):
                    o = out.rearrange("(b t p) d -> b p t d", p=P, t=TPB)
                    with sp.Fori(0, NB // 2) as i:
                        for h in range(2):
                            sp.wait_ge(added[h], i * TPB + 2 * TPB)
                            sp.dma_start(o[bass.ds(i * 2 + h, 1)].rearrange("b p t d -> (b p) t d"),
                                         X[:, bass.ds((i * 2 + h) * TPB, TPB), :]).then_inc(stored, 16)
                    sp.wait_ge(stored, 16 * NB)
        m_.clear()


def state_space(nc, g, X, ident):
    DI = 2 * D
    CI = DI // P
    N = 16
    TAPS = 4
    RING = 4
    PREP = CI * TAPS + 3 + 7
    with ExitStack() as stack:
        m_ = Memory(nc, stack, "ss")
        WI, WO = m_.sb("wi", [P, KD, 2 * DI]), m_.sb("wo", [P, CI, D])
        WX, WT = m_.sb("wx", [P, CI, P]), m_.sb("wt", [N, DI])
        norm_w = m_.sb("norm_w", [P, KD])
        conv_w, conv_b, dt_b, skip = m_.sb("conv_w", [P, CI, TAPS]), m_.sb("conv_b", [P, CI]), m_.sb("dt_b", [P, CI]), m_.sb("skip", [P, CI])
        DECAY = m_.sb("decay", [P, CI, N])
        SEL = m_.sb("sel", [P, 2 * N], BF16)
        keep = m_.sb("keep", [P, NB + 1])
        stats, mv = m_.sb("stats", [P, NT, 6]), m_.sb("mv", [P, NT, 2])
        rstd, tmp, var, rms = (m_.sb(n, [P, NT]) for n in ("rstd", "tmp", "var", "rms"))
        HN = m_.sb("hn", [P, TPB, D])
        XR = m_.sb("xr", [P, CI, TAPS - 1 + BT])
        two = lambda name, shape, dt=F32: [m_.sb(f"{name}{b}", shape, dt) for b in range(2)]
        HT, XC, DT, DTX, BC = two("ht", [P, KD, BT]), two("xc", [P, CI, BT]), two("dt", [P, CI, BT]), two("dtx", [P, CI, BT]), two("bc", [P, BT], BF16)
        ZS, DBU, LN1 = (m_.sb(n, [P, CI, BT]) for n in ("zs", "dbu", "ln1"))
        DA, CS = two("da", [P, CI, BT]), two("cs", [P, BT])
        H = [m_.sb(f"h{b}", [P, CI, BT]) for b in range(RING)]
        DR, REST, BC2 = m_.sb("dr", [N, BT]), m_.sb("rest", [P, 2, BT]), m_.sb("bc2", [P, BT], BF16)
        c_h = m_.sb("c_h", [P, N, CI])
        y, bB, bC = m_.ps("y", [P, CI, BT]), m_.ps("bB", [P, 2, BT]), m_.ps("bC", [P, BT])
        Q = m_.ps("q", [P, BT])
        s = {n: m_.sem(n) for n in (
            "loaded", "sel_steps", "decay_done", "pre", "steps", "h_done", "t_raw", "ht_done", "x_raw", "x_done", "z_raw", "z_done",
            "conv_done", "xc_done", "zs_done", "xp_raw", "bc1_done", "bc_done", "dt_raw", "u_done", "exp_done", "ln_done",
            "dt_done", "dtx_done", "spread", "c_copied", "da_done", "dbu_done", "scan_steps", "scanned", "pr_done", "summed",
            "skip_done", "yz_done", "out_raw", "out_done")}

        def wait(engine, name, value):
            if not isinstance(value, int) or value > 0:
                engine.wait_ge(s[name], value)

        def blocks(engine, body):
            body(0, 0, True, False)
            with engine.Fori(0, NB // 2 - 1) as q:
                body(q * 2 + 1, 1, True, True)
                body(q * 2 + 2, 0, True, True)
            body(NB - 1, 1, False, True)

        with nc.Block() as block:

            @block.sync
            def _(sp):
                for dst, src in ((WI, g["in_w"]), (WO, g["out_w"]), (WX, g["xp_w"])):
                    sp.dma_start(dst[:], src.rearrange("(k p) n -> p k n", p=P)).then_inc(s["loaded"], 16)
                sp.dma_start(WT[:], g["dt_w"]).then_inc(s["loaded"], 16)
                for dst, name in ((DECAY, "A_log"), (conv_w, "conv_w")):
                    sp.dma_start(dst[:], g[name].rearrange("(c p) n -> p c n", p=P)).then_inc(s["loaded"], 16)
                for dst, name in ((norm_w, "norm_weight"), (conv_b, "conv_b"), (dt_b, "dt_b"), (skip, "skip")):
                    sp.dma_start(dst[:], g[name].rearrange("(c p) -> p c", p=P), allow_slow_non_contiguous=True)\
                        .then_inc(s["loaded"], 16)
            LOADED = 16 * 10

            @block.gpsimd
            def _(pool):
                pool.memset(SEL[:], 0.0).then_inc(s["sel_steps"], 1)
                for part in range(1, 4):
                    pool.wait_ge(s["sel_steps"], part)
                    pool.affine_select(out=SEL[:], in_=SEL[:], compare_op=ALU.not_equal, fill=1.0, base=-32 * part,
                                       pattern=[[-1, 2 * N]], channel_multiplier=1).then_inc(s["sel_steps"], 1)

                def times_x(b, par):
                    wait(pool, "dt_done", b + 1)
                    pool.tensor_tensor(DTX[par][:], DT[par][:], XC[par][:], ALU.mult).then_inc(s["dtx_done"], 1)

                def gate(b, par):
                    wait(pool, "zs_done", b + 1)
                    for c in range(CI):
                        wait(pool, "skip_done", b * CI + (c + 1))
                        pool.tensor_tensor(DTX[par][:, c], DTX[par][:, c], ZS[:, c], ALU.mult).then_inc(s["yz_done"], 1)

                def main(b, par, prep, tail):
                    for n in range(N):
                        wait(pool, "scanned", b * N + (n + 1))
                        wait(pool, "c_copied", b * N + (n + 1))
                        h = H[n % RING]
                        pool.tensor_tensor(h[:], h[:], CS[n % 2][:].unsqueeze(1).to_broadcast([P, CI, BT]), ALU.mult)\
                            .then_inc(s["pr_done"], 1)
                        if n == 1 and tail:
                            gate(b - 1, 1 - par)
                        if n == 13 and prep:
                            times_x(b + 1, 1 - par)
                times_x(0, 0)
                blocks(pool, main)
                gate(NB - 1, 1)

            @block.tensor
            def _(pe):
                pe.wait_ge(s["loaded"], LOADED)
                pe.wait_ge(s["sel_steps"], 4)

                def project(out, w, col, rhs, chunks):
                    for k in range(chunks):
                        mm = pe.matmul(out, w[:, k, col:col + P], rhs[:, k], start=(k == 0), stop=(k == chunks - 1))
                    return mm

                def turn(b, par, c):
                    wait(pe, "h_done", b * TPB + TPB)
                    wait(pe, "z_done", (b - 1) * CI) if c == 0 else wait(pe, "ht_done", b * KD + c)
                    for j in range(TPB):
                        mm = pe.transpose(Q[:, j * P:(j + 1) * P], HN[:, j, c * P:(c + 1) * P], ident[:])
                    mm.then_inc(s["t_raw"], 1)

                def x_part(b, par, c):
                    wait(pe, "ht_done", b * KD + KD) if c == 0 else wait(pe, "x_done", b * CI + c)
                    project(Q[:], WI, c * P, HT[par], KD).then_inc(s["x_raw"], 1)

                def z_part(b, par, c):
                    wait(pe, "z_done", b * CI + c)
                    project(Q[:], WI, DI + c * P, HT[par], KD).then_inc(s["z_raw"], 1)

                def x_proj(b, par):
                    wait(pe, "xc_done", b + 1)
                    project(Q[:], WX, 0, XC[par], CI).then_inc(s["xp_raw"], 1)

                def dt_proj(b, c):
                    wait(pe, "bc_done", b + 1) if c == 0 else wait(pe, "u_done", b * CI + c)
                    pe.matmul(Q[:], WT[:, c * P:(c + 1) * P], DR[:], start=True, stop=True).then_inc(s["dt_raw"], 1)

                def spread(b, par, n):
                    wait(pe, "bc_done", b + 1)
                    wait(pe, "dbu_done", b * N + (n - 1))
                    wait(pe, "c_copied", b * N + n)
                    pe.matmul(bB[:, n % 2], SEL[:, n:n + 1].to_broadcast([P, P]), BC[par][:], start=True, stop=True)
                    pe.matmul(bC[:], SEL[:, N + n:N + n + 1].to_broadcast([P, P]), BC[par][:], start=True, stop=True)\
                        .then_inc(s["spread"], 1)

                def add_up(b, n):
                    wait(pe, "pr_done", b * N + (n + 1))
                    if n == 0:
                        wait(pe, "skip_done", b * CI)
                    for c in range(CI):
                        mm = pe.matmul(y[:, c], ident[:], H[n % RING][:, c], start=(n == 0), stop=(n == N - 1))
                    mm.then_inc(s["summed"], 1)

                def out_part(b, par, half):
                    wait(pe, "yz_done", b * CI + CI)
                    for j in range(2):
                        t = (half * 2 + j) * P
                        for c in range(CI):
                            mm = pe.matmul(Q[:, j * D:(j + 1) * D], DTX[par][:, c, t:t + P], WO[:, c], start=(c == 0), stop=(c == CI - 1))
                    mm.then_inc(s["out_raw"], 1)

                def main(b, par, prep, tail):
                    def piece(n):
                        if prep and n == 1:
                            turn(b + 1, 1 - par, 0)
                            turn(b + 1, 1 - par, 1)
                        if prep and n in (2, 3, 4, 5):
                            x_part(b + 1, 1 - par, n - 2)
                        if tail and n == 6:
                            wait(pe, "x_done", (b + 2) * CI) if prep else wait(pe, "z_done", b * CI)
                            out_part(b - 1, 1 - par, 0)
                        if tail and n == 7:
                            wait(pe, "out_done", b * 2 - 1)
                            out_part(b - 1, 1 - par, 1)
                        if prep and n == 8:
                            wait(pe, "out_done", b * 2) if tail else wait(pe, "x_done", (b + 2) * CI)
                            x_proj(b + 1, 1 - par)
                        if prep and n in (10, 11):
                            dt_proj(b + 1, 2 * n - 20)
                            dt_proj(b + 1, 2 * n - 19)
                        if n in (12, 13, 14, 15):
                            if n == 12:
                                wait(pe, "u_done", (b + 2) * CI) if prep else wait(pe, "out_done", b * 2)
                            z_part(b, par, n - 12)

                    for n in range(N):
                        if n < N - 1:
                            spread(b, par, n + 1)
                        elif prep:
                            spread(b + 1, 1 - par, 0)
                        piece(n)
                        if n >= 2:
                            add_up(b, n - 2)
                        elif tail:
                            add_up(b - 1, n + N - 2)

                turn(0, 0, 0)
                turn(0, 0, 1)
                for c in range(CI):
                    x_part(0, 0, c)
                wait(pe, "x_done", CI)
                x_proj(0, 0)
                for c in range(CI):
                    dt_proj(0, c)
                spread(0, 0, 0)
                blocks(pe, main)
                add_up(NB - 1, N - 2)
                add_up(NB - 1, N - 1)
                wait(pe, "z_done", NB * CI)
                out_part(NB - 1, 1, 0)
                wait(pe, "out_done", NB * 2 - 1)
                out_part(NB - 1, 1, 1)

            @block.scalar
            def _(act):
                A_ = nc.scalar.activation
                act.wait_ge(s["loaded"], LOADED)
                A_(DECAY[:], DECAY[:], ACT.Exp).then_inc(s["decay_done"], 1)
                act.wait_ge(s["decay_done"], 2)

                def copy_ht(b, par, c):
                    wait(act, "t_raw", b * KD + (c + 1))
                    A_(HT[par][:, c], Q[:], ACT.Copy, scale=norm_w[:, c:c + 1]).then_inc(s["ht_done"], 1)

                def copy_x(b, c):
                    wait(act, "conv_done", b * CI)
                    wait(act, "x_raw", b * CI + (c + 1))
                    A_(XR[:, c, TAPS - 1:], Q[:], ACT.Copy).then_inc(s["x_done"], 1)

                def copy_z(b, c):
                    wait(act, "yz_done", b * CI)
                    wait(act, "z_raw", b * CI + (c + 1))
                    A_(ZS[:, c], Q[:], ACT.Copy).then_inc(s["z_done"], 1)

                def silu_x(b, par):
                    wait(act, "conv_done", b * CI + CI)
                    A_(XC[par][:], XC[par][:], ACT.Silu).then_inc(s["xc_done"], 1)

                def copy_bc(b, par):
                    wait(act, "xp_raw", b + 1)
                    A_(BC[par][:], Q[:], ACT.Copy)
                    A_(DR[:], Q[0:N], ACT.Copy).then_inc(s["bc1_done"], 1)

                def copy_dt(b, par, c):
                    wait(act, "out_raw", b * 2 - 2)
                    wait(act, "dt_raw", b * CI + (c + 1))
                    A_(DTX[par][:, c], Q[:], ACT.Abs, bias=dt_b[:, c:c + 1])
                    A_(DT[par][:, c], Q[:], ACT.Identity, bias=dt_b[:, c:c + 1]).then_inc(s["u_done"], 1)

                def exp(b, par):
                    wait(act, "u_done", b * CI + CI)
                    A_(DTX[par][:], DTX[par][:], ACT.Exp, scale=-1.0).then_inc(s["exp_done"], 1)

                def log(b, par):
                    wait(act, "exp_done", b + 1)
                    A_(LN1[:], DTX[par][:], ACT.Ln, bias=1.0).then_inc(s["ln_done"], 1)

                def main(b, par, prep, tail):
                    wait(act, "dt_done", b + 1)
                    for n in range(N):
                        wait(act, "scanned", b * N + (n - 1))
                        for c in range(CI):
                            ins = A_(DA[n % 2][:, c], DT[par][:, c], ACT.Exp, scale=DECAY[:, c, n:n + 1])
                        ins.then_inc(s["da_done"], 1)
                        wait(act, "spread", b * N + (n + 1))
                        wait(act, "pr_done", b * N + (n - 1))
                        A_(CS[n % 2][:], bC[:], ACT.Copy).then_inc(s["c_copied"], 1)
                        if prep and n == 2:
                            copy_ht(b + 1, 1 - par, 0)
                            copy_ht(b + 1, 1 - par, 1)
                        if prep and n in (3, 4, 5, 6):
                            copy_x(b + 1, n - 3)
                        if prep and n == 8:
                            silu_x(b + 1, 1 - par)
                        if prep and n == 9:
                            copy_bc(b + 1, 1 - par)
                        if prep and n in (11, 12):
                            copy_dt(b + 1, 1 - par, 2 * n - 22)
                            copy_dt(b + 1, 1 - par, 2 * n - 21)
                        if prep and n == 12:
                            exp(b + 1, 1 - par)
                            log(b + 1, 1 - par)
                        if n in (13, 14, 15):
                            copy_z(b, n - 13)
                    copy_z(b, 3)
                    wait(act, "z_done", b * CI + CI)
                    A_(ZS[:], ZS[:], ACT.Silu).then_inc(s["zs_done"], 1)

                copy_ht(0, 0, 0)
                copy_ht(0, 0, 1)
                for c in range(CI):
                    copy_x(0, c)
                silu_x(0, 0)
                copy_bc(0, 0)
                for c in range(CI):
                    copy_dt(0, 0, c)
                exp(0, 0)
                log(0, 0)
                blocks(act, main)

            @block.vector
            def _(dve):
                V = nc.vector
                pre = Chain(dve, s["pre"])
                pre.link(V.memset(keep[:], 1.0))
                pre.link(V.memset(keep[:, SB:SB + 1], 0.0))
                pre.mark(V.memset(c_h[:], 0.0))
                pre.link(V.memset(XR[:], 0.0))
                dve.wait_ge(s["loaded"], LOADED)
                dve.wait_ge(s["decay_done"], 1)
                V.tensor_scalar(DECAY[:], DECAY[:], -1.0, None, ALU.mult).then_inc(s["decay_done"], 1)
                ends_here = lambda b: keep[:, bass.ds(b + 1, 1)] if not isinstance(b, int) else keep[:, b + 1:b + 2]
                tiles = lambda t, n=1: X[:, bass.ds(t, n), :] if not isinstance(t, int) else X[:, t:t + n, :]

                norm_stats(nc, pre, lambda j: X[:, j], stats, mv, rstd[:], tmp[:], 1e-5, var=var[:])
                pre.link(V.tensor_tensor(var[:], var[:], rstd[:], ALU.mult))
                pre.link(V.tensor_tensor(var[:], var[:], rstd[:], ALU.mult))
                rsqrt(nc, pre, rms[:], var[:], tmp[:])
                pre.link(V.tensor_tensor(rms[:], rms[:], var[:], ALU.mult))
                pre.link(V.tensor_scalar(rms[:], rms[:], 1e-5, None, ALU.add))
                pre.link(V.reciprocal(tmp[:], rms[:]))
                pre.link(V.tensor_tensor(rstd[:], rstd[:], tmp[:], ALU.mult))

                def normalise(b):
                    wait(dve, "t_raw", b * KD)
                    for j in range(TPB):
                        t = b * TPB + j
                        at = (lambda buf: buf[:, t:t + 1]) if isinstance(t, int) else (lambda buf: buf[:, bass.ds(t, 1)])
                        V.tensor_scalar(HN[:, j], tiles(t).rearrange("p o d -> p (o d)"), at(mv)[:, :, 0], at(rstd),
                                        ALU.subtract, ALU.mult).then_inc(s["h_done"], 1)

                def convolve(b, par, c, n0):
                    ch = Chain(dve, s["steps"], b * PREP + n0)
                    wait(dve, "x_done", b * CI + (c + 1))
                    xc = XC[par][:, c]
                    ch.link(V.tensor_scalar(xc, XR[:, c, 0:BT], conv_w[:, c, 0:1], conv_b[:, c:c + 1], ALU.mult, ALU.add))
                    for t in range(1, TAPS):
                        ch.link(V.scalar_tensor_tensor(xc, XR[:, c, t:t + BT], conv_w[:, c, t:t + 1], xc, ALU.mult, ALU.add))
                    V.tensor_scalar(XR[:, c, 0:TAPS - 1], XR[:, c, BT:], ends_here(b), None, ALU.mult).then_inc(s["conv_done"], 1)
                    return n0 + ch.n

                def split_bc(b, par, n0):
                    ch = Chain(dve, s["steps"], b * PREP + n0)
                    wait(dve, "bc1_done", b + 1)
                    R1 = REST[:, 0]
                    ch.link(V.tensor_tensor(R1, Q[:], BC[par][:], ALU.subtract))
                    ch.link(V.tensor_scalar(BC2[:], R1, 1.0, None, ALU.mult))
                    ch.mark(V.tensor_scalar(BC[par][2 * 32:3 * 32], BC2[2 * 32:3 * 32], 1.0, None, ALU.mult))
                    V.tensor_tensor(BC[par][3 * 32:], REST[3 * 32:, 0], BC2[3 * 32:], ALU.subtract).then_inc(s["bc_done"], 1)
                    return n0 + ch.n

                def time_steps(b, par, n0):
                    ch = Chain(dve, s["steps"], b * PREP + n0)
                    wait(dve, "bc_done", b + 1)
                    wait(dve, "ln_done", b + 1)
                    for half in range(2):
                        e, u, ln = (buf[:, 2 * half:2 * half + 2] for buf in (DTX[par], DT[par], LN1))
                        ch.link(V.tensor_scalar(REST[:], e, 1.0, 1.0, ALU.add, ALU.subtract))
                        ch.mark(V.tensor_tensor(e, e, REST[:], ALU.subtract))
                        ch.link(V.scalar_tensor_tensor(u, u, 0.0, ln, ALU.max, ALU.add))
                        ins = V.tensor_tensor(u, u, e, ALU.add)
                        if half == 0:
                            ch.link(ins)
                    ins.then_inc(s["dt_done"], 1)
                    return n0 + ch.n

                def add_skip(b, par):
                    wait(dve, "summed", b * N + N)
                    for c in range(CI):
                        V.scalar_tensor_tensor(DTX[par][:, c], XC[par][:, c], skip[:, c:c + 1], y[:, c], ALU.mult, ALU.add)\
                            .then_inc(s["skip_done"], 1)

                def add_out(b, half):
                    wait(dve, "out_raw", b * 2 + (half + 1))
                    x = tiles(b * TPB + 2 * half, 2)
                    V.tensor_tensor(x, x, Q[:].rearrange("p (t d) -> p t d", d=D), ALU.add).then_inc(s["out_done"], 1)

                def main(b, par, prep, tail):
                    wait(dve, "dtx_done", b + 1)
                    wait(dve, "scanned", b * N)
                    for n in range(N):
                        wait(dve, "spread", b * N + (n + 1))
                        V.tensor_tensor(DBU[:], DTX[par][:], bB[:, n % 2].unsqueeze(1).to_broadcast([P, CI, BT]), ALU.mult)\
                            .then_inc(s["dbu_done"], 1)
                        wait(dve, "dbu_done", b * N + (n + 1))
                        wait(dve, "da_done", b * N + (n + 1))
                        wait(dve, "summed", b * N + (n + 1 - RING))
                        h = H[n % RING]
                        for c in range(CI):
                            ins = V.tensor_tensor_scan(h[:, c], DA[n % 2][:, c], DBU[:, c], c_h[:, n, c:c + 1], ALU.mult, ALU.add)
                        ins.then_inc(s["scan_steps"], 1)
                        wait(dve, "scan_steps", b * N + (n + 1))
                        V.tensor_scalar(c_h[:, n, :], h[:, :, BT - 1], ends_here(b), None, ALU.mult).then_inc(s["scanned"], 1)
                        if prep and n == 0:
                            normalise(b + 1)
                            n1 = 0
                        if tail and n == 1:
                            add_skip(b - 1, 1 - par)
                        if prep and n in (3, 4, 5, 6):
                            n1 = convolve(b + 1, 1 - par, n - 3, n1)
                        if tail and n == 6:
                            add_out(b - 1, 0)
                        if tail and n == 7:
                            add_out(b - 1, 1)
                        if prep and n == 9:
                            n1 = split_bc(b + 1, 1 - par, n1)
                        if prep and n == 13:
                            n1 = time_steps(b + 1, 1 - par, n1)
                    assert not prep or n1 == PREP, n1

                normalise(0)
                n1 = 0
                for c in range(CI):
                    n1 = convolve(0, 0, c, n1)
                n1 = split_bc(0, 0, n1)
                time_steps(0, 0, n1)
                blocks(dve, main)
                add_skip(NB - 1, 1)
                add_out(NB - 1, 0)
                add_out(NB - 1, 1)
        m_.clear()



def build(nc, g, out):
    with ExitStack() as stack:
        m_ = Memory(nc, stack, "all")
        ident = m_.sb("ident", [P, P])
        X = m_.sb("x", [P, NT, D])
        r0, r1 = Routing(nc, stack, "moe0", 64, 2), Routing(nc, stack, "moe1", 16, 1)
        with ExitStack() as inner:
            m_ = Memory(nc, inner, "attn")
            YS, SG = m_.sb("ys", [P, KD, T]), m_.sb("sg", [P, KD, T])
            SUMS = m_.sb("sums", [P, NB * KD * 4])
            gate_loop(nc, g["x"], g["w_proj"], X, YS, SG, SUMS, ident, (r0.xs, r1.xs))
            gate_ffn(nc, g, X, YS, SG, SUMS, ident)
        route(nc, "route0", X, g["router0"], r0, ident)
        expert_tiles(nc, "experts0", r0, g["w0"], g["w1"], g["wo"], ident)
        combine(nc, "combine0", X, r0)
        state_space(nc, g, X, ident)
        route(nc, "route1", X, g["router1"], r1, ident, shared=(g["sh_gate"], g["sh_up"], g["sh_down"]))
        half = g["gate_up"].shape[2] // 2
        expert_tiles(nc, "experts1", r1, g["gate_up"][:, :, 0:half], g["gate_up"][:, :, half:], g["down"], ident)
        combine(nc, "combine1", X, r1, out=out)


def mamba_layout(inputs):
    import numpy as np
    L = lambda n: np.asarray(inputs["L1_attn_" + n])
    w = L("x_proj_w")
    return {"in_w": L("in_proj_w").T, "out_w": L("out_proj_w").T, "dt_w": L("dt_proj_w").T,
            "xp_w": np.concatenate([w[:16], w[:16], w[16:], w[16:], w[16:]]).T,
            "A_log": L("A_log"), "conv_w": L("conv_w"), "norm_weight": L("norm_weight"), "conv_b": L("conv_b"),
            "dt_b": L("dt_proj_b"), "skip": L("D")}


def layout(inputs):
    import numpy as np
    g = mamba_layout(inputs)
    A = lambda n: np.asarray(inputs["L0_attn_" + n])
    F = lambda n: np.asarray(inputs["L1_ffn_" + n])
    g["x"] = A("x").reshape(T, D)
    g["w_proj"] = np.concatenate([A("Wa"), A("Wk"), A("Wv"), A("Wq"), A("Wg")], axis=1)
    for ours, theirs in (("Wo", "Wo"), ("gn_scale", "gn_scale"), ("gn_bias", "gn_bias"), ("W1", "W1"), ("W2", "W2"),
                         ("b1", "b1"), ("b2", "b2"), ("ln1s", "ln1_scale"), ("ln1b", "ln1_bias"),
                         ("ln2s", "ln2_scale"), ("ln2b", "ln2_bias")):
        g[ours] = A(theirs)
    g["router0"] = inputs["L0_ffn_gate_kernel"]
    for n in ("w0", "w1", "wo"):
        g[n] = inputs["L0_ffn_" + n]
    g["router1"], g["gate_up"], g["down"] = F("w_router").T, F("gate_up_proj"), F("down_proj")
    g["sh_gate"], g["sh_up"], g["sh_down"] = F("w_gate").T, F("w_up").T, F("w_down").T
    return g


_OUTS = [((BATCH, T // BATCH, D), "float32")]


def kernel(**inputs):
    import numpy as _np
    import concourse.bacc as _bacc
    from concourse.bass_utils import run_bass_kernel_spmd as _run

    given = layout(inputs)
    nc = _bacc.Bacc("TRN2", target_bir_lowering=False, num_devices=1)
    arrays, args = {}, {}
    for name, a in given.items():
        a = _np.ascontiguousarray(a)
        arrays[f"in_{name}"] = a
        args[name] = nc.dram_tensor(f"in_{name}", a.shape, mybir.dt.from_np(a.dtype), kind="ExternalInput").ap()
    outs = [nc.dram_tensor(f"out_{i}", shape, F32, kind="ExternalOutput").ap() for i, (shape, _) in enumerate(_OUTS)]
    build(nc, args, outs[0].rearrange("b s d -> (b s) d"))
    r = _run(nc, [arrays], core_ids=[0])
    return r.results[0]["out_0"]
```

```python
import math
from contextlib import ExitStack

import concourse.bass as bass
from concourse import mybir

F32 = mybir.dt.float32
BF16 = mybir.dt.bfloat16
I32 = mybir.dt.int32
U32 = mybir.dt.uint32
ALU = mybir.AluOpType
ACT = mybir.ActivationFunctionType
AX = mybir.AxisListType

P = 128
T = 4096
D = 256
KD = D // P
BATCH = 2
BT = 512
NB = T // BT
SB = NB // BATCH
TPB = BT // P
NT = T // P
ROUND = 12582912.0
RSQRT_SEED = float(0x5F3759DF)


class Chain:

    def __init__(self, engine, sem, base=0):
        self.engine, self.sem, self.base, self.n = engine, sem, base, 0

    def mark(self, ins):
        self.n += 1
        ins.then_inc(self.sem, 1)
        return self.n

    def wait(self, n):
        self.engine.wait_ge(self.sem, self.base + n)

    def link(self, ins):
        self.wait(self.mark(ins))


def rsqrt(nc, chain, out, v, tmp):
    V = nc.vector
    chain.link(V.tensor_scalar(tmp.bitcast(I32), v.bitcast(I32), 1, None, ALU.logical_shift_right))
    chain.link(V.tensor_scalar(out.bitcast(I32), tmp.bitcast(I32), -1.0, RSQRT_SEED, ALU.mult, ALU.add))
    for _ in range(3):
        chain.link(V.tensor_tensor(tmp, out, out, ALU.mult))
        chain.link(V.tensor_tensor(tmp, tmp, v, ALU.mult))
        chain.link(V.tensor_scalar(tmp, tmp, -0.5, 1.5, ALU.mult, ALU.add))
        chain.link(V.tensor_tensor(out, out, tmp, ALU.mult))


def norm_stats(nc, chain, src, stats, mv, rstd, tmp, eps, var=None):
    V = nc.vector
    n = stats.shape[1]
    for j in range(n):
        last = chain.mark(V.bn_stats(stats[:, j, :], src(j)))
    chain.wait(last)
    V.memset(tmp, 0.0)
    for j in range(n):
        last = chain.mark(V.bn_aggr(mv[:, j, :], stats[:, j, :]))
    chain.wait(last)
    if var is not None:
        chain.mark(V.tensor_copy(var, mv[:, :, 1]))
    chain.link(V.tensor_scalar(mv[:, :, 1], mv[:, :, 1], 1.0, eps, ALU.mult, ALU.add))
    rsqrt(nc, chain, rstd, mv[:, :, 1], tmp)


NORM_STEPS = 2 * TPB + 1 + 2 + 3 * 4


class Memory:

    def __init__(self, nc, stack, tag):
        self.nc, self.stack, self.tag, self.sems = nc, stack, tag, []

    def sb(self, name, shape, dt=F32):
        return self.stack.enter_context(self.nc.sbuf_tensor(f"{self.tag}_{name}", shape, dt))

    def ps(self, name, shape, dt=F32):
        return self.stack.enter_context(self.nc.psum_tensor(f"{self.tag}_{name}", shape, dt))

    def sem(self, name):
        self.sems.append(self.stack.enter_context(self.nc.semaphore(f"{self.tag}_{name}")))
        return self.sems[-1]

    def clear(self):
        with self.nc.Block() as block:

            @block.gpsimd
            def _(pool):
                for sem in self.sems:
                    pool.sem_clear(sem)


def gate_loop(nc, x_in, w_proj, XN, YS, SG, SUMS, ident, to_zero):
    TURN = 2.0 * math.pi * (1.0 - 2.0 ** -23)
    AR, AI_, K_, V_, Q_, G_ = range(6)
    SEQ = [(AR, 0), (AI_, 0), (AR, 1), (AI_, 1), (K_, 0), (V_, 0), (K_, 1), (V_, 1), (Q_, 0), (G_, 0), (Q_, 1), (G_, 1)]
    RING = 6
    slot = {fc: n for n, fc in enumerate(SEQ)}
    with ExitStack() as stack:
        m_ = Memory(nc, stack, "gl")
        W = m_.sb("w", [P, KD, 6 * D])
        XNB = m_.sb("xnb", [P, TPB, D])
        XT = m_.sb("xt", [P, KD, BT])
        stats, mv = m_.sb("stats", [P, NT, 6]), m_.sb("mv", [P, NT, 2])
        rstd, tmp = m_.sb("rstd", [P, NT]), m_.sb("tmp", [P, NT])
        SQR, SQI, AIM, ABR, KS, QS, KV, NEG, SGN, MAG, A, PHI, WR, SN, CS, UR, UI, T1, T2, T3, T4 = (
            m_.sb(n, [P, KD, BT]) for n in ("sqr", "sqi", "aim", "abr", "ks", "qs", "kv", "neg", "sgn", "mag",
                                            "a", "phi", "wr", "sn", "cs", "ur", "ui", "t1", "t2", "t3", "t4"))
        TAN, YI = SQI, T4
        zeros = m_.sb("zeros", [P, D])
        quarter = m_.sb("quarter", [P, 1])
        keep = m_.sb("keep", [P, NB + 1])
        c_phase, c_u = m_.sb("c_phase", [P, KD]), m_.sb("c_u", [P, KD, 2])
        pT = m_.ps("pT", [P, KD, BT])
        bank = [m_.ps(f"bank{i}", [P, BT]) for i in range(RING)]
        s = {n: m_.sem(n) for n in (
            "w_loaded", "consts", "pre", "zeroed", "xn_done", "xn_kept", "xt_raw", "xt_done", "sq_done", "m2_done", "mag_done",
            "t_done", "atan_done", "turn_done", "abs_done", "trig_done", "u_done", "hi_done", "pool_steps", "y_done", "steps")}
        x_loaded = [m_.sem(f"x_loaded{i}") for i in range(NB)]
        bank_free = [m_.sem(f"bank_free{i}") for i in range(RING)]
        proj = [m_.sem(f"proj{i}") for i in range(6)]

        def freed(i, fc):
            return bank_free[slot[fc] % RING], i * 2 + (slot[fc] // RING + 2)

        with nc.Block() as block:

            @block.sync
            def _(sp):
                x_blocks = x_in.rearrange("(b t p) d -> b p t d", p=P, t=TPB)
                for i in range(NB):
                    sp.dma_start(XN[:, i * TPB:(i + 1) * TPB], x_blocks[i]).then_inc(x_loaded[i], 16)
                    if i == 0:
                        sp.dma_start(W[:], w_proj.rearrange("(k p) n -> p k n", p=P)).then_inc(s["w_loaded"], 16)

                def fill(i):
                    for array in to_zero:
                        part = array.rearrange("(b t p) d -> b p t d", b=NB, p=P)
                        n = part.shape[2]
                        part = part[i] if isinstance(i, int) else part[bass.ds(i, 1)].rearrange("b p t d -> (b p) t d")
                        sp.dma_start(part, zeros[:].unsqueeze(1).to_broadcast([P, n, D])).then_inc(s["zeroed"], 16)
                sp.wait_ge(s["consts"], 3)
                fill(0)
                with sp.Fori(1, NB) as i:
                    sp.wait_ge(s["xn_done"], i * TPB)
                    fill(i)
                sp.wait_ge(s["zeroed"], 16 * NB * len(to_zero))

            @block.gpsimd
            def _(pool):
                pool.memset(ident[:], 0.0).then_inc(s["consts"], 1)
                pool.wait_ge(s["consts"], 1)
                pool.affine_select(out=ident[:], in_=ident[:], compare_op=ALU.not_equal, fill=1.0, base=0,
                                   pattern=[[-1, P]], channel_multiplier=1).then_inc(s["consts"], 1)
                pool.memset(zeros[:], 0.0)
                pool.memset(quarter[:], math.pi / 2).then_inc(s["consts"], 1)
                with pool.Fori(0, NB) as i:
                    for c in range(KD):
                        n = i * KD + (c + 1)
                        pool.wait_ge(s["trig_done"], n)
                        pool.wait_ge(s["u_done"], n)
                        pool.tensor_tensor(T3[:, c], SN[:, c], UR[:, c], ALU.mult).then_inc(s["pool_steps"], 1)
                        pool.tensor_tensor(T4[:, c], CS[:, c], UI[:, c], ALU.mult).then_inc(s["pool_steps"], 1)
                        pool.wait_ge(s["pool_steps"], i * (2 * KD) + (2 * c + 2))
                        pool.tensor_tensor(T3[:, c], T3[:, c], T4[:, c], ALU.subtract).then_inc(s["hi_done"], 1)

            @block.tensor
            def _(pe):
                pe.wait_ge(s["consts"], 2)
                pe.wait_ge(s["w_loaded"], 16)
                for b in bank_free:
                    pe.sem_inc(b, 1)

                def turn(i):
                    pe.wait_ge(s["xn_done"], i * TPB + TPB)
                    for j in range(TPB):
                        for c in range(KD):
                            mm = pe.transpose(pT[:, c, j * P:(j + 1) * P], XNB[:, j, c * P:(c + 1) * P], ident[:])
                    mm.then_inc(s["xt_raw"], 1)

                def project(i):
                    pe.wait_ge(s["xt_done"], i * KD + KD)
                    for n, (f, c) in enumerate(SEQ):
                        pe.wait_ge(bank_free[n % RING], i * 2 + (n // RING + 1))
                        for k in range(KD):
                            mm = pe.matmul(bank[n % RING][:], W[:, k, f * D + c * P:f * D + (c + 1) * P], XT[:, k],
                                           start=(k == 0), stop=(k == KD - 1))
                        mm.then_inc(proj[f], 1)

                turn(0)
                with pe.Fori(0, NB - 1) as i:
                    project(i)
                    turn(i + 1)
                project(NB - 1)

            @block.scalar
            def _(act):
                act.wait_ge(s["consts"], 3)
                A_ = nc.scalar.activation

                def copy_xt(i):
                    act.wait_ge(s["xt_raw"], i + 1)
                    for c in range(KD):
                        A_(XT[:, c], pT[:, c], ACT.Copy).then_inc(s["xt_done"], 1)
                    A_(XN[:, i * TPB:(i + 1) * TPB] if isinstance(i, int) else XN[:, bass.ds(i * TPB, TPB), :], XNB[:], ACT.Copy)\
                        .then_inc(s["xn_kept"], 1)

                def body(i, more):
                    bank_of = lambda f, c: bank[slot[f, c] % RING][:]
                    free_of = lambda f, c: bank_free[slot[f, c] % RING]
                    for c in range(KD):
                        act.wait_ge(proj[AR], i * KD + (c + 1))
                        A_(SQR[:, c], bank_of(AR, c), ACT.Square)
                        A_(ABR[:, c], bank_of(AR, c), ACT.Abs)
                        act.wait_ge(proj[AI_], i * KD + (c + 1))
                        A_(SQI[:, c], bank_of(AI_, c), ACT.Square).then_inc(s["sq_done"], 1)
                        A_(AIM[:, c], bank_of(AI_, c), ACT.Copy).then_inc(free_of(AI_, c), 1)
                    for c in range(KD):
                        act.wait_ge(proj[K_], i * KD + (c + 1))
                        A_(KS[:, c], bank_of(K_, c), ACT.Copy).then_inc(free_of(K_, c), 1)
                    for c in range(KD):
                        act.wait_ge(s["m2_done"], i * KD + (c + 1))
                        A_(MAG[:, c], SQR[:, c], ACT.Sqrt).then_inc(s["mag_done"], 1)
                    for c in range(KD):
                        act.wait_ge(s["mag_done"], i * KD + (c + 1))
                        A_(A[:, c], MAG[:, c], ACT.Sigmoid)
                    for c in range(KD):
                        act.wait_ge(s["t_done"], i * KD + (c + 1))
                        A_(PHI[:, c], TAN[:, c], ACT.Arctan).then_inc(s["atan_done"], 1)
                    for c in range(KD):
                        act.wait_ge(proj[Q_], i * KD + (c + 1))
                        A_(QS[:, c], bank_of(Q_, c), ACT.Copy).then_inc(free_of(Q_, c), 1)
                        act.wait_ge(proj[G_], i * KD + (c + 1))
                        A_((SG[:, c, i * BT:(i + 1) * BT] if isinstance(i, int) else SG[:, c, bass.ds(i * BT, BT)]), bank_of(G_, c), ACT.Silu).then_inc(free_of(G_, c), 1)
                    for c in range(KD):
                        act.wait_ge(s["turn_done"], i * KD + (c + 1))
                        A_(ABR[:, c], WR[:, c], ACT.Abs).then_inc(s["abs_done"], 1)
                        A_(SN[:, c], WR[:, c], ACT.Sin, scale=TURN)
                        act.wait_ge(s["abs_done"], i * KD + (c + 1))
                        A_(CS[:, c], ABR[:, c], ACT.Sin, scale=-TURN, bias=quarter[:]).then_inc(s["trig_done"], 1)
                    act.wait_ge(s["trig_done"], i * KD + KD)
                    if more:
                        copy_xt(i + 1)

                copy_xt(0)
                with act.Fori(0, NB - 1) as i:
                    body(i, True)
                body(NB - 1, False)

            @block.vector
            def _(dve):
                V = nc.vector
                pre = Chain(dve, s["pre"])

                def x_tile(j):
                    if j % TPB == 0:
                        dve.wait_ge(x_loaded[j // TPB], 16)
                    return XN[:, j]

                def row_stats(a, b):
                    norm_stats(nc, pre, lambda j: x_tile(a + j), stats[:, a:b], mv[:, a:b], rstd[:, a:b], tmp[:, a:b], 1e-5)
                pre.mark(V.memset(c_phase[:], 0.0))
                pre.mark(V.memset(c_u[:], 0.0))
                pre.link(V.memset(keep[:], 1.0))
                pre.link(V.memset(keep[:, SB:SB + 1], 0.0))
                dve.wait_ge(s["consts"], 3)
                of = lambda buf, t, n=1: buf[:, t:t + n] if isinstance(t, int) else buf[:, bass.ds(t, n)]

                def normalise(i):
                    for j in range(TPB):
                        t = i * TPB + j
                        V.tensor_scalar(XNB[:, j], of(XN, t).rearrange("p o d -> p (o d)"), of(mv, t)[:, :, 0], of(rstd, t),
                                        ALU.subtract, ALU.mult).then_inc(s["xn_done"], 1)

                def squares(i):
                    for c in range(KD):
                        dve.wait_ge(s["sq_done"], i * KD + (c + 1))
                        V.tensor_tensor(SQR[:, c], SQR[:, c], SQI[:, c], ALU.add).then_inc(s["m2_done"], 1)
                        V.tensor_scalar(NEG[:, c], bank[slot[AR, c] % RING][:], 0.0, 0.5, ALU.is_lt, ALU.mult)\
                            .then_inc(bank_free[slot[AR, c] % RING], 1)

                PER = 19 * KD
                def body(i, more):
                    ch = Chain(dve, s["steps"], i * PER)
                    def after(name, c):
                        dve.wait_ge(s[name], i * KD + (c + 1))
                    for c in range(KD):
                        dve.wait_ge(*freed(i, (AR, c)))
                        ch.mark(V.tensor_scalar(SGN[:, c], NEG[:, c], -4.0 / math.pi, 1.0 / math.pi, ALU.mult, ALU.add))
                        dve.wait_ge(proj[V_], i * KD + (c + 1))
                        dve.wait_ge(*freed(i, (K_, c)))
                        V.tensor_tensor(KV[:, c], KS[:, c], bank[slot[V_, c] % RING][:], ALU.mult)\
                            .then_inc(bank_free[slot[V_, c] % RING], 1)
                    for c in range(KD):
                        after("mag_done", c)
                        ch.link(V.scalar_tensor_tensor(T1[:, c], ABR[:, c], 1e-30, MAG[:, c], ALU.add, ALU.add))
                        ch.link(V.reciprocal(T2[:, c], T1[:, c]))
                        V.tensor_tensor(TAN[:, c], AIM[:, c], T2[:, c], ALU.mult).then_inc(s["t_done"], 1)
                    for c in range(KD):
                        after("atan_done", c)
                        ch.link(V.tensor_tensor(T1[:, c], PHI[:, c], SGN[:, c], ALU.mult))
                        ch.link(V.tensor_tensor_scan(PHI[:, c], T1[:, c], NEG[:, c], c_phase[:, c:c + 1], ALU.add, ALU.add))
                        ch.link(V.tensor_scalar(T2[:, c], PHI[:, c], ROUND, ROUND, ALU.add, ALU.subtract))
                        V.tensor_tensor(WR[:, c], PHI[:, c], T2[:, c], ALU.subtract).then_inc(s["turn_done"], 1)
                        after("turn_done", c)
                        ch.mark(V.tensor_copy(c_phase[:, c:c + 1], WR[:, c, BT - 1:BT]))
                    if more:
                        dve.wait_ge(s["xt_raw"], i + 1)
                        dve.wait_ge(s["xn_kept"], i + 1)
                        normalise(i + 1)
                    for c in range(KD):
                        after("trig_done", c)
                        ch.mark(V.tensor_tensor(T1[:, c], KV[:, c], CS[:, c], ALU.mult))
                        ch.link(V.tensor_tensor(T2[:, c], KV[:, c], SN[:, c], ALU.mult))
                        ch.link(V.tensor_tensor_scan(UR[:, c], A[:, c], T1[:, c], c_u[:, c, 0:1], ALU.mult, ALU.add))
                        V.tensor_tensor_scan(UI[:, c], A[:, c], T2[:, c], c_u[:, c, 1:2], ALU.mult, ALU.add)\
                            .then_inc(s["u_done"], 1)
                        after("u_done", c)
                        ch.mark(V.tensor_scalar(c_u[:, c, 0:1], UR[:, c, BT - 1:BT], of(keep, i + 1), None, ALU.mult))
                        ch.mark(V.tensor_scalar(c_u[:, c, 1:2], UI[:, c, BT - 1:BT], of(keep, i + 1), None, ALU.mult))
                        ch.mark(V.tensor_tensor(T1[:, c], CS[:, c], UR[:, c], ALU.mult))
                        ch.link(V.tensor_tensor(T2[:, c], SN[:, c], UI[:, c], ALU.mult))
                        ch.link(V.tensor_tensor(T1[:, c], T1[:, c], T2[:, c], ALU.add))
                    if more:
                        squares(i + 1)
                    for c in range(KD):
                        ys = YS[:, c, i * BT:(i + 1) * BT] if isinstance(i, int) else YS[:, c, bass.ds(i * BT, BT)]
                        at = lambda n: of(SUMS, (i * KD + c) * 4 + n)
                        ch.link(V.scalar_tensor_tensor(ys, T1[:, c], 1.0, QS[:, c], ALU.mult, ALU.mult, accum_out=at(0)))
                        ch.mark(V.scalar_tensor_tensor(T2[:, c], ys, 1.0, ys, ALU.mult, ALU.mult, accum_out=at(2)))
                        after("hi_done", c)
                        ch.link(V.scalar_tensor_tensor(YI[:, c], T3[:, c], 1.0, QS[:, c], ALU.mult, ALU.mult, accum_out=at(1)))
                        ch.link(V.scalar_tensor_tensor(T2[:, c], YI[:, c], 1.0, YI[:, c], ALU.mult, ALU.mult, accum_out=at(3)))
                    assert ch.n == PER, ch.n

                row_stats(0, TPB)
                normalise(0)
                row_stats(TPB, NT)
                squares(0)
                with dve.Fori(0, NB - 1) as i:
                    body(i, True)
                body(NB - 1, False)
        m_.clear()


def gate_ffn(nc, g, X, YS, SG, SUMS, ident):
    F = 4 * D
    FC = F // P
    with ExitStack() as stack:
        m_ = Memory(nc, stack, "gf")
        WO, W1, W2 = m_.sb("wo", [P, KD, D]), m_.sb("w1", [P, KD, F]), m_.sb("w2", [P, FC, D])
        gns, gnb, b1 = m_.sb("gns", [P, KD]), m_.sb("gnb", [P, KD]), m_.sb("b1", [P, FC])
        rows = {n: m_.sb(n, [P, D]) for n in ("ln1s", "ln1b", "b2", "ln2s", "ln2b")}
        group = m_.sb("group", [P, P])
        ST, MEAN = m_.sb("st", [P, BATCH, KD, 4]), m_.sb("mean", [P, BATCH, KD, 4])
        VAR, SQ, RS, TMP = (m_.sb(n, [P, BATCH, KD]) for n in ("var", "sq", "rs", "tmp"))
        AB = m_.sb("ab", [P, NB, KD, 2])
        Z = m_.sb("z", [P, KD, BT])
        XB = m_.sb("xb", [P, TPB, D])
        R, R2, X1N, X1, O2N = (m_.sb(n, [P, TPB, D]) for n in ("r", "r2", "x1n", "x1", "o2n"))
        XT, H = m_.sb("xt", [P, KD, BT]), m_.sb("h", [P, FC, BT])
        stats, mv = m_.sb("stats", [P, TPB, 6]), m_.sb("mv", [P, TPB, 2])
        rstd, tmp = m_.sb("rstd", [P, TPB]), m_.sb("tmp2", [P, TPB])
        pO, pW, pT = (m_.ps(n, [P, TPB, D]) for n in ("pO", "pW", "pT"))
        pH = [m_.ps(f"pH{n}", [P, BT]) for n in range(2)]
        pTf = pT[:].rearrange("p (c a) d -> p c (a d)", c=KD)
        s = {n: m_.sem(n) for n in ("gn_loaded", "wo_loaded", "loaded", "group_done", "st_done", "mean_done", "steps", "z_steps", "z_done", "wo_done",
                                    "residual_done", "x_loaded", "x1n_done", "x1_done", "xt_raw", "xt_done", "h_ready", "h_free", "w2_done",
                                    "r2_done", "o2n_done", "out_done", "pool_steps", "act_steps")}
        row = lambda n: rows[n][:].unsqueeze(1).to_broadcast([P, TPB, D])
        blk = lambda buf, i: buf[:, bass.ds(i * TPB, TPB), :]

        with nc.Block() as block:

            @block.sync
            def _(sp):
                for dst, name, done in ((gns, "gn_scale", "gn_loaded"), (gnb, "gn_bias", "gn_loaded"), (b1, "b1", "loaded")):
                    sp.dma_start(dst[:], g[name].rearrange("(k p) -> p k", p=P), allow_slow_non_contiguous=True)\
                        .then_inc(s[done], 16)
                for dst, name, done in ((WO, "Wo", "wo_loaded"), (W1, "W1", "loaded"), (W2, "W2", "loaded")):
                    sp.dma_start(dst[:], g[name].rearrange("(k p) n -> p k n", p=P)).then_inc(s[done], 16)
                for name in rows:
                    sp.dma_start(rows[name][:], g[name].partition_broadcast(P)).then_inc(s["loaded"], 16)
                x_blocks = g["x"].rearrange("(b t p) d -> b p t d", p=P, t=TPB)
                sp.dma_start(XB[:], x_blocks[0]).then_inc(s["x_loaded"], 16)
                with sp.Fori(1, NB) as i:
                    sp.wait_ge(s["out_done"], i + 1)
                    sp.dma_start(XB[:], x_blocks[bass.ds(i, 1)].rearrange("b p t d -> (b p) t d"))\
                        .then_inc(s["x_loaded"], 16)
            LOADED = 16 * 8

            @block.gpsimd
            def _(pool):
                gm = group[:].rearrange("p (a b) -> p a b", b=8)
                pool.memset(group[:], 1.0 / (8 * (T // BATCH))).then_inc(s["pool_steps"], 1)
                pool.wait_ge(s["pool_steps"], 1)
                pool.affine_select(out=gm, in_=gm, compare_op=ALU.is_ge, fill=0.0, base=0,
                                   pattern=[[-8, P // 8], [0, 8]], channel_multiplier=1).then_inc(s["pool_steps"], 1)
                pool.wait_ge(s["pool_steps"], 2)
                pool.affine_select(out=gm, in_=gm, compare_op=ALU.is_ge, fill=0.0, base=7,
                                   pattern=[[8, P // 8], [0, 8]], channel_multiplier=-1).then_inc(s["group_done"], 1)
                pool.wait_ge(s["loaded"], LOADED)
                pool.sem_inc(s["out_done"], 1)

                def x1(i, base, first=False):
                    if not first:
                        pool.wait_ge(s["xt_raw"], i)
                    pool.wait_ge(s["x1n_done"], i * TPB + TPB)
                    ch = Chain(pool, s["pool_steps"], base)
                    ch.link(pool.tensor_tensor(X1[:], X1N[:], row("ln1s"), ALU.mult))
                    pool.tensor_tensor(X1[:], X1[:], row("ln1b"), ALU.add).then_inc(s["x1_done"], 1)
                    pool.wait_ge(s["x1_done"], i + 1)
                    pool.tensor_tensor(blk(X, i), X1[:], row("b2"), ALU.add).then_inc(s["residual_done"], 1)
                    pool.wait_ge(s["residual_done"], i + 1)

                def out(i, base):
                    pool.wait_ge(s["o2n_done"], i * TPB + 2 * TPB)
                    ch = Chain(pool, s["pool_steps"], base)
                    ch.link(pool.tensor_tensor(O2N[:], O2N[:], row("ln2s"), ALU.mult))
                    ch.link(pool.tensor_tensor(O2N[:], O2N[:], row("ln2b"), ALU.add))
                    pool.wait_ge(s["x_loaded"], i * 16 + 16)
                    pool.tensor_tensor(blk(X, i), XB[:], O2N[:], ALU.add).then_inc(s["out_done"], 1)

                x1(0, 2, first=True)
                with pool.Fori(1, NB) as i:
                    x1(i, i * 3)
                    out(i - 1, i * 3 + 1)
                out(NB - 1, NB * 3)

            @block.tensor
            def _(pe):
                pe.wait_ge(s["group_done"], 1)
                pe.wait_ge(s["st_done"], BATCH)
                pe.matmul(pO[:].rearrange("p t d -> p (t d)")[:, 0:16], group[:], ST[:].rearrange("p b c f -> p (b c f)"),
                          start=True, stop=True).then_inc(s["mean_done"], 1)
                pe.sem_inc(s["h_free"], 2)
                pe.sem_inc(s["o2n_done"], TPB)

                def wo(i):
                    pe.wait_ge(s["z_done"], i * KD + KD)
                    for j in range(TPB):
                        for k in range(KD):
                            mm = pe.matmul(pO[:, j], Z[:, k, j * P:(j + 1) * P], WO[:, k], start=(k == 0), stop=(k == KD - 1))
                        mm.then_inc(s["wo_done"], 1)

                def turn(i):
                    pe.wait_ge(s["x1_done"], i + 1)
                    for c in range(KD):
                        for j in range(TPB):
                            mm = pe.transpose(pTf[:, c, j * P:(j + 1) * P], X1[:, j, c * P:(c + 1) * P], ident[:])
                    mm.then_inc(s["xt_raw"], 1)

                def ffn(i):
                    pe.wait_ge(s["xt_done"], i * KD + KD)
                    for f in range(FC):
                        pe.wait_ge(s["h_free"], i * FC + (f + 1))
                        for k in range(KD):
                            mm = pe.matmul(pH[f % 2][:], W1[:, k, f * P:(f + 1) * P], XT[:, k], start=(k == 0), stop=(k == KD - 1))
                        mm.then_inc(s["h_ready"], 1)
                    pe.wait_ge(s["h_free"], i * FC + (FC + 2))
                    pe.wait_ge(s["o2n_done"], i * TPB + TPB)
                    for j in range(TPB):
                        for f in range(FC):
                            mm = pe.matmul(pW[:, j], H[:, f, j * P:(j + 1) * P], W2[:, f], start=(f == 0), stop=(f == FC - 1))
                        mm.then_inc(s["w2_done"], 1)

                pe.wait_ge(s["wo_loaded"], 16)
                wo(0)
                pe.wait_ge(s["loaded"], LOADED)
                turn(0)
                with pe.Fori(1, NB) as i:
                    wo(i)
                    ffn(i - 1)
                    turn(i)
                ffn(NB - 1)

            @block.scalar
            def _(act):
                act.wait_ge(s["loaded"], LOADED)

                def copy_xt(i):
                    act.wait_ge(s["xt_raw"], i + 1)
                    for c in range(KD):
                        nc.scalar.activation(XT[:, c], pTf[:, c], ACT.Copy).then_inc(s["xt_done"], 1)

                def gelu(i):
                    for f in range(FC):
                        act.wait_ge(s["h_ready"], i * FC + (f + 1))
                        nc.scalar.activation(H[:, f], pH[f % 2][:], ACT.Gelu_apprx_tanh, bias=b1[:, f:f + 1])\
                            .then_inc(s["h_free"], 1)

                copy_xt(0)
                with act.Fori(1, NB) as i:
                    gelu(i - 1)
                    copy_xt(i)
                gelu(NB - 1)

            @block.vector
            def _(dve):
                V = nc.vector
                pre = Chain(dve, s["steps"])
                for b in range(BATCH):
                    V.tensor_reduce(ST[:, b], SUMS[:].rearrange("p (b s c f) -> p b c f s", b=BATCH, s=SB, c=KD)[:, b], AX.X, ALU.add)\
                        .then_inc(s["st_done"], 1)
                dve.wait_ge(s["gn_loaded"], 32)
                dve.wait_ge(s["mean_done"], 1)
                pre.link(V.tensor_copy(MEAN[:].rearrange("p b c f -> p (b c f)"), pO[:].rearrange("p t d -> p (t d)")[:, 0:16]))
                f_ = lambda n: MEAN[:, :, :, n]
                pre.link(V.tensor_tensor(VAR[:], f_(2), f_(3), ALU.add))
                pre.link(V.tensor_tensor(SQ[:], f_(0), f_(0), ALU.mult))
                pre.link(V.tensor_tensor(VAR[:], VAR[:], SQ[:], ALU.subtract))
                pre.link(V.tensor_tensor(SQ[:], f_(1), f_(1), ALU.mult))
                pre.link(V.tensor_tensor(VAR[:], VAR[:], SQ[:], ALU.subtract))
                pre.link(V.tensor_scalar(VAR[:], VAR[:], 1.0, 1e-6, ALU.mult, ALU.add))
                rsqrt(nc, pre, RS[:], VAR[:], TMP[:])
                gs = gns[:].unsqueeze(1).to_broadcast([P, BATCH, KD])
                gb = gnb[:].unsqueeze(1).to_broadcast([P, BATCH, KD])
                pre.link(V.tensor_tensor(RS[:], RS[:], gs, ALU.mult))
                pre.link(V.tensor_tensor(SQ[:], f_(0), RS[:], ALU.mult))
                pre.link(V.tensor_tensor(SQ[:], gb, SQ[:], ALU.subtract))
                for n, src in ((0, RS), (1, SQ)):
                    pre.link(V.tensor_copy(AB[:, :, :, n].rearrange("p (b s) c -> p b s c", b=BATCH),
                                           src[:].unsqueeze(2).to_broadcast([P, BATCH, SB, KD])))

                def z(i):
                    scale = lambda c, n: AB[:, bass.ds(i, 1), c, n] if not isinstance(i, int) else AB[:, i:i + 1, c, n]
                    for c in range(KD):
                        pre_z = V.tensor_scalar(Z[:, c], YS[:, c, bass.ds(i * BT, BT)], scale(c, 0), scale(c, 1), ALU.mult, ALU.add)
                        pre_z.then_inc(s["z_steps"], 1)
                        dve.wait_ge(s["z_steps"], i * KD + (c + 1))
                        V.tensor_tensor(Z[:, c], Z[:, c], SG[:, c, bass.ds(i * BT, BT)], ALU.mult).then_inc(s["z_done"], 1)

                def norm(i, base, psum, psum_done, residual, buf, out, out_done):
                    ch = Chain(dve, s["steps"], base)
                    for j in range(TPB):
                        if j % 2 == 0:
                            dve.wait_ge(s[psum_done], i * TPB + (j + 2))
                        last = ch.mark(V.tensor_tensor(buf[:, j], psum[:, j], residual(j), ALU.add))
                    ch.wait(last)
                    norm_stats(nc, ch, lambda j: buf[:, j], stats, mv, rstd[:], tmp[:], 1e-6)
                    for j in range(TPB):
                        V.tensor_scalar(out[:, j], buf[:, j], mv[:, j, 0:1], rstd[:, j:j + 1], ALU.subtract, ALU.mult)\
                            .then_inc(s[out_done], 1)

                PER = TPB + NORM_STEPS
                tile = lambda i: (lambda j: X[:, bass.ds(i * TPB + j, 1), :].rearrange("p o d -> p (o d)"))

                def first(i, base):
                    norm(i, base, pO, "wo_done", tile(i), R, X1N, "x1n_done")

                def second(i, base):
                    dve.wait_ge(s["out_done"], i + 1)
                    dve.wait_ge(s["residual_done"], i + 1)
                    norm(i, base, pW, "w2_done", tile(i), R2, O2N, "o2n_done")

                n0 = pre.n
                z(0)
                first(0, n0)
                z(1)
                with dve.Fori(1, NB - 1) as i:
                    dve.wait_ge(s["x1_done"], i)
                    first(i, (i * 2 - 1) * PER + n0)
                    z(i + 1)
                    second(i - 1, (i * 2) * PER + n0)
                dve.wait_ge(s["x1_done"], NB - 1)
                first(NB - 1, (2 * NB - 3) * PER + n0)
                second(NB - 2, (2 * NB - 2) * PER + n0)
                second(NB - 1, (2 * NB - 1) * PER + n0)
        m_.clear()


class Routing:

    def __init__(self, nc, stack, tag, experts, k):
        m_ = Memory(nc, stack, tag)
        self.E, self.K = experts, k
        self.tiles = (T * k + experts * (P - 1)) // P
        self.tiles += -self.tiles % 4
        self.slot = m_.sb("slot", [P, NT, k], I32)
        self.weight = m_.sb("weight", [P, NT, k])
        self.expert = m_.sb("expert", [1, P], I32)
        self.xs = nc.dram_tensor(f"{tag}_xs", (self.tiles * P, D), F32).ap()
        self.ys = nc.dram_tensor(f"{tag}_ys", (self.tiles * P, D), F32).ap()


def route(nc, tag, X, gate, r, ident, shared=None):
    E, K = r.E, r.K
    FS = 512 // P
    with ExitStack() as stack:
        m_ = Memory(nc, stack, tag)
        G = m_.sb("gate", [P, KD, E])
        iota_i, iota = m_.sb("iota_i", [P, E], I32), m_.sb("iota", [P, E])
        part_i, part = m_.sb("part_i", [P, 1], I32), m_.sb("part", [P, 1])
        tri, ones = m_.sb("tri", [P, P], BF16), m_.sb("ones", [P, P], BF16)
        onef = m_.sb("onef", [P, E])
        stats, mv = m_.sb("stats", [P, NT, 6]), m_.sb("mv", [P, NT, 2])
        rstd, tmp = m_.sb("rstd", [P, NT]), m_.sb("tmp", [P, NT])
        XN = m_.sb("xn", [P, TPB, D])
        XT = [m_.sb(f"xt{h}", [P, KD, BT]) for h in range(2)]
        IDXA, RKA, DIF = m_.sb("idxa", [P, NT, K]), m_.sb("rka", [P, NT, K]), m_.sb("dif", [P, NT])
        XS = [m_.sb(f"xs{h}", [P, TPB, D]) for h in range(2)]
        SL = [m_.sb(f"sl{h}", [P, TPB, K], I32) for h in range(2)]
        BASE, pause = m_.sb("base", [P, TPB, K]), m_.sb("pause", [P, 1])
        V8, I8 = m_.sb("v8", [P, TPB, 8]), m_.sb("i8", [P, TPB, 8], U32)
        IDX, RK = m_.sb("idx", [P, TPB, K]), m_.sb("rk", [P, TPB, K])
        EX, DEN, W0 = (m_.sb(n, [P, NT]) for n in ("ex", "den", "w0"))
        OH0, OH, JUNK = m_.sb("oh0", [P, TPB, E], BF16), m_.sb("oh", [P, TPB, E], BF16), m_.sb("junk", [P, TPB * K, E])
        JUNKS = [JUNK[:, n] for n in range(TPB * K)]
        COUNT = m_.sb("count", [P, E])
        NTILE, END = m_.sb("ntile", [P, E]), m_.sb("end", [P, E])
        START, OWNER = m_.sb("start", [P, E]), m_.sb("owner", [P, 1])
        pT = m_.ps("pT", [P, KD, BT])
        pL, pR = m_.ps("pL", [P, BT]), m_.ps("pR", [P, BT])
        pLt = pL[:, 0:TPB * E].rearrange("p (t e) -> p t e", e=E)
        pRt = pR[:, 0:(TPB + 1) * E].rearrange("p (t e) -> p t e", e=E)
        names = ["loaded", "consts", "pre", "steps", "pool_steps", "xn_done", "xa_done", "xt_raw", "xt_done", "logits_done",
                 "max_done", "index_done", "dif_done", "exp_done", "onehot_done", "rank_done", "rows_ready", "passed",
                 "owner_done", "owner_turned", "expert_ready"]
        if shared:
            XA = m_.sb("xa", [P, NT, D])
            SW = [m_.sb(f"sw{n}", [P, KD, 512]) for n in range(2)]
            SD = m_.sb("sd", [P, FS, D])
            SIL, IN = m_.sb("sil", [P, 2, BT]), m_.sb("in", [P, FS, BT])
            pG, pU = m_.ps("pG", [P, 2, BT]), m_.ps("pU", [P, 2, BT])
            pS = pT[:].rearrange("p c (t d) -> p (c t) d", d=D)
            names += ["gate_up", "silu_done", "inner_done", "shared_done", "shared_added"]
        s = {n: m_.sem(n) for n in names}
        sent = [m_.sem(f"sent{h}") for h in range(2)]
        SENT = 16 * TPB * K
        LOADED = 16 * (4 if shared else 1)

        def blocks(engine, body):
            with engine.Fori(0, NB // 2 - 1) as q:
                body(q * 2, 0, True)
                body(q * 2 + 1, 1, True)
            body(NB - 2, 0, True)
            body(NB - 1, 1, False)

        with nc.Block() as block:

            @block.sync
            def _(sp):
                sp.dma_start(G[:], gate.rearrange("(k p) e -> p k e", p=P)).then_inc(s["loaded"], 16)
                if shared:
                    for dst, src in zip(SW, shared):
                        sp.dma_start(dst[:], src.rearrange("(k p) n -> p k n", p=P)).then_inc(s["loaded"], 16)
                    sp.dma_start(SD[:], shared[2].rearrange("(k p) n -> p k n", p=P)).then_inc(s["loaded"], 16)

            @block.gpsimd
            def _(pool):
                pool.memset(onef[:], 1.0)
                pool.memset(pause[:], 0.0)
                pool.memset(ones[:], 1.0)
                pool.memset(tri[:], 1.0).then_inc(s["pool_steps"], 1)
                pool.iota(iota_i[:], [[1, E]], base=0, channel_multiplier=0)
                pool.iota(part_i[:], [[0, 1]], base=0, channel_multiplier=1).then_inc(s["pool_steps"], 1)
                pool.wait_ge(s["pool_steps"], 2)
                pool.affine_select(out=tri[:], in_=tri[:], compare_op=ALU.is_gt, fill=0.0, base=0,
                                   pattern=[[1, P]], channel_multiplier=-1)
                pool.tensor_copy(iota[:], iota_i[:])
                pool.tensor_copy(part[:], part_i[:]).then_inc(s["consts"], 1)
                with pool.Fori(0, NB // 2) as i:
                    for h in range(2):
                        pool.wait_ge(s["rows_ready"], i * 2 + (h + 1))
                        pool.tensor_tensor(pause[:], onef[:, 0:1], onef[:, 0:1], ALU.add).then_inc(s["passed"], 1)
                        pool.wait_ge(s["passed"], 1)
                        pool.sem_clear(s["passed"])
                        for j in range(TPB):
                            for k in range(K):
                                pool.indirect_dma_start(r.xs, bass.IndirectOffsetOnAxis(ap=SL[h][:, j, k:k + 1], axis=0),
                                                        XS[h][:, j], None).then_inc(sent[h], 16)
                for h in range(2):
                    pool.wait_ge(sent[h], SENT * (NB // 2))

            @block.tensor
            def _(pe):
                pe.wait_ge(s["consts"], 1)
                pe.wait_ge(s["loaded"], LOADED)
                if shared:
                    pe.sem_inc(s["shared_added"], 1)

                def turn(b):
                    pe.wait_ge(s["xn_done"], b * TPB + TPB)
                    for c in range(KD):
                        for j in range(TPB):
                            mm = pe.transpose(pT[:, c, j * P:(j + 1) * P], XN[:, j, c * P:(c + 1) * P], ident[:])
                    mm.then_inc(s["xt_raw"], 1)

                def body(b, par, more):
                    pe.wait_ge(s["xt_done"], b * KD + KD)
                    for j in range(TPB):
                        for k in range(KD):
                            mm = pe.matmul(pLt[:, j], XT[par][:, k, j * P:(j + 1) * P], G[:, k], start=(k == 0), stop=(k == KD - 1))
                    mm.then_inc(s["logits_done"], 1)
                    if shared:
                        pe.wait_ge(s["shared_added"], b + 1)
                    if more:
                        turn(b + 1)
                    if shared:
                        for f in range(FS):
                            if f >= 2:
                                pe.wait_ge(s["inner_done"], b * FS + (f - 1))
                            for w, out in zip(SW, (pG, pU)):
                                for k in range(KD):
                                    mm = pe.matmul(out[:, f % 2], w[:, k, f * P:(f + 1) * P], XT[par][:, k], start=(k == 0), stop=(k == KD - 1))
                            mm.then_inc(s["gate_up"], 1)
                    pe.wait_ge(s["onehot_done"], b * TPB + TPB)
                    for j in range(TPB + 1):
                        pe.matmul(pRt[:, j], ident[:], COUNT[:], start=True, stop=False)
                        for q in range(j):
                            mm = pe.matmul(pRt[:, j], ones[:], OH[:, q], start=False, stop=(j == TPB and q == TPB - 1))
                        if j < TPB:
                            mm = pe.matmul(pRt[:, j], tri[:], OH[:, j], start=False, stop=True)
                    mm.then_inc(s["rank_done"], 1)
                    if shared:
                        pe.wait_ge(s["inner_done"], b * FS + FS)
                        if more:
                            pe.wait_ge(s["xt_done"], b * KD + 2 * KD)
                        for j in range(TPB):
                            for f in range(FS):
                                mm = pe.matmul(pS[:, j], IN[:, f, j * P:(j + 1) * P], SD[:, f], start=(f == 0), stop=(f == FS - 1))
                        mm.then_inc(s["shared_done"], 1)

                turn(0)
                blocks(pe, body)
                pe.wait_ge(s["owner_done"], 1)
                pe.matmul(pL[0:1, 0:P], OWNER[:], ident[:], start=True, stop=True).then_inc(s["owner_turned"], 1)

            @block.scalar
            def _(act):
                def copy_xt(b, par):
                    if shared:
                        act.wait_ge(s["xn_done"], b * TPB + TPB)
                        nc.scalar.activation(XA[:, b * TPB:(b + 1) * TPB] if isinstance(b, int) else XA[:, bass.ds(b * TPB, TPB), :],
                                             XN[:], ACT.Copy).then_inc(s["xa_done"], 1)
                    act.wait_ge(s["xt_raw"], b + 1)
                    for c in range(KD):
                        nc.scalar.activation(XT[par][:, c], pT[:, c], ACT.Copy).then_inc(s["xt_done"], 1)

                def body(b, par, more):
                    if more:
                        copy_xt(b + 1, 1 - par)
                    if shared:
                        for f in range(FS):
                            act.wait_ge(s["gate_up"], b * FS + (f + 1))
                            nc.scalar.activation(SIL[:, f % 2], pG[:, f % 2], ACT.Silu).then_inc(s["silu_done"], 1)
                copy_xt(0, 0)
                blocks(act, body)
                act.wait_ge(s["dif_done"], NB)
                nc.scalar.activation(EX[:], DIF[:], ACT.Exp).then_inc(s["exp_done"], 1)

            @block.vector
            def _(dve):
                V = nc.vector
                pre = Chain(dve, s["pre"])

                def row_stats(a, b):
                    norm_stats(nc, pre, lambda j: X[:, a + j], stats[:, a:b], mv[:, a:b], rstd[:, a:b], tmp[:, a:b], 1e-5)
                dve.wait_ge(s["consts"], 1)
                pre.link(V.memset(COUNT[:], 0.0))
                of = lambda buf, t, n: buf[:, t:t + n] if isinstance(t, int) else buf[:, bass.ds(t, n)]

                def normalised(out, t):
                    return V.tensor_scalar(out, of(X, t, 1).rearrange("p o d -> p (o d)"), of(mv, t, 1)[:, :, 0], of(rstd, t, 1),
                                           ALU.subtract, ALU.mult)

                def normalise(b):
                    for j in range(TPB):
                        normalised(XN[:, j], b * TPB + j).then_inc(s["xn_done"], 1)

                PER = 1 + TPB * (K - 1) + TPB * K + 3
                def body(b, par, more):
                    ch = Chain(dve, s["steps"], b * PER)
                    all_ = lambda buf: of(buf, b * TPB, TPB)
                    if more:
                        dve.wait_ge(s["xt_raw"], b + 1)
                        if shared:
                            dve.wait_ge(s["xa_done"], b + 1)
                        normalise(b + 1)
                    dve.wait_ge(s["logits_done"], b + 1)
                    V.memset(tmp[:], 0.0)
                    for j in range(TPB):
                        mx = V.max(V8[:, j], pLt[:, j])
                    mx.then_inc(s["max_done"], 1)
                    dve.wait_ge(s["max_done"], 1)
                    dve.sem_clear(s["max_done"])
                    for j in range(TPB):
                        mx = V.max_index(I8[:, j], V8[:, j], pLt[:, j])
                    mx.then_inc(s["index_done"], 1)
                    if K == 2:
                        V.tensor_tensor(all_(DIF), V8[:, :, 1], V8[:, :, 0], ALU.subtract).then_inc(s["dif_done"], 1)
                    else:
                        V.tensor_scalar(all_(DIF), V8[:, :, 0], -1.0, None, ALU.mult).then_inc(s["dif_done"], 1)
                    dve.wait_ge(s["index_done"], b + 1)
                    ch.link(V.tensor_copy(IDX[:], I8[:, :, 0:K]))
                    for j in range(TPB):
                        out = OH[:, j] if K == 1 else OH0[:, j]
                        ins = V.tensor_scalar(out, iota[:], IDX[:, j, 0:1], None, ALU.is_equal)
                        if K == 1:
                            ins.then_inc(s["onehot_done"], 1)
                        else:
                            last = ch.mark(ins)
                    if K == 2:
                        ch.wait(last)
                        for j in range(TPB):
                            V.scalar_tensor_tensor(OH[:, j], iota[:], IDX[:, j, 1:2], OH0[:, j], ALU.is_equal, ALU.add)\
                                .then_inc(s["onehot_done"], 1)
                    if shared:
                        for f in range(FS):
                            dve.wait_ge(s["silu_done"], b * FS + (f + 1))
                            V.tensor_tensor(IN[:, f], SIL[:, f % 2], pU[:, f % 2], ALU.mult).then_inc(s["inner_done"], 1)
                    dve.wait_ge(s["rank_done"], b + 1)
                    for j in range(TPB):
                        for k in range(K):
                            last = ch.mark(V.scalar_tensor_tensor(JUNKS[j * K + k], iota[:], IDX[:, j, k:k + 1], pRt[:, j],
                                                                  ALU.is_equal, ALU.mult, accum_out=RK[:, j, k:k + 1]))
                    ch.mark(V.tensor_copy(all_(IDXA), IDX[:]))
                    last = ch.mark(V.tensor_copy(COUNT[:], pRt[:, TPB]))
                    ch.wait(last)
                    ch.mark(V.tensor_copy(all_(RKA), RK[:]))
                    if shared:
                        dve.wait_ge(s["shared_done"], b + 1)
                        V.tensor_tensor(all_(X), all_(X), pS, ALU.add).then_inc(s["shared_added"], 1)
                    assert ch.n == PER, (ch.n, PER)

                row_stats(0, TPB)
                normalise(0)
                row_stats(TPB, NT)
                blocks(dve, body)
                ch = Chain(dve, s["steps"], NB * PER)
                ch.link(V.tensor_scalar(NTILE[:], COUNT[:], 1.0 / P, 0.5 - 0.5 / P, ALU.mult, ALU.add))
                ch.link(V.tensor_scalar(NTILE[:], NTILE[:], ROUND, ROUND, ALU.add, ALU.subtract))
                ch.link(V.tensor_tensor_scan(END[:], NTILE[:], NTILE[:], 0.0, ALU.add, ALU.bypass))
                ch.link(V.tensor_tensor(START[:], END[:], NTILE[:], ALU.subtract))
                ch.mark(V.tensor_scalar(START[:], START[:], float(P), None, ALU.mult))
                ch.link(V.scalar_tensor_tensor(JUNKS[0], END[:], part[:], onef[:], ALU.is_le, ALU.mult, accum_out=OWNER[:]))
                V.tensor_scalar(OWNER[:], OWNER[:], float(E - 1), None, ALU.min).then_inc(s["owner_done"], 1)
                dve.wait_ge(s["exp_done"], 1)
                ch.link(V.tensor_scalar(DEN[:], EX[:], 1.0, None, ALU.add))
                ch.link(V.reciprocal(W0[:], DEN[:]))
                ch.mark(V.tensor_scalar(r.weight[:, :, 0], W0[:], 1.0, None, ALU.mult))
                if K == 2:
                    ch.mark(V.tensor_tensor(r.weight[:, :, 1], W0[:], EX[:], ALU.mult))
                n1 = ch.base + ch.n
                PER2 = TPB + TPB * K + 1

                def send(i, again):
                    for h in range(2):
                        ch = Chain(dve, s["steps"], (i * 2 + h) * PER2 + n1)
                        at = lambda buf: of(buf, (i * 2 + h) * TPB, TPB)
                        if again:
                            dve.wait_ge(sent[h], i * SENT)
                        for j in range(TPB):
                            t = (i * 2 + h) * TPB + j
                            if shared:
                                ch.mark(V.tensor_scalar(XS[h][:, j], of(XA, t, 1).rearrange("p o d -> p (o d)"), of(W0, t, 1), None, ALU.mult))
                            else:
                                ch.mark(normalised(XS[h][:, j], t))
                        for j in range(TPB):
                            for k in range(K):
                                expert = of(IDXA, (i * 2 + h) * TPB + j, 1)[:, :, k]
                                last = ch.mark(V.scalar_tensor_tensor(JUNKS[j * K + k], iota[:], expert, START[:],
                                                                      ALU.is_equal, ALU.mult, accum_out=BASE[:, j, k:k + 1]))
                        ch.wait(last)
                        ch.link(V.tensor_tensor(at(r.slot), BASE[:], at(RKA), ALU.add))
                        V.tensor_tensor(SL[h][:], BASE[:], at(RKA), ALU.add).then_inc(s["rows_ready"], 1)
                        dve.wait_ge(s["rows_ready"], i * 2 + (h + 1))

                send(0, False)
                with dve.Fori(1, NB // 2) as i:
                    send(i, True)
                dve.wait_ge(s["owner_turned"], 1)
                V.tensor_copy(r.expert[:], pL[0:1, 0:P]).then_inc(s["expert_ready"], 1)
        m_.clear()


def expert_tiles(nc, tag, r, w_gate, w_up, w_down, ident):
    BUF = 4
    FS = 512 // P
    N = r.tiles
    xs, ys = (a.rearrange("(t p) d -> t p d", p=P) for a in (r.xs, r.ys))
    assert N % BUF == 0
    with ExitStack() as stack:
        m_ = Memory(nc, stack, tag)
        ring = lambda name, shape, n=BUF: [m_.sb(f"{name}{b}", shape) for b in range(n)]
        WG, WU, WD = ring("wg", [P, KD, 512]), ring("wu", [P, KD, 512]), ring("wd", [P, FS, D])
        XR, Y = ring("xr", [P, D]), ring("y", [P, D])
        XT, SIL, IN = ring("xt", [P, KD, P], 2), ring("sil", [P, FS, P], 2), ring("in", [P, FS, P], 2)
        pT, pG, pU, pY = ([m_.ps(f"{n}{b}", [P, 512]) for b in range(2)] for n in ("pT", "pG", "pU", "pY"))
        s = {n: m_.sem(n) for n in ("xt_raw", "xt_done", "gate_done", "up_done", "silu_done", "inner_done", "down_done", "y_done")}
        x_loaded, w_loaded, stored = ([m_.sem(f"{n}{b}") for b in range(BUF)] for n in ("x_loaded", "w_loaded", "stored"))

        class Tile:

            def __init__(self, q, b):
                self.q, self.b, self.two = q, b, b % 2
                self.t = q * BUF + b

            def __add__(self, d):
                return Tile(self.q + (self.b + d) // BUF, (self.b + d) % BUF)

            def at_least(self, n):
                return not isinstance(self.q, int) or self.t >= n

        def steps(engine, body):
            for b in range(BUF):
                body(Tile(0, b), b == 0, False)
            with engine.Fori(1, N // BUF - 1) as q:
                for b in range(BUF):
                    body(Tile(q, b), False, False)
            for b in range(BUF):
                body(Tile(N // BUF - 1, b), False, b == BUF - 1)

        with nc.Block() as block:

            @block.sync
            def _(sp):
                def load(t, first, last):
                    if t.at_least(BUF):
                        sp.wait_ge(s["down_done"], t.t - (BUF - 1))
                    sp.dma_start(XR[t.b][:], xs[bass.ds(t.t, 1)].rearrange("t p d -> (t p) d")).then_inc(x_loaded[t.b], 16)
                    e = sp.value_load(r.expert[0:1, bass.ds(t.t, 1)], min_val=0, max_val=r.E - 1)
                    for dst, src in ((WG, w_gate), (WU, w_up), (WD, w_down)):
                        sp.dma_start(dst[t.b][:], src[bass.ds(e, 1)].rearrange("e (k p) n -> p (e k) n", p=P))\
                            .then_inc(w_loaded[t.b], 16)
                steps(sp, load)

            @block.tensor
            def _(pe):
                def turn(t):
                    pe.wait_ge(x_loaded[t.b], t.q * 16 + 16)
                    for k in range(KD):
                        mm = pe.transpose(pT[t.two][:, k * P:(k + 1) * P], XR[t.b][:, k * P:(k + 1) * P], ident[:])
                    mm.then_inc(s["xt_raw"], 1)

                def up(t):
                    pe.wait_ge(s["xt_done"], t.t + 1)
                    pe.wait_ge(w_loaded[t.b], t.q * 48 + 48)
                    for w, out, done in ((WG, pG, "gate_done"), (WU, pU, "up_done")):
                        for f in range(FS):
                            for k in range(KD):
                                mm = pe.matmul(out[t.two][:, f * P:(f + 1) * P], w[t.b][:, k, f * P:(f + 1) * P],
                                               XT[t.two][:, k], start=(k == 0), stop=(k == KD - 1))
                        mm.then_inc(s[done], 1)

                def down(t):
                    pe.wait_ge(s["inner_done"], t.t + 1)
                    if t.at_least(2):
                        pe.wait_ge(s["y_done"], t.t - 1)
                    for f in range(FS):
                        mm = pe.matmul(pY[t.two][:, 0:D], IN[t.two][:, f], WD[t.b][:, f], start=(f == 0), stop=(f == FS - 1))
                    mm.then_inc(s["down_done"], 1)

                def step(t, first, last):
                    if not last:
                        turn(t + 1)
                    up(t)
                    if not first:
                        down(t + -1)
                turn(Tile(0, 0))
                steps(pe, step)
                down(Tile(N // BUF - 1, BUF - 1))

            @block.scalar
            def _(act):
                def copy_xt(t):
                    act.wait_ge(s["xt_raw"], t.t + 1)
                    nc.scalar.activation(XT[t.two][:].rearrange("p k t -> p (k t)"), pT[t.two][:, 0:D], ACT.Copy)\
                        .then_inc(s["xt_done"], 1)

                def store(t):
                    act.wait_ge(s["y_done"], t.t + 1)
                    act.dma_start(ys[bass.ds(t.t, 1)].rearrange("t p d -> (t p) d"), Y[t.b][:]).then_inc(stored[t.b], 16)

                def step(t, first, last):
                    if not last:
                        copy_xt(t + 1)
                    act.wait_ge(s["gate_done"], t.t + 1)
                    if t.at_least(2):
                        act.wait_ge(s["inner_done"], t.t - 1)
                    nc.scalar.activation(SIL[t.two][:].rearrange("p f t -> p (f t)"), pG[t.two][:], ACT.Silu)\
                        .then_inc(s["silu_done"], 1)
                    if t.at_least(2):
                        store(t + -2)
                copy_xt(Tile(0, 0))
                steps(act, step)
                store(Tile(N // BUF - 1, BUF - 2))
                store(Tile(N // BUF - 1, BUF - 1))
                for b in range(BUF):
                    act.wait_ge(stored[b], 16 * (N // BUF))

            @block.vector
            def _(dve):
                def copy_y(t):
                    dve.wait_ge(s["down_done"], t.t + 1)
                    if t.at_least(BUF):
                        dve.wait_ge(stored[t.b], t.q * 16)
                    nc.vector.tensor_scalar(Y[t.b][:], pY[t.two][:, 0:D], 1.0, None, ALU.mult).then_inc(s["y_done"], 1)

                def step(t, first, last):
                    dve.wait_ge(s["silu_done"], t.t + 1)
                    dve.wait_ge(s["up_done"], t.t + 1)
                    if t.at_least(2):
                        dve.wait_ge(s["down_done"], t.t - 1)
                    nc.vector.tensor_tensor(IN[t.two][:].rearrange("p f t -> p (f t)"), SIL[t.two][:], pU[t.two][:], ALU.mult)\
                        .then_inc(s["inner_done"], 1)
                    if not first:
                        copy_y(t + -1)
                steps(dve, step)
                copy_y(Tile(N // BUF - 1, BUF - 1))
        m_.clear()


def combine(nc, tag, X, r, out=None):
    with ExitStack() as stack:
        m_ = Memory(nc, stack, tag)
        Y = [[m_.sb(f"y{h}{k}", [P, TPB, D]) for k in range(r.K)] for h in range(2)]
        SL = [m_.sb(f"sl{h}", [P, TPB * r.K], I32) for h in range(2)]
        copied = m_.sem("copied")
        fetched, added = ([m_.sem(f"{n}{h}") for h in range(2)] for n in ("fetched", "added"))
        stored = m_.sem("stored")
        ONE = 16 * TPB * r.K
        with nc.Block() as block:

            @block.gpsimd
            def _(pool):
                for h in range(2):
                    pool.sem_inc(added[h], TPB)
                with pool.Fori(0, NB // 2) as i:
                    for h in range(2):
                        pool.wait_ge(added[h], i * TPB + TPB)
                        pool.tensor_copy(SL[h][:], r.slot[:, bass.ds((i * 2 + h) * TPB, TPB), :].rearrange("p t k -> p (t k)"))\
                            .then_inc(copied, 1)
                        pool.wait_ge(copied, 1)
                        pool.sem_clear(copied)
                        for j in range(TPB):
                            for k in range(r.K):
                                n = j * r.K + k
                                pool.indirect_dma_start(Y[h][k][:, j], None, r.ys,
                                                        bass.IndirectOffsetOnAxis(ap=SL[h][:, n:n + 1], axis=0)).then_inc(fetched[h], 16)

            @block.vector
            def _(dve):
                V = nc.vector
                steps = m_.sem("steps")
                with dve.Fori(0, NB // 2) as i:
                    for h in range(2):
                        dve.wait_ge(fetched[h], i * ONE + ONE)
                        for j in range(TPB):
                            t = (i * 2 + h) * TPB + j
                            x = X[:, bass.ds(t, 1), :].rearrange("p o d -> p (o d)")
                            if r.K == 1:
                                V.tensor_tensor(x, x, Y[h][0][:, j], ALU.add).then_inc(added[h], 1)
                            else:
                                V.scalar_tensor_tensor(x, Y[h][0][:, j], r.weight[:, bass.ds(t, 1), 0], x, ALU.mult, ALU.add)\
                                    .then_inc(steps, 1)
                                dve.wait_ge(steps, i * (2 * TPB) + (h * TPB + j + 1))
                                V.scalar_tensor_tensor(x, Y[h][1][:, j], r.weight[:, bass.ds(t, 1), 1], x, ALU.mult, ALU.add)\
                                    .then_inc(added[h], 1)

            if out is not None:

                @block.sync
                def _(sp):
                    o = out.rearrange("(b t p) d -> b p t d", p=P, t=TPB)
                    with sp.Fori(0, NB // 2) as i:
                        for h in range(2):
                            sp.wait_ge(added[h], i * TPB + 2 * TPB)
                            sp.dma_start(o[bass.ds(i * 2 + h, 1)].rearrange("b p t d -> (b p) t d"),
                                         X[:, bass.ds((i * 2 + h) * TPB, TPB), :]).then_inc(stored, 16)
                    sp.wait_ge(stored, 16 * NB)
        m_.clear()


def state_space(nc, g, X, r, ident):
    DI = 2 * D
    CI = DI // P
    N = 16
    TAPS = 4
    RING = 4
    PREP = CI * (TAPS - 1) + 3 + 7
    with ExitStack() as stack:
        m_ = Memory(nc, stack, "ss")
        WI, WO = m_.sb("wi", [P, KD, 2 * DI]), m_.sb("wo", [P, CI, D])
        WX, WT = m_.sb("wx", [P, CI, P]), m_.sb("wt", [N, DI])
        norm_w = m_.sb("norm_w", [P, KD])
        conv_w, conv_b, dt_b, skip = m_.sb("conv_w", [P, CI, TAPS]), m_.sb("conv_b", [P, CI]), m_.sb("dt_b", [P, CI]), m_.sb("skip", [P, CI])
        DECAY = m_.sb("decay", [P, CI, N])
        SEL = m_.sb("sel", [P, 2 * N], BF16)
        keep = m_.sb("keep", [P, NB + 1])
        stats, mv = m_.sb("stats", [P, NT, 6]), m_.sb("mv", [P, NT, 2])
        rstd, tmp, var, rms = (m_.sb(n, [P, NT]) for n in ("rstd", "tmp", "var", "rms"))
        HN = m_.sb("hn", [P, TPB, D])
        XR = m_.sb("xr", [P, CI, TAPS - 1 + BT])
        two = lambda name, shape, dt=F32: [m_.sb(f"{name}{b}", shape, dt) for b in range(2)]
        HT, XC, DT, DTX, BC = two("ht", [P, KD, BT]), two("xc", [P, CI, BT]), two("dt", [P, CI, BT]), two("dtx", [P, CI, BT]), two("bc", [P, BT], BF16)
        ZS, DBU, LN1 = (m_.sb(n, [P, CI, BT]) for n in ("zs", "dbu", "ln1"))
        DA, CS = two("da", [P, CI, BT]), two("cs", [P, BT])
        H = [m_.sb(f"h{b}", [P, CI, BT]) for b in range(RING)]
        Y = [[H[2 * h + k][:, 0:2].rearrange("p a (t d) -> p (a t) d", d=D) for k in range(2)] for h in range(2)]
        SL = [m_.sb(f"sl{h}", [P, TPB * r.K], I32) for h in range(2)]
        DR, REST, BC2 = m_.sb("dr", [N, BT]), m_.sb("rest", [P, 2, BT]), m_.sb("bc2", [P, BT], BF16)
        c_h = m_.sb("c_h", [P, N, CI])
        y, bB, bC = m_.ps("y", [P, CI, BT]), m_.ps("bB", [P, 2, BT]), m_.ps("bC", [P, BT])
        Q = m_.ps("q", [P, BT])
        s = {n: m_.sem(n) for n in (
            "loaded", "sel_steps", "decay_done", "pre", "steps", "h_done", "t_raw", "ht_done", "x_raw", "x_done", "z_raw", "z_done",
            "conv_done", "xc_done", "zs_done", "xp_raw", "bc1_done", "bc_done", "dt_raw", "u_done", "exp_done", "ln_done",
            "dt_done", "dtx_done", "spread", "c_copied", "da_done", "dbu_done", "scan_steps", "scanned", "pr_done", "summed",
            "skip_done", "yz_done", "out_raw", "out_done", "copied", "half_added")}
        fetched, added = ([m_.sem(f"{n}{h}") for h in range(2)] for n in ("fetched", "added"))

        def wait(engine, name, value):
            if not isinstance(value, int) or value > 0:
                engine.wait_ge(s[name], value)

        def blocks(engine, body):
            body(0, 0, True, False)
            with engine.Fori(0, NB // 2 - 1) as q:
                body(q * 2 + 1, 1, True, True)
                body(q * 2 + 2, 0, True, True)
            body(NB - 1, 1, False, True)

        with nc.Block() as block:

            @block.sync
            def _(sp):
                for dst, src in ((WI, g["in_w"]), (WO, g["out_w"]), (WX, g["xp_w"])):
                    sp.dma_start(dst[:], src.rearrange("(k p) n -> p k n", p=P)).then_inc(s["loaded"], 16)
                sp.dma_start(WT[:], g["dt_w"]).then_inc(s["loaded"], 16)
                for dst, name in ((DECAY, "A_log"), (conv_w, "conv_w")):
                    sp.dma_start(dst[:], g[name].rearrange("(c p) n -> p c n", p=P)).then_inc(s["loaded"], 16)
                for dst, name in ((norm_w, "norm_weight"), (conv_b, "conv_b"), (dt_b, "dt_b"), (skip, "skip")):
                    sp.dma_start(dst[:], g[name].rearrange("(c p) -> p c", p=P), allow_slow_non_contiguous=True)\
                        .then_inc(s["loaded"], 16)
            LOADED = 16 * 10

            @block.gpsimd
            def _(pool):
                pool.memset(SEL[:], 0.0).then_inc(s["sel_steps"], 1)
                for part in range(1, 4):
                    pool.wait_ge(s["sel_steps"], part)
                    pool.affine_select(out=SEL[:], in_=SEL[:], compare_op=ALU.not_equal, fill=1.0, base=-32 * part,
                                       pattern=[[-1, 2 * N]], channel_multiplier=1).then_inc(s["sel_steps"], 1)
                for h in range(2):
                    pool.sem_inc(added[h], TPB)
                with pool.Fori(0, NB // 2) as i:
                    for h in range(2):
                        pool.wait_ge(added[h], i * TPB + TPB)
                        pool.tensor_copy(SL[h][:], r.slot[:, bass.ds((i * 2 + h) * TPB, TPB), :].rearrange("p t k -> p (t k)"))\
                            .then_inc(s["copied"], 1)
                        pool.wait_ge(s["copied"], 1)
                        pool.sem_clear(s["copied"])
                        for j in range(TPB):
                            for k in range(r.K):
                                n = j * r.K + k
                                pool.indirect_dma_start(Y[h][k][:, j], None, r.ys,
                                                        bass.IndirectOffsetOnAxis(ap=SL[h][:, n:n + 1], axis=0)).then_inc(fetched[h], 16)

                def times_x(b, par):
                    wait(pool, "dt_done", b + 1)
                    pool.tensor_tensor(DTX[par][:], DT[par][:], XC[par][:], ALU.mult).then_inc(s["dtx_done"], 1)

                def gate(b, par):
                    wait(pool, "zs_done", b + 1)
                    for c in range(CI):
                        wait(pool, "skip_done", b * CI + (c + 1))
                        pool.tensor_tensor(DTX[par][:, c], DTX[par][:, c], ZS[:, c], ALU.mult).then_inc(s["yz_done"], 1)

                def main(b, par, prep, tail):
                    for n in range(N):
                        wait(pool, "scanned", b * N + (n + 1))
                        wait(pool, "c_copied", b * N + (n + 1))
                        h = H[n % RING]
                        pool.tensor_tensor(h[:], h[:], CS[n % 2][:].unsqueeze(1).to_broadcast([P, CI, BT]), ALU.mult)\
                            .then_inc(s["pr_done"], 1)
                        if n == 2 and tail:
                            gate(b - 1, 1 - par)
                        if n == 14 and prep:
                            times_x(b + 1, 1 - par)
                times_x(0, 0)
                blocks(pool, main)
                gate(NB - 1, 1)

            @block.tensor
            def _(pe):
                pe.wait_ge(s["loaded"], LOADED)
                pe.wait_ge(s["sel_steps"], 4)

                def project(out, w, col, rhs, chunks):
                    for k in range(chunks):
                        mm = pe.matmul(out, w[:, k, col:col + P], rhs[:, k], start=(k == 0), stop=(k == chunks - 1))
                    return mm

                def turn(b, par, c):
                    wait(pe, "h_done", b * TPB + TPB)
                    wait(pe, "z_done", (b - 1) * CI) if c == 0 else wait(pe, "ht_done", b * KD + c)
                    for j in range(TPB):
                        mm = pe.transpose(Q[:, j * P:(j + 1) * P], HN[:, j, c * P:(c + 1) * P], ident[:])
                    mm.then_inc(s["t_raw"], 1)

                def x_part(b, par, c):
                    wait(pe, "ht_done", b * KD + KD) if c == 0 else wait(pe, "x_done", b * CI + c)
                    project(Q[:], WI, c * P, HT[par], KD).then_inc(s["x_raw"], 1)

                def z_part(b, par, c):
                    wait(pe, "z_done", b * CI + c)
                    project(Q[:], WI, DI + c * P, HT[par], KD).then_inc(s["z_raw"], 1)

                def x_proj(b, par):
                    wait(pe, "xc_done", b + 1)
                    project(Q[:], WX, 0, XC[par], CI).then_inc(s["xp_raw"], 1)

                def dt_proj(b, c):
                    wait(pe, "bc_done", b + 1) if c == 0 else wait(pe, "u_done", b * CI + c)
                    pe.matmul(Q[:], WT[:, c * P:(c + 1) * P], DR[:], start=True, stop=True).then_inc(s["dt_raw"], 1)

                def spread(b, par, n):
                    wait(pe, "bc_done", b + 1)
                    wait(pe, "dbu_done", b * N + (n - 1))
                    wait(pe, "c_copied", b * N + n)
                    pe.matmul(bB[:, n % 2], SEL[:, n:n + 1].to_broadcast([P, P]), BC[par][:], start=True, stop=True)
                    pe.matmul(bC[:], SEL[:, N + n:N + n + 1].to_broadcast([P, P]), BC[par][:], start=True, stop=True)\
                        .then_inc(s["spread"], 1)

                def add_up(b, n):
                    wait(pe, "pr_done", b * N + (n + 1))
                    if n == 0:
                        wait(pe, "skip_done", b * CI)
                    for c in range(CI):
                        mm = pe.matmul(y[:, c], ident[:], H[n % RING][:, c], start=(n == 0), stop=(n == N - 1))
                    mm.then_inc(s["summed"], 1)

                def out_part(b, par, half):
                    wait(pe, "yz_done", b * CI + CI)
                    for j in range(2):
                        t = (half * 2 + j) * P
                        for c in range(CI):
                            mm = pe.matmul(Q[:, j * D:(j + 1) * D], DTX[par][:, c, t:t + P], WO[:, c], start=(c == 0), stop=(c == CI - 1))
                    mm.then_inc(s["out_raw"], 1)

                def main(b, par, prep, tail):
                    def piece(n):
                        if prep and n == 1:
                            turn(b + 1, 1 - par, 0)
                            turn(b + 1, 1 - par, 1)
                        if prep and n in (2, 3, 4, 5):
                            x_part(b + 1, 1 - par, n - 2)
                        if tail and n == 6:
                            wait(pe, "x_done", (b + 2) * CI) if prep else wait(pe, "z_done", b * CI)
                            out_part(b - 1, 1 - par, 0)
                        if tail and n == 7:
                            wait(pe, "out_done", b * 2 - 1)
                            out_part(b - 1, 1 - par, 1)
                        if prep and n == 8:
                            wait(pe, "out_done", b * 2) if tail else wait(pe, "x_done", (b + 2) * CI)
                            x_proj(b + 1, 1 - par)
                        if prep and n in (10, 11):
                            dt_proj(b + 1, 2 * n - 20)
                            dt_proj(b + 1, 2 * n - 19)
                        if n in (12, 13, 14, 15):
                            if n == 12:
                                wait(pe, "u_done", (b + 2) * CI) if prep else wait(pe, "out_done", b * 2)
                            z_part(b, par, n - 12)

                    for n in range(N):
                        if n < N - 1:
                            spread(b, par, n + 1)
                        elif prep:
                            spread(b + 1, 1 - par, 0)
                        piece(n)
                        if n >= 2:
                            add_up(b, n - 2)
                        elif tail:
                            add_up(b - 1, n + N - 2)

                turn(0, 0, 0)
                turn(0, 0, 1)
                for c in range(CI):
                    x_part(0, 0, c)
                wait(pe, "x_done", CI)
                x_proj(0, 0)
                for c in range(CI):
                    dt_proj(0, c)
                spread(0, 0, 0)
                blocks(pe, main)
                add_up(NB - 1, N - 2)
                add_up(NB - 1, N - 1)
                wait(pe, "z_done", NB * CI)
                out_part(NB - 1, 1, 0)
                wait(pe, "out_done", NB * 2 - 1)
                out_part(NB - 1, 1, 1)

            @block.scalar
            def _(act):
                A_ = nc.scalar.activation
                act.wait_ge(s["loaded"], LOADED)
                A_(DECAY[:], DECAY[:], ACT.Exp).then_inc(s["decay_done"], 1)
                act.wait_ge(s["decay_done"], 2)

                def copy_ht(b, par, c):
                    wait(act, "t_raw", b * KD + (c + 1))
                    A_(HT[par][:, c], Q[:], ACT.Copy, scale=norm_w[:, c:c + 1]).then_inc(s["ht_done"], 1)

                def copy_x(b, par, c):
                    wait(act, "conv_done", b * CI)
                    wait(act, "x_raw", b * CI + (c + 1))
                    wait(act, "skip_done", (b - 1) * CI)
                    A_(XC[par][:, c], Q[:], ACT.Identity, scale=conv_w[:, c, TAPS - 1:], bias=conv_b[:, c:c + 1])
                    A_(XR[:, c, TAPS - 1:], Q[:], ACT.Copy).then_inc(s["x_done"], 1)

                def copy_z(b, c):
                    wait(act, "yz_done", b * CI)
                    wait(act, "z_raw", b * CI + (c + 1))
                    A_(ZS[:, c], Q[:], ACT.Copy).then_inc(s["z_done"], 1)

                def silu_x(b, par):
                    wait(act, "conv_done", b * CI + CI)
                    A_(XC[par][:], XC[par][:], ACT.Silu).then_inc(s["xc_done"], 1)

                def copy_bc(b, par):
                    wait(act, "xp_raw", b + 1)
                    A_(BC[par][:], Q[:], ACT.Copy)
                    A_(DR[:], Q[0:N], ACT.Copy).then_inc(s["bc1_done"], 1)

                def copy_dt(b, par, c):
                    wait(act, "out_raw", b * 2 - 2)
                    wait(act, "dt_raw", b * CI + (c + 1))
                    A_(DTX[par][:, c], Q[:], ACT.Abs, bias=dt_b[:, c:c + 1])
                    A_(DT[par][:, c], Q[:], ACT.Identity, bias=dt_b[:, c:c + 1]).then_inc(s["u_done"], 1)

                def exp(b, par):
                    wait(act, "u_done", b * CI + CI)
                    A_(DTX[par][:], DTX[par][:], ACT.Exp, scale=-1.0).then_inc(s["exp_done"], 1)

                def log(b, par):
                    wait(act, "exp_done", b + 1)
                    A_(LN1[:], DTX[par][:], ACT.Ln, bias=1.0).then_inc(s["ln_done"], 1)

                def main(b, par, prep, tail):
                    wait(act, "dt_done", b + 1)
                    for n in range(N):
                        wait(act, "scanned", b * N + (n - 1))
                        for c in range(CI):
                            ins = A_(DA[n % 2][:, c], DT[par][:, c], ACT.Exp, scale=DECAY[:, c, n:n + 1])
                        ins.then_inc(s["da_done"], 1)
                        wait(act, "spread", b * N + (n + 1))
                        wait(act, "pr_done", b * N + (n - 1))
                        A_(CS[n % 2][:], bC[:], ACT.Copy).then_inc(s["c_copied"], 1)
                        if prep and n == 2:
                            copy_ht(b + 1, 1 - par, 0)
                            copy_ht(b + 1, 1 - par, 1)
                        if prep and n in (3, 4, 5, 6):
                            copy_x(b + 1, 1 - par, n - 3)
                        if prep and n == 8:
                            silu_x(b + 1, 1 - par)
                        if prep and n == 9:
                            copy_bc(b + 1, 1 - par)
                        if prep and n in (11, 12):
                            copy_dt(b + 1, 1 - par, 2 * n - 22)
                            copy_dt(b + 1, 1 - par, 2 * n - 21)
                        if prep and n == 12:
                            exp(b + 1, 1 - par)
                        if prep and n == 13:
                            log(b + 1, 1 - par)
                        if n in (13, 14, 15):
                            copy_z(b, n - 13)
                    copy_z(b, 3)
                    wait(act, "z_done", b * CI + CI)
                    A_(ZS[:], ZS[:], ACT.Silu).then_inc(s["zs_done"], 1)

                copy_ht(0, 0, 0)
                copy_ht(0, 0, 1)
                for c in range(CI):
                    copy_x(0, 0, c)
                silu_x(0, 0)
                copy_bc(0, 0)
                for c in range(CI):
                    copy_dt(0, 0, c)
                exp(0, 0)
                log(0, 0)
                blocks(act, main)

            @block.vector
            def _(dve):
                V = nc.vector
                pre = Chain(dve, s["pre"])
                pre.link(V.memset(keep[:], 1.0))
                pre.link(V.memset(keep[:, SB:SB + 1], 0.0))
                pre.mark(V.memset(c_h[:], 0.0))
                pre.link(V.memset(XR[:], 0.0))
                dve.wait_ge(s["loaded"], LOADED)
                dve.wait_ge(s["decay_done"], 1)
                V.tensor_scalar(DECAY[:], DECAY[:], -1.0, None, ALU.mult).then_inc(s["decay_done"], 1)
                ends_here = lambda b: keep[:, bass.ds(b + 1, 1)] if not isinstance(b, int) else keep[:, b + 1:b + 2]
                tiles = lambda t, n=1: X[:, bass.ds(t, n), :] if not isinstance(t, int) else X[:, t:t + n, :]

                def add_experts(i):
                    for h in range(2):
                        dve.wait_ge(fetched[h], (i + 1) * 16 * TPB * r.K)
                        for j in range(TPB):
                            t = (i * 2 + h) * TPB + j
                            V.scalar_tensor_tensor(X[:, t], Y[h][0][:, j], r.weight[:, t, 0:1], X[:, t], ALU.mult, ALU.add)\
                                .then_inc(s["half_added"], 1)
                        for j in range(TPB):
                            t = (i * 2 + h) * TPB + j
                            dve.wait_ge(s["half_added"], t + 1)
                            V.scalar_tensor_tensor(X[:, t], Y[h][1][:, j], r.weight[:, t, 1:2], X[:, t], ALU.mult, ALU.add)\
                                .then_inc(added[h], 1)

                def row_stats(i, n):
                    a, b = i * 2 * TPB, (i + n) * 2 * TPB
                    for h in range(2):
                        dve.wait_ge(added[h], TPB * (i + n + 1))
                    v, d, q, t = var[:, a:b], rstd[:, a:b], rms[:, a:b], tmp[:, a:b]
                    norm_stats(nc, pre, lambda j: X[:, a + j], stats[:, a:b], mv[:, a:b], d, t, 1e-5, var=v)
                    pre.link(V.tensor_tensor(v, v, d, ALU.mult))
                    pre.link(V.tensor_tensor(v, v, d, ALU.mult))
                    rsqrt(nc, pre, q, v, t)
                    pre.link(V.tensor_tensor(q, q, v, ALU.mult))
                    pre.link(V.tensor_scalar(q, q, 1e-5, None, ALU.add))
                    pre.link(V.reciprocal(t, q))
                    pre.link(V.tensor_tensor(d, d, t, ALU.mult))

                def normalise(b):
                    wait(dve, "t_raw", b * KD)
                    for j in range(TPB):
                        t = b * TPB + j
                        at = (lambda buf: buf[:, t:t + 1]) if isinstance(t, int) else (lambda buf: buf[:, bass.ds(t, 1)])
                        V.tensor_scalar(HN[:, j], tiles(t).rearrange("p o d -> p (o d)"), at(mv)[:, :, 0], at(rstd),
                                        ALU.subtract, ALU.mult).then_inc(s["h_done"], 1)

                def convolve(b, par, c, n0):
                    ch = Chain(dve, s["steps"], b * PREP + n0)
                    wait(dve, "x_done", b * CI + (c + 1))
                    xc = XC[par][:, c]
                    for t in range(TAPS - 1):
                        ch.link(V.scalar_tensor_tensor(xc, XR[:, c, t:t + BT], conv_w[:, c, t:t + 1], xc, ALU.mult, ALU.add))
                    V.tensor_scalar(XR[:, c, 0:TAPS - 1], XR[:, c, BT:], ends_here(b), None, ALU.mult).then_inc(s["conv_done"], 1)
                    return n0 + ch.n

                def split_bc(b, par, n0):
                    ch = Chain(dve, s["steps"], b * PREP + n0)
                    wait(dve, "bc1_done", b + 1)
                    R1 = REST[:, 0]
                    ch.link(V.tensor_tensor(R1, Q[:], BC[par][:], ALU.subtract))
                    ch.link(V.tensor_scalar(BC2[:], R1, 1.0, None, ALU.mult))
                    ch.mark(V.tensor_scalar(BC[par][2 * 32:3 * 32], BC2[2 * 32:3 * 32], 1.0, None, ALU.mult))
                    V.tensor_tensor(BC[par][3 * 32:], REST[3 * 32:, 0], BC2[3 * 32:], ALU.subtract).then_inc(s["bc_done"], 1)
                    return n0 + ch.n

                def time_steps(b, par, n0):
                    ch = Chain(dve, s["steps"], b * PREP + n0)
                    wait(dve, "bc_done", b + 1)
                    wait(dve, "ln_done", b + 1)
                    for half in range(2):
                        e, u, ln = (buf[:, 2 * half:2 * half + 2] for buf in (DTX[par], DT[par], LN1))
                        ch.link(V.tensor_scalar(REST[:], e, 1.0, 1.0, ALU.add, ALU.subtract))
                        ch.mark(V.tensor_tensor(e, e, REST[:], ALU.subtract))
                        ch.link(V.scalar_tensor_tensor(u, u, 0.0, ln, ALU.max, ALU.add))
                        ins = V.tensor_tensor(u, u, e, ALU.add)
                        if half == 0:
                            ch.link(ins)
                    ins.then_inc(s["dt_done"], 1)
                    return n0 + ch.n

                def add_skip(b, par):
                    wait(dve, "summed", b * N + N)
                    for c in range(CI):
                        V.scalar_tensor_tensor(DTX[par][:, c], XC[par][:, c], skip[:, c:c + 1], y[:, c], ALU.mult, ALU.add)\
                            .then_inc(s["skip_done"], 1)

                def add_out(b, half):
                    wait(dve, "out_raw", b * 2 + (half + 1))
                    x = tiles(b * TPB + 2 * half, 2)
                    V.tensor_tensor(x, x, Q[:].rearrange("p (t d) -> p t d", d=D), ALU.add).then_inc(s["out_done"], 1)

                def main(b, par, prep, tail):
                    wait(dve, "dtx_done", b + 1)
                    wait(dve, "scanned", b * N)
                    for n in range(N):
                        wait(dve, "spread", b * N + (n + 1))
                        V.tensor_tensor(DBU[:], DTX[par][:], bB[:, n % 2].unsqueeze(1).to_broadcast([P, CI, BT]), ALU.mult)\
                            .then_inc(s["dbu_done"], 1)
                        wait(dve, "dbu_done", b * N + (n + 1))
                        wait(dve, "da_done", b * N + (n + 1))
                        wait(dve, "summed", b * N + (n + 1 - RING))
                        h = H[n % RING]
                        for c in range(CI):
                            ins = V.tensor_tensor_scan(h[:, c], DA[n % 2][:, c], DBU[:, c], c_h[:, n, c:c + 1], ALU.mult, ALU.add)
                        ins.then_inc(s["scan_steps"], 1)
                        wait(dve, "scan_steps", b * N + (n + 1))
                        V.tensor_scalar(c_h[:, n, :], h[:, :, BT - 1], ends_here(b), None, ALU.mult).then_inc(s["scanned"], 1)
                        if prep and n == 0:
                            normalise(b + 1)
                            n1 = 0
                        if tail and n == 2:
                            add_skip(b - 1, 1 - par)
                        if prep and n in (3, 4, 5, 6):
                            n1 = convolve(b + 1, 1 - par, n - 3, n1)
                        if tail and n == 6:
                            add_out(b - 1, 0)
                        if tail and n == 7:
                            add_out(b - 1, 1)
                        if prep and n == 9:
                            n1 = split_bc(b + 1, 1 - par, n1)
                        if prep and n == 14:
                            n1 = time_steps(b + 1, 1 - par, n1)
                    assert not prep or n1 == PREP, n1

                add_experts(0)
                row_stats(0, 1)
                normalise(0)
                add_experts(1)
                n1 = 0
                for c in range(CI):
                    n1 = convolve(0, 0, c, n1)
                add_experts(2)
                n1 = split_bc(0, 0, n1)
                add_experts(3)
                row_stats(1, NB // 2 - 1)
                time_steps(0, 0, n1)
                blocks(dve, main)
                add_skip(NB - 1, 1)
                add_out(NB - 1, 0)
                add_out(NB - 1, 1)
        m_.clear()



def build(nc, g, out):
    with ExitStack() as stack:
        m_ = Memory(nc, stack, "all")
        ident = m_.sb("ident", [P, P])
        X = m_.sb("x", [P, NT, D])
        r0, r1 = Routing(nc, stack, "moe0", 64, 2), Routing(nc, stack, "moe1", 16, 1)
        with ExitStack() as inner:
            m_ = Memory(nc, inner, "attn")
            YS, SG = m_.sb("ys", [P, KD, T]), m_.sb("sg", [P, KD, T])
            SUMS = m_.sb("sums", [P, NB * KD * 4])
            gate_loop(nc, g["x"], g["w_proj"], X, YS, SG, SUMS, ident, (r0.xs, r1.xs))
            gate_ffn(nc, g, X, YS, SG, SUMS, ident)
        route(nc, "route0", X, g["router0"], r0, ident)
        expert_tiles(nc, "experts0", r0, g["w0"], g["w1"], g["wo"], ident)
        state_space(nc, g, X, r0, ident)
        route(nc, "route1", X, g["router1"], r1, ident, shared=(g["sh_gate"], g["sh_up"], g["sh_down"]))
        half = g["gate_up"].shape[2] // 2
        expert_tiles(nc, "experts1", r1, g["gate_up"][:, :, 0:half], g["gate_up"][:, :, half:], g["down"], ident)
        combine(nc, "combine1", X, r1, out=out)


def mamba_layout(inputs):
    import numpy as np
    L = lambda n: np.asarray(inputs["L1_attn_" + n])
    w = L("x_proj_w")
    return {"in_w": L("in_proj_w").T, "out_w": L("out_proj_w").T, "dt_w": L("dt_proj_w").T,
            "xp_w": np.concatenate([w[:16], w[:16], w[16:], w[16:], w[16:]]).T,
            "A_log": L("A_log"), "conv_w": L("conv_w"), "norm_weight": L("norm_weight"), "conv_b": L("conv_b"),
            "dt_b": L("dt_proj_b"), "skip": L("D")}


def layout(inputs):
    import numpy as np
    g = mamba_layout(inputs)
    A = lambda n: np.asarray(inputs["L0_attn_" + n])
    F = lambda n: np.asarray(inputs["L1_ffn_" + n])
    g["x"] = A("x").reshape(T, D)
    g["w_proj"] = np.concatenate([A("Wa"), A("Wk"), A("Wv"), A("Wq"), A("Wg")], axis=1)
    for ours, theirs in (("Wo", "Wo"), ("gn_scale", "gn_scale"), ("gn_bias", "gn_bias"), ("W1", "W1"), ("W2", "W2"),
                         ("b1", "b1"), ("b2", "b2"), ("ln1s", "ln1_scale"), ("ln1b", "ln1_bias"),
                         ("ln2s", "ln2_scale"), ("ln2b", "ln2_bias")):
        g[ours] = A(theirs)
    g["router0"] = inputs["L0_ffn_gate_kernel"]
    for n in ("w0", "w1", "wo"):
        g[n] = inputs["L0_ffn_" + n]
    g["router1"], g["gate_up"], g["down"] = F("w_router").T, F("gate_up_proj"), F("down_proj")
    g["sh_gate"], g["sh_up"], g["sh_down"] = F("w_gate").T, F("w_up").T, F("w_down").T
    return g


_OUTS = [((BATCH, T // BATCH, D), "float32")]


def kernel(**inputs):
    import numpy as _np
    import concourse.bacc as _bacc
    from concourse.bass_utils import run_bass_kernel_spmd as _run

    given = layout(inputs)
    nc = _bacc.Bacc("TRN2", target_bir_lowering=False, num_devices=1)
    arrays, args = {}, {}
    for name, a in given.items():
        a = _np.ascontiguousarray(a)
        arrays[f"in_{name}"] = a
        args[name] = nc.dram_tensor(f"in_{name}", a.shape, mybir.dt.from_np(a.dtype), kind="ExternalInput").ap()
    outs = [nc.dram_tensor(f"out_{i}", shape, F32, kind="ExternalOutput").ap() for i, (shape, _) in enumerate(_OUTS)]
    build(nc, args, outs[0].rearrange("b s d -> (b s) d"))
    r = _run(nc, [arrays], core_ids=[0])
    return r.results[0]["out_0"]
```
